# Optimizing a Trainium2 kernel written in Bass

```python
import numpy as np
import jax
import jax.numpy as jnp

def _softmax(x, axis=-1):
    return jax.nn.softmax(x, axis=axis)

def _gelu(x):
    return jax.nn.gelu(x, approximate=True)

def _silu(x):
    return jax.nn.silu(x)

def _sigmoid(x):
    return jax.nn.sigmoid(x)

def _layernorm(x, axis=-1, eps=1e-05):
    m = jnp.mean(x, axis=axis, keepdims=True)
    v = jnp.var(x, axis=axis, keepdims=True)
    return (x - m) / jnp.sqrt(v + eps)

def _scatter_add(tgt, idx, src, axis=0):
    return tgt.at[idx].add(src)

def _segment_sum(src, seg, n):
    return jax.ops.segment_sum(src, seg, n)
kernel_name = 'mk_seq_postln_d2_jaxref_r8_b38f14'

def setup_inputs(seed: int=0):
    np.random.seed(seed)
    _w = jnp.asarray

    def _L0_attn_setup():
        import math
        import jax, jax.numpy as jnp
        import numpy as np
        EPS = 1e-06
        NEG = -1000000000.0

        def rms_norm(x):
            return x * jax.lax.rsqrt(jnp.mean(x * x, axis=-1, keepdims=True) + EPS)

        def apply_rope(x, cos, sin):
            d2 = x.shape[-1] // 2
            x1, x2 = (x[..., :d2], x[..., d2:])
            c = cos[None, None, :, :]
            s = sin[None, None, :, :]
            return jnp.concatenate([x1 * c - x2 * s, x2 * c + x1 * s], axis=-1)
        key = jax.random.key(seed)
        k1, k2, k3 = jax.random.split(key, 3)
        B, T, C = (2, 256, 128)
        H, D = (16, 64)
        dim_inner = H * D
        x = jax.random.normal(k1, (B, T, C), dtype=jnp.float32)
        w_qkv = jax.random.normal(k2, (3 * dim_inner, C), dtype=jnp.float32) * (1.0 / math.sqrt(C))
        w_out = jax.random.normal(k3, (C, dim_inner), dtype=jnp.float32) * (1.0 / math.sqrt(dim_inner))
        return {'x': x, 'w_qkv': w_qkv, 'w_out': w_out}
    _L0_attn_in = _L0_attn_setup()

    def _L0_ffn_setup():
        import jax, jax.numpy as jnp
        import numpy as np
        HIDDEN = 128
        INTER = 512
        key = jax.random.key(seed)
        k1, k2, k3, k4, k5 = jax.random.split(key, 5)
        hidden_states = jax.random.normal(k1, (4, 256, HIDDEN), dtype=jnp.float32)
        W1 = jax.random.normal(k2, (HIDDEN, INTER), dtype=jnp.float32) * (1.0 / np.sqrt(HIDDEN))
        b1 = jax.random.normal(k3, (INTER,), dtype=jnp.float32) * 0.02
        W2 = jax.random.normal(k4, (INTER, HIDDEN), dtype=jnp.float32) * (1.0 / np.sqrt(INTER))
        b2 = jax.random.normal(k5, (HIDDEN,), dtype=jnp.float32) * 0.02
        return {'hidden_states': hidden_states, 'W1': W1, 'b1': b1, 'W2': W2, 'b2': b2}
    _L0_ffn_in = _L0_ffn_setup()

    def _L1_attn_setup():
        import jax, jax.numpy as jnp
        import numpy as np
        EPS = 1e-05

        def layernorm(x, g, b):
            m = jnp.mean(x, axis=-1, keepdims=True)
            v = jnp.mean(jnp.square(x - m), axis=-1, keepdims=True)
            return (x - m) * jax.lax.rsqrt(v + EPS) * g + b

        def delta(x, gates_w, gates_b, lr_w, lr_b, out_w, out_b):
            N, T, C = x.shape
            qkv = x @ gates_w + gates_b
            q, k, v = jnp.split(qkv, 3, axis=-1)
            lr = x @ lr_w + lr_b
            k = k / jnp.linalg.norm(k, axis=-1, keepdims=True)
            K = jnp.tril(jnp.einsum('ntc,nsc->nts', k, k), k=-1)
            A = K + jnp.eye(T, dtype=x.dtype)
            u = jax.scipy.linalg.solve_triangular(A, v, lower=True)
            score = jnp.einsum('nsk,ntk->nst', q, k)
            y = jnp.einsum('nst,ntv->nsv', score, lr * u)
            return y @ out_w + out_b

        def mlp(x, w1, b1, w2, b2):
            return jax.nn.relu(x @ w1 + b1) @ w2 + b2
        N, T, C = (8, 256, 128)
        key = jax.random.key(seed)
        ks = jax.random.split(key, 16)
        s = 0.02
        return {'x': jax.random.normal(ks[0], (N, T, C), jnp.float32), 'dn_g': jnp.ones((C,), jnp.float32), 'dn_b': jnp.zeros((C,), jnp.float32), 'gates_w': jax.random.normal(ks[1], (C, 3 * C), jnp.float32) * s, 'gates_b': jnp.zeros((3 * C,), jnp.float32), 'lr_w': jax.random.normal(ks[2], (C, 1), jnp.float32) * s, 'lr_b': jnp.zeros((1,), jnp.float32), 'out_w': jax.random.normal(ks[3], (C, C), jnp.float32) * s, 'out_b': jnp.zeros((C,), jnp.float32), 'mn_g': jnp.ones((C,), jnp.float32), 'mn_b': jnp.zeros((C,), jnp.float32), 'w1': jax.random.normal(ks[4], (C, C), jnp.float32) * s, 'b1': jnp.zeros((C,), jnp.float32), 'w2': jax.random.normal(ks[5], (C, C), jnp.float32) * s, 'b2': jnp.zeros((C,), jnp.float32)}
    _L1_attn_in = _L1_attn_setup()

    def _L1_ffn_setup():
        import jax, jax.numpy as jnp
        import numpy as np
        NUM_HEAVY = 128
        N_ITERS = 50
        FETCH_K_RATIO = 9.0 / 8.0
        EPS = 1.0

        def rmsnorm(x, gamma):
            scale = gamma.shape[0] ** 0.5
            normed = x / jnp.maximum(jnp.linalg.norm(x, axis=-1, keepdims=True), 1e-12)
            return normed * scale * gamma

        def feedforward(x, gamma, w1, b1, w2, b2):
            h = rmsnorm(x, gamma)
            h = jax.nn.gelu(h @ w1.T + b1, approximate=False)
            return h @ w2.T + b2

        def coor_descent(s, n_iters, k, eps):
            logk = jnp.log(jnp.asarray(k, s.dtype))
            a0 = jnp.zeros_like(s[..., :1])
            b0 = -s

            def body(carry, _):
                a, b = carry
                a = eps * (logk - jax.nn.logsumexp((s + b) / eps, axis=-1, keepdims=True))
                b = -jax.nn.relu(s + a)
                return ((a, b), None)
            (a, b), _ = jax.lax.scan(body, (a0, b0), None, length=n_iters)
            return jnp.exp((s + a + b) / eps)
        key = jax.random.key(seed)
        ks = jax.random.split(key, 12)
        b, n, dim = (8, 1024, 128)
        d_light, d_heavy = (int(dim * 0.5), dim * 4)

        def lin(k, dout, din):
            bound = 1.0 / np.sqrt(din)
            k1, k2 = jax.random.split(k)
            w = jax.random.uniform(k1, (dout, din), jnp.float32, -bound, bound)
            bb = jax.random.uniform(k2, (dout,), jnp.float32, -bound, bound)
            return (w, bb)
        x = jax.random.normal(ks[0], (b, n, dim), jnp.float32)
        routing_token = jax.random.normal(ks[1], (dim,), jnp.float32)
        w1_l, b1_l = lin(ks[2], d_light, dim)
        w2_l, b2_l = lin(ks[3], dim, d_light)
        w1_h, b1_h = lin(ks[4], d_heavy, dim)
        w2_h, b2_h = lin(ks[5], dim, d_heavy)
        return dict(x=x, routing_token=routing_token, gamma_l=jnp.ones((dim,), jnp.float32), w1_l=w1_l, b1_l=b1_l, w2_l=w2_l, b2_l=b2_l, gamma_h=jnp.ones((dim,), jnp.float32), w1_h=w1_h, b1_h=b1_h, w2_h=w2_h, b2_h=b2_h)
    _L1_ffn_in = _L1_ffn_setup()
    _d = {'L0_attn_x': _L0_attn_in['x'], 'L0_attn_w_qkv': _L0_attn_in['w_qkv'], 'L0_attn_w_out': _L0_attn_in['w_out'], 'L0_ffn_W1': _L0_ffn_in['W1'], 'L0_ffn_b1': _L0_ffn_in['b1'], 'L0_ffn_W2': _L0_ffn_in['W2'], 'L0_ffn_b2': _L0_ffn_in['b2'], 'L1_attn_dn_g': _L1_attn_in['dn_g'], 'L1_attn_dn_b': _L1_attn_in['dn_b'], 'L1_attn_gates_w': _L1_attn_in['gates_w'], 'L1_attn_gates_b': _L1_attn_in['gates_b'], 'L1_attn_lr_w': _L1_attn_in['lr_w'], 'L1_attn_lr_b': _L1_attn_in['lr_b'], 'L1_attn_out_w': _L1_attn_in['out_w'], 'L1_attn_out_b': _L1_attn_in['out_b'], 'L1_attn_mn_g': _L1_attn_in['mn_g'], 'L1_attn_mn_b': _L1_attn_in['mn_b'], 'L1_attn_w1': _L1_attn_in['w1'], 'L1_attn_b1': _L1_attn_in['b1'], 'L1_attn_w2': _L1_attn_in['w2'], 'L1_attn_b2': _L1_attn_in['b2'], 'L1_ffn_routing_token': _L1_ffn_in['routing_token'], 'L1_ffn_gamma_l': _L1_ffn_in['gamma_l'], 'L1_ffn_w1_l': _L1_ffn_in['w1_l'], 'L1_ffn_b1_l': _L1_ffn_in['b1_l'], 'L1_ffn_w2_l': _L1_ffn_in['w2_l'], 'L1_ffn_b2_l': _L1_ffn_in['b2_l'], 'L1_ffn_gamma_h': _L1_ffn_in['gamma_h'], 'L1_ffn_w1_h': _L1_ffn_in['w1_h'], 'L1_ffn_b1_h': _L1_ffn_in['b1_h'], 'L1_ffn_w2_h': _L1_ffn_in['w2_h'], 'L1_ffn_b2_h': _L1_ffn_in['b2_h']}
    _x0 = _d['L0_attn_x']
    _d['L0_attn_x'] = jax.random.normal(jax.random.fold_in(jax.random.key(seed), 1), (1, 2048, 128), dtype=_x0.dtype)
    del _x0
    return _d

def reference(L0_attn_x, L0_attn_w_qkv, L0_attn_w_out, L0_ffn_W1, L0_ffn_b1, L0_ffn_W2, L0_ffn_b2, L1_attn_dn_g, L1_attn_dn_b, L1_attn_gates_w, L1_attn_gates_b, L1_attn_lr_w, L1_attn_lr_b, L1_attn_out_w, L1_attn_out_b, L1_attn_mn_g, L1_attn_mn_b, L1_attn_w1, L1_attn_b1, L1_attn_w2, L1_attn_b2, L1_ffn_routing_token, L1_ffn_gamma_l, L1_ffn_w1_l, L1_ffn_b1_l, L1_ffn_w2_l, L1_ffn_b2_l, L1_ffn_gamma_h, L1_ffn_w1_h, L1_ffn_b1_h, L1_ffn_w2_h, L1_ffn_b2_h):

    def _L0_attn_ref(x, w_qkv, w_out):
        import math
        import jax, jax.numpy as jnp
        import numpy as np
        EPS = 1e-06
        NEG = -1000000000.0

        def rms_norm(x):
            return x * jax.lax.rsqrt(jnp.mean(x * x, axis=-1, keepdims=True) + EPS)

        def apply_rope(x, cos, sin):
            d2 = x.shape[-1] // 2
            x1, x2 = (x[..., :d2], x[..., d2:])
            c = cos[None, None, :, :]
            s = sin[None, None, :, :]
            return jnp.concatenate([x1 * c - x2 * s, x2 * c + x1 * s], axis=-1)
        H, D, window_size = (16, 64, 32)
        B, T, C = x.shape
        xn = rms_norm(x)
        qkv = xn @ w_qkv.T
        q, k, v = jnp.split(qkv, 3, axis=-1)
        q = q.reshape(B, T, H, D).transpose(0, 2, 1, 3)
        k = k.reshape(B, T, H, D).transpose(0, 2, 1, 3)
        v = v.reshape(B, T, H, D).transpose(0, 2, 1, 3)
        inv_freq = 1.0 / 10000.0 ** (jnp.arange(0, D, 2, dtype=jnp.float32) / D)
        freqs = jnp.outer(jnp.arange(T, dtype=jnp.float32), inv_freq)
        cos, sin = (jnp.cos(freqs), jnp.sin(freqs))
        q = apply_rope(q, cos, sin)
        k = apply_rope(k, cos, sin)
        scale = 1.0 / math.sqrt(D)
        attn = jnp.einsum('bhqd,bhkd->bhqk', q, k) * scale
        q_pos = jnp.arange(T)[:, None]
        k_pos = jnp.arange(T)[None, :]
        mask = (q_pos >= k_pos) & (q_pos - k_pos <= window_size)
        attn = jnp.where(mask[None, None], attn, NEG)
        attn = jax.nn.softmax(attn.astype(jnp.float32), axis=-1).astype(q.dtype)
        out = jnp.einsum('bhqk,bhkd->bhqd', attn, v)
        out = out.transpose(0, 2, 1, 3).reshape(B, T, H * D)
        return out @ w_out.T

    def _L0_ffn_ref(hidden_states, W1, b1, W2, b2):
        import jax, jax.numpy as jnp
        import numpy as np
        HIDDEN = 128
        INTER = 512
        h = jax.nn.relu(jnp.einsum('bsh,hi->bsi', hidden_states, W1) + b1)
        return jnp.einsum('bsi,ih->bsh', h, W2) + b2

    def _L1_attn_ref(x, dn_g, dn_b, gates_w, gates_b, lr_w, lr_b, out_w, out_b, mn_g, mn_b, w1, b1, w2, b2):
        import jax, jax.numpy as jnp
        import numpy as np
        EPS = 1e-05

        def layernorm(x, g, b):
            m = jnp.mean(x, axis=-1, keepdims=True)
            v = jnp.mean(jnp.square(x - m), axis=-1, keepdims=True)
            return (x - m) * jax.lax.rsqrt(v + EPS) * g + b

        def delta(x, gates_w, gates_b, lr_w, lr_b, out_w, out_b):
            N, T, C = x.shape
            qkv = x @ gates_w + gates_b
            q, k, v = jnp.split(qkv, 3, axis=-1)
            lr = x @ lr_w + lr_b
            k = k / jnp.linalg.norm(k, axis=-1, keepdims=True)
            K = jnp.tril(jnp.einsum('ntc,nsc->nts', k, k), k=-1)
            A = K + jnp.eye(T, dtype=x.dtype)
            u = jax.scipy.linalg.solve_triangular(A, v, lower=True)
            score = jnp.einsum('nsk,ntk->nst', q, k)
            y = jnp.einsum('nst,ntv->nsv', score, lr * u)
            return y @ out_w + out_b

        def mlp(x, w1, b1, w2, b2):
            return jax.nn.relu(x @ w1 + b1) @ w2 + b2
        x = x + delta(layernorm(x, dn_g, dn_b), gates_w, gates_b, lr_w, lr_b, out_w, out_b)
        x = x + mlp(layernorm(x, mn_g, mn_b), w1, b1, w2, b2)
        return x

    def _L1_ffn_ref(x, routing_token, gamma_l, w1_l, b1_l, w2_l, b2_l, gamma_h, w1_h, b1_h, w2_h, b2_h):
        import jax, jax.numpy as jnp
        import numpy as np
        NUM_HEAVY = 128
        N_ITERS = 50
        FETCH_K_RATIO = 9.0 / 8.0
        EPS = 1.0

        def rmsnorm(x, gamma):
            scale = gamma.shape[0] ** 0.5
            normed = x / jnp.maximum(jnp.linalg.norm(x, axis=-1, keepdims=True), 1e-12)
            return normed * scale * gamma

        def feedforward(x, gamma, w1, b1, w2, b2):
            h = rmsnorm(x, gamma)
            h = jax.nn.gelu(h @ w1.T + b1, approximate=False)
            return h @ w2.T + b2

        def coor_descent(s, n_iters, k, eps):
            logk = jnp.log(jnp.asarray(k, s.dtype))
            a0 = jnp.zeros_like(s[..., :1])
            b0 = -s

            def body(carry, _):
                a, b = carry
                a = eps * (logk - jax.nn.logsumexp((s + b) / eps, axis=-1, keepdims=True))
                b = -jax.nn.relu(s + a)
                return ((a, b), None)
            (a, b), _ = jax.lax.scan(body, (a0, b0), None, length=n_iters)
            return jnp.exp((s + a + b) / eps)
        b, n, dim = x.shape
        light_out = feedforward(x, gamma_l, w1_l, b1_l, w2_l, b2_l)
        s = jnp.einsum('bnd,d->bn', x, routing_token)
        effective_k = min(NUM_HEAVY * FETCH_K_RATIO, n)
        scores = coor_descent(s, N_ITERS, effective_k, EPS)
        selected_scores, selected_indices = jax.lax.top_k(scores, NUM_HEAVY)
        selected_scores = selected_scores + jax.lax.stop_gradient(1.0 - selected_scores)
        routed = jnp.take_along_axis(x, selected_indices[..., None], axis=1)
        routed_out = feedforward(routed, gamma_h, w1_h, b1_h, w2_h, b2_h)
        routed_out = routed_out * selected_scores[..., None]
        batch_range = jnp.arange(b)[:, None]
        heavy_out = jnp.zeros_like(x).at[batch_range, selected_indices].set(routed_out)
        return light_out + heavy_out
    x = L0_attn_x
    x = _layernorm(x + _L0_attn_ref(x, L0_attn_w_qkv, L0_attn_w_out), axis=-1)
    x = _layernorm(x + _L0_ffn_ref(x, L0_ffn_W1, L0_ffn_b1, L0_ffn_W2, L0_ffn_b2), axis=-1)
    x = _layernorm(x + _L1_attn_ref(x, L1_attn_dn_g, L1_attn_dn_b, L1_attn_gates_w, L1_attn_gates_b, L1_attn_lr_w, L1_attn_lr_b, L1_attn_out_w, L1_attn_out_b, L1_attn_mn_g, L1_attn_mn_b, L1_attn_w1, L1_attn_b1, L1_attn_w2, L1_attn_b2), axis=-1)
    x = _layernorm(x + _L1_ffn_ref(x, L1_ffn_routing_token, L1_ffn_gamma_l, L1_ffn_w1_l, L1_ffn_b1_l, L1_ffn_w2_l, L1_ffn_b2_l, L1_ffn_gamma_h, L1_ffn_w1_h, L1_ffn_b1_h, L1_ffn_w2_h, L1_ffn_b2_h), axis=-1)
    return x

_drawn_inputs = setup_inputs


def setup_inputs(seed=0):
    import zlib

    import numpy as np

    out = dict(_drawn_inputs(seed))
    spreads = {'L1_attn_dn_g': (1.0, 0.6),
     'L1_attn_dn_b': (0.0, 0.519),
     'L1_attn_gates_b': (0.0, 0.1),
     'L1_attn_out_b': (0.0, 0.1),
     'L1_attn_mn_g': (1.0, 0.6),
     'L1_attn_mn_b': (0.0, 0.8),
     'L1_attn_b1': (0.0, 0.8),
     'L1_attn_b2': (0.0, 0.1),
     'L1_ffn_gamma_l': (1.0, 0.2),
     'L1_ffn_gamma_h': (1.0, 0.6)}
    factors = {'L0_ffn_b1': 5.108,
     'L0_ffn_b2': 3.451,
     'L1_attn_w1': 3.668,
     'L1_attn_w2': 2.773,
     'L1_ffn_b1_l': 3.408,
     'L1_ffn_b1_h': 8.0,
     'L1_ffn_b2_h': 8.0}
    for name, (base, spread) in spreads.items():
        noise = np.random.default_rng([zlib.crc32(name.encode()), seed]).standard_normal(out[name].shape)
        drawn = base * np.exp(spread * noise) if base else spread * noise
        out[name] = jnp.asarray(drawn.astype(out[name].dtype))
    for name, factor in factors.items():
        out[name] = (out[name] * factor).astype(out[name].dtype)
    return out
```

```python
from contextlib import ExitStack

import numpy as np

import concourse.bass as bass
from concourse import mybir

F32 = mybir.dt.float32
BF16 = mybir.dt.bfloat16
I32 = mybir.dt.int32
ALU = mybir.AluOpType
ACT = mybir.ActivationFunctionType
AX_X = mybir.AxisListType.X

P = 128


def static(v):
    return isinstance(v, int)


def wait(eng, sem, value):
    if static(value) and value <= 0:
        return
    eng.wait_ge(sem, value)


def rope_tables(tokens, dim):
    half = dim // 2
    inv = (1.0 / 10000.0 ** (np.arange(0, dim, 2, dtype=np.float32) / np.float32(dim))).astype(np.float32)
    angle = np.outer(np.arange(tokens, dtype=np.float32), inv).astype(np.float32)
    cos, sin = np.cos(angle).T, np.sin(angle).T
    return (np.concatenate([cos] * 4).astype(np.float32),
            np.concatenate([sin, -sin, sin, -sin]).astype(np.float32))


def band_masks(window, blocked):
    q, k = np.arange(P)[:, None], np.arange(P)[None, :]
    own = (k <= q) & (q - k <= window)
    before = (q < window) & (k >= P - window) & (q - (k - P) <= window)
    out = np.stack([np.where(own, 0.0, blocked), np.where(own | before, 0.0, blocked)])
    return out.transpose(1, 0, 2).copy()


def level_masks(size, levels):
    i, j = np.arange(P)[:, None], np.arange(P)[None, :]
    out = []
    for _ in range(levels):
        out.append((i // (2 * size) == j // (2 * size)) & (i // size < j // size))
        size *= 2
    return np.stack(out).astype(np.float32).transpose(1, 0, 2).copy()


def build(nc, x, w_q, w_k, w_v, w_o, late_weights, row_vectors, kv_bias, out, late):
    T, C = x.shape
    INNER = w_v.shape[1]
    D = 64
    WINDOW = 32
    H = INNER // D
    NB = T // P
    G = 4
    GH = H // G
    PAIRS = GH // 2
    KEEP = P - WINDOW
    SCALE = float(D) ** -0.5
    BLOCKED = -1e9
    NCH = INNER // P
    UNITS = NB * G
    TG = T // 512
    GB = NB // TG
    NF = (late["b_f1"][1] - late["b_f1"][0])
    NHF = (late["b_h1"][1] - late["b_h1"][0])
    LF = late["w_l1"][1] - late["w_l1"][0]
    KVW = 2 * C + 1
    SUB = 16
    NSUB = P // SUB
    NLEV = 3
    HEAVY = 128
    EFFECTIVE = HEAVY * 9.0 / 8.0
    DESCENT = 50
    REBASE = (12, 24, 36)
    CAP = 80.0
    EPS = 1e-5
    assert SUB << NLEV == P and GB * TG == NB and NSUB * NB == P

    cos_np, sin_np = rope_tables(T, D)
    cos_dram = nc.inline_tensor(cos_np, name="rope_cos").ap()
    sin_dram = nc.inline_tensor(sin_np, name="rope_sin").ap()
    mask_np = band_masks(WINDOW, BLOCKED).astype(mybir.dt.np(BF16))
    mask_dram = nc.inline_tensor(mask_np, name="band_masks").ap()
    ident_dram = nc.inline_tensor(np.eye(P, dtype=np.float32), name="identity_f").ap()
    level_dram = nc.inline_tensor(level_masks(SUB, NLEV), name="level_masks").ap()
    before_dram = nc.inline_tensor(np.triu(np.ones((P, P), np.float32), 1), name="tokens_before").ap()

    with ExitStack() as ctx:
        scope = [ctx]

        def sb(name, shape, dt=F32):
            return scope[0].enter_context(nc.sbuf_tensor(name, shape, dt))

        def bank(name):
            return ctx.enter_context(nc.psum_tensor(name, [P, 512], F32))

        def sem(name):
            return ctx.enter_context(nc.semaphore(name))

        ident = sb("ident", [P, P])
        expo = sb("expo", [P, NB])
        r1 = sb("r1", [P, NB, C])
        mv = sb("mv", [P, NB, 2])
        late_sb = sb("late_sb", [P, late["end"][0]])
        W = {n: late_sb[:, a:b] for n, (a, b) in late.items() if n != "end"}
        rows = sb("rows", [P, 6, C])
        row = {n: rows[:, i, :] for i, n in enumerate(("b_f2", "b_do", "b_m2", "b_l2", "b_h2", "token"))}
        kv_b = sb("kv_b", [P, KVW])
        lmask = sb("lmask", [P, NLEV, P])
        before = sb("before", [P, P])
        first = ExitStack()
        scope[0] = first
        x_sb = sb("x_sb", [P, NB, C])
        ident_bf = sb("ident_bf", [P, P], BF16)
        masks = sb("masks", [P, 2, P], BF16)
        cos = sb("cos", [P, T])
        sin = sb("sin", [P, T])
        wq = sb("wq", [P, INNER])
        wk = sb("wk", [P, INNER])
        wv = sb("wv", [P, INNER])
        wo = sb("wo", [P, NCH, C])
        xn = sb("xn", [P, NB, C])
        xnT = sb("xnT", [P, T])
        xv = sb("xv", [P, P])
        stat = sb("stat", [P, NB])
        mean2 = sb("mean2", [P, NB])
        rms = sb("rms", [P, NB])
        t_cos = sb("t_cos", [P, G, 4, P])
        t_sin = sb("t_sin", [P, G, 4, P])
        t_swap = sb("t_swap", [P, G, 4, P])
        qk = sb("qk", [P, G, 4, P])
        k_tail = sb("k_tail", [P, G, PAIRS, WINDOW])
        k_diff = sb("k_diff", [P, G, PAIRS, WINDOW])
        negmax = sb("negmax", [P, 2, 2, PAIRS])
        total = sb("total", [P, 2, 2, PAIRS])
        inv_total = sb("inv_total", [P, 2, 2, PAIRS])
        probs = sb("probs", [P, 2, 2, PAIRS, P])
        probsT = sb("probsT", [P, 2, GH, P])
        v_own = sb("v_own", [P, G, GH, D])
        v_mix = sb("v_mix", [P, G, GH, D])
        oT = sb("oT", [P, NCH, P])
        bn = sb("bn", [P, 6])
        first.close()

        scope[0] = ctx
        XA = sb("XA", [P, NB, C])
        XB = sb("XB", [P, NB, C])
        XC = sb("XC", [P, NB, C])
        XD = sb("XD", [P, NB, C])
        XE = sb("XE", [P, NB, C])
        bns = sb("bns", [P, NB, 6])
        var_eps = sb("var_eps", [P, NB])
        rstd = sb("rstd", [P, NB])
        act_junk = sb("act_junk", [P, 2, C])
        act_one = sb("act_one", [P, 1])
        djunk2 = sb("djunk2", [P, 2, C])
        nsq = sb("nsq", [P, NB])
        hT = sb("hT", [P, T])
        kth = sb("kth", [P, P])
        ones = sb("ones", [P, P])
        second = ExitStack()
        scope[0] = second
        kv = sb("kv", [P, NB, KVW + 3])
        khT = sb("khT", [P, NB, C])
        gram = sb("gram", [P, NB, P])
        l16 = sb("l16", [P, SUB, SUB])
        x16 = sb("x16", [P, SUB, SUB])
        prod = sb("prod", [P, SUB, SUB])
        BT = sb("BT", [P, NLEV, NB, P])
        invT = sb("invT", [P, NB, P])
        inv = sb("inv", [P, NB, P])
        bx = sb("bx", [P, NB, P])
        naq = sb("naq", [P, NB, 2 * C])
        state = sb("state", [P, NB, C])
        wv2 = sb("wv2", [P, NB, 2 * C])
        g_sb = sb("g_sb", [P, C])
        zT = sb("zT", [P, C + 1])
        z_bias = sb("z_bias", [P, C])
        e_sb = sb("e_sb", [P, C])
        delta_bias = sb("delta_bias", [P, C])
        dk = khT
        second.close()
        scope[0] = ctx
        hid = sb("hid", [P, max(NF, NHF), T])
        light = sb("light", [P, T])
        s_tok = sb("s_tok", [P, NB])
        f_tok = sb("f_tok", [P, NB])
        args = sb("args", [P, NB])
        log_in = sb("log_in", [P, 1])
        one = sb("one", [P, 1])
        escore = sb("escore", [P, NB])
        djunk = sb("djunk", [P, NB])
        cjunk = sb("cjunk", [P, NB])
        dpart = sb("dpart", [P, 2])
        cpart = sb("cpart", [P, 2])
        widths = sb("widths", [P, DESCENT])
        halves = sb("halves", [P, DESCENT])
        ends = sb("ends", [P, 2])
        ends_t = sb("ends_t", [2, P])
        ends_m = sb("ends_m", [2, 1])
        ends_d = sb("ends_d", [2, 2])
        base = sb("base", [P, 1])
        log_a = sb("log_a", [P, 1])
        theta = sb("theta", [P, 1])
        low = sb("low", [P, 1])
        step_w = sb("step_w", [P, 1])
        need = sb("need", [P, 1])
        key = sb("key", [P, NB])
        strict = sb("strict", [P, NB])
        tie = sb("tie", [P, NB])
        fits = sb("fits", [P, NB])
        tot_t = sb("tot_t", [NB, P])
        sel = sb("sel", [P, NB])
        score = sb("score", [P, NB])

        blocks_out = nc.dram_tensor("blocks_out", [NSUB, NB, SUB, SUB], F32).ap()
        blocks_in = nc.dram_tensor("blocks_in", [NSUB, NB, SUB, SUB], F32).ap()
        S_banks = ctx.enter_context(nc.psum_tensor("S", [P, 2, 4, P], F32))
        S = S_banks[:, :, 0:PAIRS, :]
        QK = [bank("QK0"), bank("QK1")]
        PT = bank("PT")
        V_bank, Y_bank = bank("V"), bank("Y")
        V_ps, Y_ps = V_bank[:, 0:GH * D], Y_bank[:, 0:C]
        O_ps = bank("O")
        XT_ps = [PT, Y_bank]

        B = [S_banks[:, 0].rearrange("p a k -> p (a k)"), S_banks[:, 1].rearrange("p a k -> p (a k)"),
             QK[0][:], QK[1][:], PT[:], V_bank[:], Y_bank[:], O_ps[:]]

        ld_x = [sem(f"ld_x{q}") for q in range(TG)]
        ld_ident, ld_masks, ld_wq, ld_wk, ld_wv, ld_wo = (sem("ld_" + n) for n in
                                                          ("ident", "masks", "wq", "wk", "wv", "wo"))
        ld_rope = [sem(f"ld_rope{q}") for q in range(3)]
        swapped = [sem(f"swapped{g}") for g in range(G)]
        stored = sem("stored")
        dve_step = sem("dve_step")
        pool_step = sem("pool_step")
        act_step = sem("act_step")
        sumsq_done = sem("sumsq_done")
        rms_done = sem("rms_done")
        squares_done = sem("squares_done")
        xn_done = sem("xn_done")
        xt_done = sem("xt_done")
        xnT_done = sem("xnT_done")
        cast_done = sem("cast_done")
        zero_done = sem("zero_done")
        scores_done = sem("scores_done")
        max_done = sem("max_done")
        exp_done = sem("exp_done")
        norm_done = sem("norm_done")
        probsT_ps = sem("probsT_ps")
        probsT_done = sem("probsT_done")
        qk_ps = sem("qk_ps")
        mul_done = sem("mul_done")
        rope_done = sem("rope_done")
        xv_done = sem("xv_done")
        v_ps = sem("v_ps")
        v_own_done = sem("v_own_done")
        v_tail_done = sem("v_tail_done")
        v_mix_done = sem("v_mix_done")
        o_ps = sem("o_ps")
        oT_done = sem("oT_done")
        y_ps = sem("y_ps")
        r1_done = sem("r1_done")
        inv_done = sem("inv_done")
        bn_done = sem("bn_done")
        mv1_done = sem("mv1_done")
        tail_done = sem("tail_done")
        scaled_done = sem("scaled_done")
        sum_done = sem("sum_done")
        ld_late = sem("ld_late")
        late_cast = sem("late_cast")
        rsq_in = sem("rsq_in")
        rsq_out = sem("rsq_out")
        x1_done = sem("x1_done")
        x1b_done = sem("x1b_done")
        tr_src = sem("tr_src")
        tr_ps = sem("tr_ps")
        tr_done = sem("tr_done")
        hid_ps = sem("hid_ps")
        hid_done = sem("hid_done")
        y2_ps = sem("y2_ps")
        r2_done = sem("r2_done")
        kv_ps = sem("kv_ps")
        kv_done = sem("kv_done")
        kh_done = sem("kh_done")
        kh_T = sem("kh_T")
        gram_ps = sem("gram_ps")
        gram_done = sem("gram_done")
        l16_done = sem("l16_done")
        x16_done = sem("x16_done")
        invT_ld = sem("invT_ld")
        bt_done = sem("bt_done")
        bx_ps = sem("bx_ps")
        bx_done = sem("bx_done")
        xbx_ps = sem("xbx_ps")
        inv_done2 = sem("inv_done2")
        xbxt_ps = sem("xbxt_ps")
        invT_done = sem("invT_done")
        ix_ps = sem("ix_ps")
        ix_done = sem("ix_done")
        wv_ps = sem("wv_ps")
        wv_done = sem("wv_done")
        dk_done = sem("dk_done")
        aq_ps = sem("aq_ps")
        aq_done = sem("aq_done")
        st_ps = sem("st_ps")
        st_done = sem("st_done")
        g_ps = sem("g_ps")
        g_done = sem("g_done")
        z_ps = sem("z_ps")
        z_done = sem("z_done")
        zb_done = sem("zb_done")
        e_ps = sem("e_ps")
        e_done = sem("e_done")
        db_ps = sem("db_ps")
        db_done = sem("db_done")
        x3_ps = sem("x3_ps")
        x3_done = sem("x3_done")
        x32_done = sem("x32_done")
        m1_ps = sem("m1_ps")
        m1_done = sem("m1_done")
        m2_ps = sem("m2_ps")
        r3_done = sem("r3_done")
        x6_done = sem("x6_done")
        x6b_done = sem("x6b_done")
        s_done = sem("s_done")
        l1_ps = sem("l1_ps")
        l1_done = sem("l1_done")
        h1_ps = sem("h1_ps")
        h1_done = sem("h1_done")
        l2_ps = sem("l2_ps")
        base_done = sem("base_done")
        h2_ps = sem("h2_ps")
        heavy_done = sem("heavy_done")
        red_done = sem("red_done")
        redT_ps = sem("redT_ps")
        redm_done = sem("redm_done")
        ends_ps = sem("ends_ps")
        desc_in = sem("desc_in")
        desc_ps = sem("desc_ps")
        cnt_in = sem("cnt_in")
        cnt_ps = sem("cnt_ps")
        arg_done = sem("arg_done")
        f_done = sem("f_done")
        ln_in = sem("ln_in")
        ln_done = sem("ln_done")
        low_done = sem("low_done")
        key_done = sem("key_done")
        strict_done = sem("strict_done")
        strict_ps = sem("strict_ps")
        tie_done = sem("tie_done")
        tot_ps = sem("tot_ps")
        tot_done = sem("tot_done")
        pre_ps = sem("pre_ps")
        score_done = sem("score_done")
        final_done = sem("final_done")
        out_ready = sem("out_ready")
        zeroed = sem("zeroed")
        gam_done = sem("gam_done")
        blocks_kept = sem("blocks_kept")
        inverses_kept = sem("inverses_kept")
        mv_all = sem("mv_all")
        x2_done = sem("x2_done")
        x16_set = sem("x16_set")
        dve_misc = sem("dve_misc")
        sq_done = sem("sq_done")
        asq = sem("asq")
        kset = sem("kset")
        pool_sum = sem("pool_sum")
        dstart = sem("dstart")

        block = ctx.enter_context(nc.Block())

        @block.sync
        def _(sp):
            def load_x(q):
                sp.dma_start(x_sb[:, GB * q:GB * q + GB, :],
                             x[512 * q:512 * q + 512, :].rearrange("(n p) c -> p n c", p=P)).then_inc(ld_x[q], 16)

            def swap_halves(n, g, b):
                sp.wait_ge(mul_done, n + 1)
                for r in range(0, P, D // 2):
                    other = r ^ (D // 2)
                    sp.dma_start(t_swap[other:other + D // 2, g], t_sin[r:r + D // 2, g]).then_inc(swapped[g], 16)

            def load_rope(h, cols):
                sp.dma_start(cos[:, cols], cos_dram[:, cols]).then_inc(ld_rope[h], 16)
                sp.dma_start(sin[:, cols], sin_dram[:, cols]).then_inc(ld_rope[h], 16)

            def swap_steps(b):
                for g in range(G):
                    swap_halves(b * G + g + G, g, b + 1)

            load_x(0)
            sp.dma_start(ident[:], ident_dram).then_inc(ld_ident, 16)
            load_rope(0, slice(0, P))
            load_x(1)
            sp.dma_start(masks[:], mask_dram).then_inc(ld_masks, 16)
            for q in range(2, TG):
                load_x(q)
            load_rope(1, slice(P, 4 * P))
            for g in range(G):
                swap_halves(g, g, 0)
            sp.dma_start(wo[:], w_o.rearrange("(n p) c -> p n c", p=P)).then_inc(ld_wo, 16)
            swap_steps(0)
            load_rope(2, slice(4 * P, T))
            swap_steps(1)
            sp.dma_start(late_sb[:], late_weights).then_inc(ld_late, 16)
            sp.dma_start(rows[:].rearrange("p a c -> p (a c)"), row_vectors.unsqueeze(0).broadcast_to([P, 6 * C])).then_inc(ld_late, 16)
            sp.dma_start(kv_b[:], kv_bias.unsqueeze(0).broadcast_to([P, KVW])).then_inc(ld_late, 16)
            sp.dma_start(lmask[:], level_dram).then_inc(ld_late, 16)
            sp.dma_start(before[:], before_dram).then_inc(ld_late, 16)
            with sp.Fori(2, NB - 1) as b:
                swap_steps(b)
            sp.wait_ge(gram_done, TG)
            for j in range(NSUB):
                r = slice(SUB * j, SUB * j + SUB)
                sp.dma_start(blocks_out[j].rearrange("n r k -> r n k"), gram[r, :, r]).then_inc(blocks_kept, 16)
            sp.wait_ge(blocks_kept, 16 * NSUB)
            sp.dma_start(l16[:], blocks_out.rearrange("j n r k -> (j n) r k")).then_inc(l16_done, 16)
            sp.wait_ge(x16_done, 1)
            sp.dma_start(blocks_in.rearrange("j n k r -> (j n) k r"), x16[:]).then_inc(inverses_kept, 16)
            sp.wait_ge(inverses_kept, 16)
            sp.wait_ge(zeroed, 1)
            for j in range(NSUB):
                r = slice(SUB * j, SUB * j + SUB)
                sp.dma_start(invT[r, :, r], blocks_in[j].rearrange("n k r -> k n r")).then_inc(invT_ld, 16)
            out_v = out.rearrange("(n p) c -> p n c", p=P)
            for q in range(TG):
                sp.wait_ge(out_ready, q + 1)
                sp.dma_start(out_v[:, GB * q:GB * q + GB], XA[:, GB * q:GB * q + GB]).then_inc(stored, 16)
            sp.wait_ge(stored, 16 * TG)

        @block.tensor
        def _(pe):
            def project_qk(n, g, tok):
                wait(pe, mul_done, n - 1)
                for j, w in enumerate((wq, wk)):
                    for pr in range(PAIRS):
                        f = slice((PAIRS * g + pr) * P, (PAIRS * g + pr + 1) * P)
                        c = slice((PAIRS * j + pr) * P, (PAIRS * j + pr + 1) * P)
                        last = nc.tensor.matmul(QK[g % 2][:, c], w[:, f], xnT[:, tok], start=True, stop=True)
                last.then_inc(qk_ps, 1)

            def project_v(n, g, b):
                pe.wait_ge(xv_done, b + 1)
                wait(pe, v_own_done, n)
                nc.tensor.matmul(V_ps, xv[:], wv[:, g * GH * D:(g + 1) * GH * D], start=True,
                                 stop=True).then_inc(v_ps, 1)

            def scores(u, g, variant):
                s = S
                pe.wait_ge(rope_done, u + 1)
                wait(pe, exp_done, u)
                for e in range(2):
                    nc.tensor.matmul(s[:, e], ident_bf[:], masks[:, variant:variant + 1, :].broadcast_to([P, PAIRS, P]),
                                     start=True, stop=False, skip_group_check=True)
                for pr in range(PAIRS):
                    for e in range(2):
                        r = slice(D * e, D * e + D)
                        q, k = qk[r, g, pr, :], qk[r, g, PAIRS + pr, :]
                        nc.tensor.matmul(s[:, e, pr], q, k, start=False, stop=True, skip_group_check=True)
                for pr in range(PAIRS):
                    for e in range(2):
                        r = slice(D * e, D * e + D)
                        last = nc.tensor.matmul(s[0:WINDOW, e, pr, KEEP:], qk[r, g, pr, 0:WINDOW],
                                                k_diff[r, g, pr, :], start=False, stop=True, skip_group_check=True)
                last.then_inc(scores_done, 1)

            def transpose_probs(u, g):
                pe.wait_ge(norm_done, u + 1)
                wait(pe, probsT_done, u)
                for h in range(GH):
                    last = nc.tensor.transpose(PT[:, h * P:(h + 1) * P], probs[:, g % 2, h % 2, h // 2, :], ident[:])
                last.then_inc(probsT_ps, 1)

            def attend(u, g):
                pe.wait_ge(probsT_done, u + 1)
                pe.wait_ge(v_mix_done, u + 1)
                wait(pe, oT_done, u)
                for h in range(GH):
                    r = slice(D * (h % 2), D * (h % 2) + D)
                    c = (h // 2) * P
                    nc.tensor.matmul(O_ps[r, c + WINDOW:c + P], v_own[:, g, h, :],
                                     probsT[:, g % 2, h, WINDOW:P], start=True, stop=True)
                    last = nc.tensor.matmul(O_ps[r, c:c + WINDOW], v_mix[:, g, h, :],
                                            probsT[:, g % 2, h, 0:WINDOW], start=True, stop=True)
                last.then_inc(o_ps, 1)

            def project_out(b):
                pe.wait_ge(oT_done, G * b + G)
                wait(pe, r1_done, b)
                if static(b) and b == 0:
                    pe.wait_ge(xnT_done, TG)
                    pe.wait_ge(ld_wo, 16)
                for n in range(NCH):
                    last = nc.tensor.matmul(Y_ps, oT[:, n, :], wo[:, n, :], start=(n == 0), stop=(n == NCH - 1))
                last.then_inc(y_ps, 1)

            def transpose_x(q):
                pe.wait_ge(xn_done, GB * q + GB)
                wait(pe, xnT_done, q)
                for i in range(GB):
                    last = nc.tensor.transpose(XT_ps[min(q, 1)][:, i * P:(i + 1) * P], xn[:, GB * q + i, :], ident[:])
                last.then_inc(xt_done, 1)

            def steps(b):
                fixed = static(b)
                for g in range(G):
                    u = b * G + g
                    if not fixed or b < NB:
                        scores(u, g, 0 if fixed and b == 0 else 1)
                    if not fixed or b < NB - 1:
                        project_qk(u + G, g, bass.ts(b + 1, P))
                    if g == 2 and (not fixed or b >= 1):
                        project_out(b - 1)
                    if not fixed or 2 <= u <= UNITS + 1:
                        attend(u - 2, (g - 2) % G)
                    if not fixed or 1 <= u <= UNITS:
                        transpose_probs(u - 1, (g - 1) % G)
                    if fixed and b == 0 and 1 <= g < TG:
                        transpose_x(g)
                    if not fixed or u + 2 < UNITS:
                        project_v(u + 2, (g + 2) % G, b + (g + 2) // G)

            pe.wait_ge(ld_ident, 16)
            transpose_x(0)
            pe.wait_ge(xnT_done, 1)
            pe.wait_ge(scaled_done, 1)
            pe.wait_ge(ld_wk, 16)
            for g in range(G):
                project_qk(g, g, slice(0, P))
            pe.wait_ge(ld_wv, 16)
            for g in range(2):
                project_v(g, g, 0)
            pe.wait_ge(ld_masks, 16)
            pe.wait_ge(cast_done, 1)
            steps(0)
            steps(1)
            with pe.Fori(2, NB - 1) as b:
                steps(b)
            steps(NB - 1)
            steps(NB)
            tok = lambda n: slice(n * P, (n + 1) * P)
            grp = lambda q: slice(q * 512, (q + 1) * 512)

            def to_channels(stage, q, src, arrived, count):
                t = stage * TG + q
                pe.wait_ge(arrived, count)
                wait(pe, tr_done, t - 1)
                for i in range(GB):
                    last = nc.tensor.transpose(B[t % 2][:, tok(i)], src(GB * q + i), ident[:])
                last.then_inc(tr_ps, 1)

            pe.wait_ge(ld_late, 80)

            def hidden1(q):
                pe.wait_ge(tr_done, q + 1)
                for j in range(NF):
                    n = NF * q + j
                    wait(pe, hid_done, n - 3)
                    nc.tensor.matmul(B[2 + j], W["w_f1"][:, tok(j)], hT[:, grp(q)], start=True,
                                     stop=True).then_inc(hid_ps, 1)

            def out1(q):
                pe.wait_ge(hid_done, NF * (q + 1))
                wait(pe, r2_done, q - 1)
                for i in range(GB):
                    for j in range(NF):
                        last = nc.tensor.matmul(B[6 + q % 2][:, tok(i)], hid[:, j, tok(GB * q + i)],
                                                W["w_f2"][:, tok(j)], start=(j == 0), stop=(j == NF - 1))
                last.then_inc(y2_ps, 1)

            for q in range(TG):
                to_channels(0, q, lambda n: XA[:, n, :], x1_done, GB * (q + 1))
                if q >= 1:
                    hidden1(q - 1)
                if q >= 2:
                    out1(q - 2)
            hidden1(TG - 1)
            out1(TG - 2)
            out1(TG - 1)

            for q in range(TG):
                to_channels(1, q, lambda n: XB[:, n, :], tr_src, GB * (q + 1))
            for n in range(NB):
                pe.wait_ge(tr_done, TG + n // GB + 1)
                wait(pe, kv_done, n - 3)
                nc.tensor.matmul(B[2 + n % 4][:, 0:KVW], hT[:, tok(n)], W["w_kv"], start=True,
                                 stop=True).then_inc(kv_ps, 1)
            for q in range(TG):
                to_channels(2, q, lambda n: kv[:, n, 0:C], kh_done, q + 1)
            for q in range(TG):
                pe.wait_ge(tr_done, 2 * TG + q + 1)
                wait(pe, gram_done, q - 1)
                for i in range(GB):
                    n = GB * q + i
                    last = nc.tensor.matmul(B[6 + q % 2][:, tok(i)], khT[:, n, :], khT[:, n, :], start=True, stop=True)
                last.then_inc(gram_ps, 1)
            pe.wait_ge(invT_ld, 16 * NSUB)
            pe.wait_ge(gram_done, TG)
            for q in range(TG):
                wait(pe, ix_done, q - 1)
                for i in range(GB):
                    last = nc.tensor.transpose(B[q % 2][:, tok(i)], invT[:, GB * q + i, :], ident[:])
                last.then_inc(ix_ps, 1)
            for l in range(NLEV):
                final = l == NLEV - 1
                pe.wait_ge(bt_done, l + 1)
                for q in range(TG):
                    t = l * TG + q
                    if l == 0:
                        pe.wait_ge(ix_done, q + 1)
                    else:
                        pe.wait_ge(inv_done2, (l - 1) * TG + q + 1)
                    wait(pe, bx_done, t - 1)
                    for i in range(GB):
                        n = GB * q + i
                        last = nc.tensor.matmul(B[2 + q % 2][:, tok(i)], BT[:, l, n, :], inv[:, n, :], start=True, stop=True)
                    last.then_inc(bx_ps, 1)
                for q in range(TG):
                    t = l * TG + q
                    pe.wait_ge(bx_done, t + 1)
                    wait(pe, invT_done, t - 1)
                    if l > 0:
                        pe.wait_ge(invT_done, (l - 1) * TG + q + 1)
                    for i in range(GB):
                        n = GB * q + i
                        if not final:
                            nc.tensor.matmul(B[4 + q % 2][:, tok(i)], invT[:, n, :], bx[:, n, :], start=True, stop=True)
                        last = nc.tensor.matmul(B[6 + q % 2][:, tok(i)], bx[:, n, :], invT[:, n, :], start=True, stop=True)
                    last.then_inc(xbxt_ps, 1)
            for m in range(NB // 2):
                wait(pe, wv_done, m - 1)
                pe.wait_ge(invT_done, (NLEV - 1) * TG + m // 2 + 1)
                for i in range(2):
                    n = 2 * m + i
                    last = nc.tensor.matmul(B[m % 2][:, 256 * i:256 * i + 256], invT[:, n, :], kv[:, n, 0:2 * C],
                                            start=True, stop=True)
                last.then_inc(wv_ps, 1)
            for m in range(NB // 2):
                pe.wait_ge(wv_done, m + 1)
                pe.wait_ge(dk_done, m // 2 + 1)
                wait(pe, aq_done, m - 1)
                for i in range(2):
                    n = 2 * m + i
                    nc.tensor.matmul(B[2 + m % 2][:, 256 * i:256 * i + C], wv2[:, n, 0:C], kv[:, n, 0:C],
                                     start=True, stop=True)
                    last = nc.tensor.matmul(B[2 + m % 2][:, 256 * i + C:256 * i + 256], wv2[:, n, 0:C], dk[:, n, :],
                                            start=True, stop=True)
                last.then_inc(aq_ps, 1)
            for n in range(NB):
                if n > 0:
                    pe.wait_ge(aq_done, n // 2 + 1)
                    pe.wait_ge(st_done, n)
                if n < NB - 1:
                    last = nc.tensor.matmul(B[6][:, 0:C], kv[:, n, 0:C], wv2[:, n, C:], start=(n == 0), stop=(n == 0),
                                            skip_group_check=True)
                    if n > 0:
                        last = nc.tensor.matmul(B[6][:, 0:C], naq[:, n, 0:C], state[:, n, :], start=False, stop=True,
                                                skip_group_check=True)
                    last.then_inc(st_ps, 1)
                last = nc.tensor.matmul(B[7][:, 0:C], dk[:, n, :], wv2[:, n, C:], start=(n == 0), stop=False,
                                        skip_group_check=True)
                if n > 0:
                    last = nc.tensor.matmul(B[7][:, 0:C], naq[:, n, C:], state[:, n, :], start=False, stop=(n == NB - 1),
                                            skip_group_check=True)
            last.then_inc(g_ps, 1)
            pe.wait_ge(g_done, 1)
            nc.tensor.matmul(B[2][:, 0:C + 1], g_sb[:], W["w_qT"], start=True, stop=True).then_inc(z_ps, 1)
            pe.wait_ge(zb_done, 2)
            nc.tensor.matmul(B[3][:, 0:C], zT[:, 0:C], W["w_do"], start=True, stop=True).then_inc(e_ps, 1)
            nc.tensor.matmul(B[4][:, 0:C], z_bias[:], W["w_do"], start=True, stop=True).then_inc(db_ps, 1)
            pe.wait_ge(e_done, 1)
            for q in range(TG):
                wait(pe, x3_done, q - 1)
                for i in range(GB):
                    last = nc.tensor.matmul(B[6 + q % 2][:, tok(i)], hT[:, tok(GB * q + i)], e_sb[:], start=True, stop=True)
                last.then_inc(x3_ps, 1)

            for q in range(TG):
                to_channels(3, q, lambda n: XB[:, n, :], tr_src, NB + GB * (q + 1))
            for q in range(TG):
                pe.wait_ge(tr_done, 3 * TG + q + 1)
                wait(pe, m1_done, q - 1)
                nc.tensor.matmul(B[2 + q % 2], W["w_m1"], hT[:, grp(q)], start=True, stop=True).then_inc(m1_ps, 1)
            for q in range(TG):
                pe.wait_ge(m1_done, q + 1)
                wait(pe, r3_done, q - 1)
                for i in range(GB):
                    last = nc.tensor.matmul(B[6 + q % 2][:, tok(i)], hid[:, 0, tok(GB * q + i)], W["w_m2"],
                                            start=True, stop=True)
                last.then_inc(m2_ps, 1)

            for q in range(TG):
                to_channels(4, q, lambda n: XB[:, n, :], tr_src, 2 * NB + GB * (q + 1))
            pe.wait_ge(gam_done, 2)
            for q in range(TG):
                pe.wait_ge(tr_done, 4 * TG + q + 1)
                wait(pe, l1_done, q)
                nc.tensor.matmul(B[2][0:LF, :], W["w_l1"], hT[:, grp(q)], start=True, stop=True).then_inc(l1_ps, 1)
                for j in range(NHF):
                    n = NHF * q + j
                    wait(pe, h1_done, n - 1)
                    nc.tensor.matmul(B[3 + n % 2], W["w_h1"][:, tok(j)], hT[:, grp(q)], start=True, stop=True).then_inc(h1_ps, 1)
            for q in range(TG):
                pe.wait_ge(l1_done, q + 1)
                wait(pe, base_done, q)
                for i in range(GB):
                    last = nc.tensor.matmul(B[5][:, tok(i)], light[0:LF, tok(GB * q + i)], W["w_l2"][0:LF],
                                            start=True, stop=True)
                last.then_inc(l2_ps, 1)
                pe.wait_ge(h1_done, NHF * (q + 1))
                wait(pe, heavy_done, q)
                for i in range(GB):
                    for j in range(NHF):
                        last = nc.tensor.matmul(B[2][:, tok(i)], hid[:, j, tok(GB * q + i)], W["w_h2"][:, tok(j)],
                                                start=(j == 0), stop=(j == NHF - 1))
                last.then_inc(h2_ps, 1)

            pe.wait_ge(red_done, 2)
            pe.wait_ge(kset, 2)
            nc.tensor.transpose(B[6][0:2, 0:P], ends[:], ident[:]).then_inc(redT_ps, 1)
            pe.wait_ge(redm_done, 2)
            nc.tensor.matmul(B[6][:, 0:2], ones[0:2, :], ends_d[:], start=True, stop=True).then_inc(ends_ps, 1)
            for i in range(DESCENT - 1):
                pe.wait_ge(desc_in, i + 1)
                nc.tensor.matmul(B[6][:, 0:1], kth[:], dpart[:, 0:1], start=True, stop=True).then_inc(desc_ps, 1)
                pe.wait_ge(cnt_in, i + 1)
                nc.tensor.matmul(B[7][:, 0:1], ones[:], cpart[:, 0:1], start=True, stop=True).then_inc(cnt_ps, 1)
            pe.wait_ge(strict_done, 2)
            nc.tensor.matmul(B[6][:, 0:1], ones[:], dpart[:, 1:2], start=True, stop=True).then_inc(strict_ps, 1)
            pe.wait_ge(tie_done, 1)
            nc.tensor.matmul(B[7][0:NB, 0:P], tie[:], ones[:], start=True, stop=True).then_inc(tot_ps, 1)
            pe.wait_ge(tot_done, 1)
            nc.tensor.matmul(B[5][:, 0:NB], before[:], tie[:], start=True, stop=False)
            nc.tensor.matmul(B[5][:, 0:NB], tot_t[:], before[0:NB, 0:NB], start=False, stop=True).then_inc(pre_ps, 1)

        @block.vector
        def _(dve):
            count = [0]

            def chained(ins):
                count[0] += 1
                ins.then_inc(dve_step, 1)
                dve.wait_ge(dve_step, count[0])

            def rope_products(n, g, tok):
                dve.wait_ge(qk_ps, n + 1)
                wait(dve, rope_done, n - 3)
                for dst, table in ((t_cos, cos), (t_sin, sin)):
                    last = nc.vector.tensor_tensor(dst[:, g], QK[g % 2][:].rearrange("p (j t) -> p j t", j=4),
                                                   table[:, tok].unsqueeze(1).broadcast_to([P, 4, P]), ALU.mult)
                last.then_inc(mul_done, 1)

            def row_max(u, g):
                dve.wait_ge(scores_done, u + 1)
                nc.vector.tensor_reduce(negmax[:, g % 2], S, AX_X,
                                        ALU.max, negate=True).then_inc(max_done, 1)

            def normalise(u, g):
                dve.wait_ge(exp_done, u + 1)
                nc.vector.reciprocal(inv_total[:, g % 2], total[:, g % 2]).then_inc(inv_done, 1)
                dve.wait_ge(inv_done, u + 1)
                nc.vector.tensor_tensor(probs[:, g % 2], probs[:, g % 2],
                                        inv_total[:, g % 2].unsqueeze(3).broadcast_to([P, 2, PAIRS, P]),
                                        ALU.mult).then_inc(norm_done, 1)

            def keep_v_tail(n, g):
                wait(dve, o_ps, n - G + 1)
                nc.vector.tensor_copy(v_mix[KEEP:P, g], v_own[KEEP:P, g]).then_inc(v_tail_done, 1)

            def mix_v(n, g):
                dve.wait_ge(v_own_done, n + 1)
                nc.vector.tensor_copy(v_mix[0:KEEP, g], v_own[0:KEEP, g]).then_inc(v_mix_done, 1)

            def residual(b, tile):
                dve.wait_ge(y_ps, b + 1)
                nc.vector.tensor_tensor(r1[:, tile, :], x_sb[:, tile, :], Y_ps.unsqueeze(1), ALU.add).then_inc(r1_done, 1)

            def normalise_x(q):
                dve.wait_ge(rms_done, 1 if q == 0 else 2)
                dve.wait_ge(ld_x[q], 16)
                for n in range(GB * q, GB * q + GB):
                    nc.vector.tensor_scalar(xn[:, n, :], x_sb[:, n, :], rms[:, n:n + 1], None, ALU.mult).then_inc(xn_done, 1)

            def steps(b):
                fixed = static(b)
                for g in range(G):
                    u = b * G + g
                    if not fixed or u + 1 < UNITS:
                        keep_v_tail(u + 1, (g + 1) % G)
                    if not fixed or u < UNITS:
                        mix_v(u, g)
                    if not fixed or b < NB:
                        row_max(u, g)
                    if not fixed or 1 <= u <= UNITS:
                        normalise(u - 1, (g - 1) % G)
                    if g == 3 and (not fixed or b >= 1):
                        residual(b - 1, bass.ds(b - 1, 1))
                    if not fixed or b < NB - 1:
                        rope_products(u + G, g, bass.ts(b + 1, P))
                    if fixed and b == 0 and g < TG - 1:
                        normalise_x(g + 1)

            nc.vector.memset(v_own[:], 0.0).then_inc(zero_done, 1)
            dve.wait_ge(ld_x[0], 16)
            for n in range(GB):
                last = nc.vector.tensor_tensor_reduce(out=xn[:, n, :], in0=x_sb[:, n, :], in1=x_sb[:, n, :],
                                                      scale=1.0, scalar=0.0, op0=ALU.mult, op1=ALU.add,
                                                      accum_out=stat[:, n:n + 1])
            last.then_inc(squares_done, 1)
            dve.wait_ge(ld_ident, 16)
            nc.vector.tensor_copy(ident_bf[:], ident[:]).then_inc(cast_done, 1)
            normalise_x(0)
            dve.wait_ge(ld_rope[0], 32)
            for g in range(G):
                rope_products(g, g, slice(0, P))
            dve.wait_ge(ld_rope[1], 32)
            dve.wait_ge(zero_done, 1)
            keep_v_tail(0, 0)
            steps(0)
            steps(1)
            dve.wait_ge(ld_rope[2], 32)
            with dve.Fori(2, NB - 1) as b:
                steps(b)
            steps(NB - 1)
            steps(NB)
            grp = lambda q: slice(GB * q, GB * q + GB)
            roots = [0]

            def inverse_roots():
                roots[0] += 1
                dve.wait_ge(rsq_out, roots[0])

            def variances():
                dve.wait_ge(mv_all, mv_count[0])
                nc.vector.tensor_scalar(var_eps[:], mv[:, :, 1], EPS, None, ALU.add).then_inc(rsq_in, 1)
                inverse_roots()

            mv_count = [0]

            def statistics(src, n0, n1):
                for n in range(n0, n1):
                    last = nc.vector.bn_stats(bns[:, n, :], src[:, n, :])
                chained(last)
                for n in range(n0, n1):
                    nc.vector.bn_aggr(mv[:, n, :], bns[:, n, :]).then_inc(mv_all, 1)
                mv_count[0] += n1 - n0

            def standardise(dst, src, done):
                for n in range(NB):
                    nc.vector.tensor_scalar(dst[:, n, :], src[:, n, :], mv[:, n, 0:1], rstd[:, n:n + 1], ALU.subtract,
                                            ALU.mult).then_inc(done, 1)

            bank4 = lambda b: B[b].rearrange("p (n c) -> p n c", n=GB)
            spread = lambda v: v.unsqueeze(1).broadcast_to([P, GB, C])

            dve.wait_ge(r1_done, NB)
            statistics(r1, 0, NB)
            variances()
            standardise(XA, r1, x1_done)
            for q in range(TG):
                dve.wait_ge(y2_ps, q + 1)
                dve.wait_ge(x1b_done, q + 1)
                nc.vector.tensor_tensor(XC[:, grp(q)], bank4(6 + q % 2), XB[:, grp(q)], ALU.add).then_inc(r2_done, 1)
                dve.wait_ge(r2_done, q + 1)
                statistics(XC, GB * q, GB * q + GB)
            variances()
            standardise(XA, XC, x2_done)

            dve.wait_ge(x2_done, NB)
            statistics(XA, 0, NB)
            variances()
            standardise(XB, XA, tr_src)
            for n in range(NB):
                dve.wait_ge(kv_ps, n + 1)
                nc.vector.tensor_tensor(kv[:, n, 0:KVW], B[2 + n % 4][:, 0:KVW], kv_b[:], ALU.add).then_inc(kv_done, 1)
            inverse_roots()
            for q in range(TG):
                nc.vector.tensor_tensor(kv[:, grp(q), 0:C], kv[:, grp(q), 0:C],
                                        rstd[:, grp(q)].unsqueeze(2).broadcast_to([P, GB, C]), ALU.mult).then_inc(kh_done, 1)
            nc.vector.memset(x16[:], 0.0).then_inc(x16_set, 1)
            dve.wait_ge(x16_set, 1)
            nc.vector.memset(x16[:].rearrange("p a b -> p (a b)")[:, 0:SUB * SUB:SUB + 1], 1.0).then_inc(x16_set, 1)
            dve.wait_ge(gram_done, TG)
            nc.vector.tensor_tensor(BT[:, 0], gram[:], lmask[:, 0:1, :].broadcast_to([P, NB, P]), ALU.mult).then_inc(bt_done, 1)
            dve.wait_ge(l16_done, 16)
            dve.wait_ge(x16_set, 2)
            for i in range(1, SUB):
                chained(nc.vector.tensor_tensor(prod[:, 0:i, 0:i], l16[:, i:i + 1, 0:i].broadcast_to([P, i, i]),
                                                x16[:, 0:i, 0:i], ALU.mult))
                last = nc.vector.tensor_reduce(x16[:, 0:i, i], prod[:, 0:i, 0:i], AX_X, ALU.add, negate=True)
                if i < SUB - 1:
                    chained(last)
            last.then_inc(x16_done, 1)
            for q in range(TG):
                nc.vector.tensor_tensor(dk[:, grp(q)], kv[:, grp(q), 0:C],
                                        kv[:, grp(q), 2 * C:2 * C + 1].broadcast_to([P, GB, C]), ALU.mult).then_inc(dk_done, 1)
            for l in range(NLEV):
                for q in range(TG):
                    t = l * TG + q
                    dve.wait_ge(xbxt_ps, t + 1)
                    if l < NLEV - 1:
                        nc.vector.tensor_tensor(inv[:, grp(q)], inv[:, grp(q)], bank4(4 + q % 2), ALU.subtract).then_inc(inv_done2, 1)
                    nc.vector.tensor_tensor(invT[:, grp(q)], invT[:, grp(q)], bank4(6 + q % 2), ALU.subtract).then_inc(invT_done, 1)
            for n in range(NB - 1):
                dve.wait_ge(st_ps, n + 1)
                nc.vector.tensor_copy(state[:, n + 1, :], B[6][:, 0:C]).then_inc(st_done, 1)
            dve.wait_ge(g_ps, 1)
            nc.vector.tensor_copy(g_sb[:], B[7][:, 0:C]).then_inc(g_done, 1)
            dve.wait_ge(db_ps, 1)
            chained(nc.vector.tensor_tensor(delta_bias[:], B[4][:, 0:C], row["b_do"], ALU.add))
            for q in range(TG):
                last = nc.vector.tensor_tensor(XC[:, grp(q)], XA[:, grp(q)], spread(delta_bias[:]), ALU.add)
            chained(last)
            for q in range(TG):
                dve.wait_ge(x3_ps, q + 1)
                nc.vector.tensor_tensor(XD[:, grp(q)], bank4(6 + q % 2), XC[:, grp(q)], ALU.add).then_inc(x3_done, 1)
                dve.wait_ge(x3_done, q + 1)
                statistics(XD, GB * q, GB * q + GB)
            variances()
            standardise(XB, XD, tr_src)
            for q in range(TG):
                dve.wait_ge(m2_ps, q + 1)
                dve.wait_ge(x32_done, q + 1)
                nc.vector.tensor_tensor(XE[:, grp(q)], bank4(6 + q % 2), XC[:, grp(q)], ALU.add).then_inc(r3_done, 1)
                dve.wait_ge(r3_done, q + 1)
                statistics(XE, GB * q, GB * q + GB)
            variances()
            standardise(XA, XE, x6_done)

            dve.wait_ge(x6_done, NB)
            for n in range(NB):
                last = nc.vector.tensor_tensor_reduce(out=djunk2[:, n % 2], in0=XA[:, n, :], in1=row["token"], scale=1.0, scalar=0.0,
                                                      op0=ALU.mult, op1=ALU.add, accum_out=s_tok[:, n:n + 1])
                chained(last)
            dve.wait_ge(sq_done, NB)
            nc.vector.tensor_scalar(var_eps[:], nsq[:], 1.0 / C, 1e-24 / C, ALU.mult, ALU.max).then_inc(rsq_in, 1)
            nc.vector.tensor_reduce(ends[:, 0:1], s_tok[:], AX_X, ALU.max).then_inc(red_done, 1)
            nc.vector.tensor_reduce(ends[:, 1:2], s_tok[:], AX_X, ALU.max, apply_absolute_value=True).then_inc(red_done, 1)
            inverse_roots()
            for n in range(NB):
                nc.vector.tensor_scalar(XB[:, n, :], XA[:, n, :], rstd[:, n:n + 1], None, ALU.mult).then_inc(tr_src, 1)
            for q in range(TG):
                dve.wait_ge(l2_ps, q + 1)
                dve.wait_ge(x6b_done, q + 1)
                nc.vector.tensor_tensor(XC[:, grp(q)], bank4(5), XC[:, grp(q)], ALU.add).then_inc(base_done, 1)
                dve.wait_ge(h2_ps, q + 1)
                nc.vector.tensor_tensor(XE[:, grp(q)], bank4(2), spread(row["b_h2"]), ALU.add).then_inc(heavy_done, 1)

            dve.wait_ge(redT_ps, 1)
            chained(nc.vector.tensor_reduce(ends_m[:], B[6][0:2, 0:P], AX_X, ALU.max))
            nc.vector.tensor_scalar(ends_d[:], ident[0:2, 0:2], ends_m[:], None, ALU.mult).then_inc(redm_done, 1)
            nc.vector.memset(halves[:, 0:1], 2.0).then_inc(redm_done, 1)
            for i in range(1, DESCENT):
                last = nc.vector.memset(halves[:, i:i + 1], 2.0 ** (1 - i))
            chained(last)
            dve.wait_ge(ends_ps, 1)
            nc.vector.tensor_scalar(base[:], B[6][:, 0:1], float(np.log(T / EFFECTIVE)), None, ALU.min).then_inc(dve_misc, 1)
            chained(nc.vector.tensor_copy(step_w[:], B[6][:, 1:2]))
            chained(nc.vector.tensor_scalar(step_w[:].bitcast(I32), step_w[:].bitcast(I32), 0x7F800000, None, ALU.bitwise_and))
            chained(nc.vector.tensor_scalar(widths[:], halves[:], step_w[:], None, ALU.mult))
            chained(nc.vector.tensor_scalar(low[:], step_w[:], -2.0, None, ALU.mult))
            nc.vector.memset(one[:], 1.0).then_inc(dve_misc, 1)
            dve.wait_ge(dve_misc, 2)
            marks = [0]

            def exponentials_from_base():
                marks[0] += 1
                nc.vector.tensor_scalar(args[:], s_tok[:], base[:], CAP, ALU.subtract, ALU.min).then_inc(arg_done, 1)
                dve.wait_ge(f_done, marks[0])

            exponentials_from_base()
            for i in range(DESCENT - 1):
                a_now = one[:] if i == 0 or i in REBASE else B[6][:, 0:1]
                if i > 0:
                    dve.wait_ge(desc_ps, i)
                if i in REBASE:
                    nc.vector.tensor_copy(log_in[:], B[6][:, 0:1]).then_inc(ln_in, 1)
                    dve.wait_ge(ln_done, REBASE.index(i) + 1)
                    chained(nc.vector.tensor_tensor(base[:], base[:], log_a[:], ALU.add))
                    exponentials_from_base()
                nc.vector.tensor_scalar(djunk[:], f_tok[:], a_now, None, ALU.min, ALU.add,
                                        accum_out=dpart[:, 0:1]).then_inc(desc_in, 1)
                if i > 0:
                    dve.wait_ge(cnt_ps, i)
                    chained(nc.vector.tensor_scalar(step_w[:], B[7][:, 0:1], HEAVY - 0.5, widths[:, i - 1:i], ALU.is_ge, ALU.mult))
                    chained(nc.vector.tensor_tensor(low[:], low[:], step_w[:], ALU.add))
                nc.vector.scalar_tensor_tensor(cjunk[:], s_tok[:], low[:], widths[:, i:i + 1].broadcast_to([P, NB]),
                                               ALU.subtract, ALU.is_ge, accum_out=cpart[:, 0:1]).then_inc(cnt_in, 1)
            last_i = DESCENT - 1
            dve.wait_ge(desc_ps, last_i)
            nc.vector.tensor_copy(log_in[:], B[6][:, 0:1]).then_inc(ln_in, 1)
            dve.wait_ge(cnt_ps, last_i)
            chained(nc.vector.tensor_scalar(step_w[:], B[7][:, 0:1], HEAVY - 0.5, widths[:, last_i - 1:last_i], ALU.is_ge, ALU.mult))
            chained(nc.vector.tensor_tensor(low[:], low[:], step_w[:], ALU.add))
            dve.wait_ge(ln_done, len(REBASE) + 1)
            chained(nc.vector.tensor_tensor(theta[:], base[:], log_a[:], ALU.add))
            nc.vector.tensor_scalar(key[:], s_tok[:], theta[:], None, ALU.min).then_inc(key_done, 1)
            chained(nc.vector.tensor_tensor(low[:], low[:], theta[:], ALU.min))
            dve.wait_ge(key_done, 1)
            nc.vector.tensor_scalar(score[:], key[:], theta[:], None, ALU.subtract).then_inc(strict_done, 1)
            nc.vector.tensor_scalar(strict[:], key[:], low[:], None, ALU.is_gt, ALU.add,
                                    accum_out=dpart[:, 1:2]).then_inc(strict_done, 1)
            nc.vector.tensor_scalar(tie[:], key[:], low[:], None, ALU.is_equal).then_inc(tie_done, 1)
            dve.wait_ge(strict_ps, 1)
            nc.vector.tensor_scalar(need[:], B[6][:, 0:1], -1.0, float(HEAVY), ALU.mult, ALU.add).then_inc(dve_misc, 1)
            dve.wait_ge(tot_ps, 1)
            nc.vector.tensor_copy(tot_t[:], B[7][0:NB, 0:P]).then_inc(tot_done, 1)
            dve.wait_ge(dve_misc, 3)
            dve.wait_ge(pre_ps, 1)
            chained(nc.vector.tensor_scalar(fits[:], B[5][:, 0:NB], need[:], None, ALU.is_lt))
            chained(nc.vector.tensor_tensor(fits[:], fits[:], tie[:], ALU.mult))
            chained(nc.vector.tensor_tensor(sel[:], fits[:], strict[:], ALU.add))
            dve.wait_ge(score_done, 1)
            chained(nc.vector.tensor_scalar(fits[:], escore[:], -1.0, 1.0, ALU.mult, ALU.add))
            chained(nc.vector.tensor_tensor(fits[:], fits[:], escore[:], ALU.add))
            chained(nc.vector.tensor_tensor(sel[:], sel[:], fits[:], ALU.mult))
            for q in range(TG):
                chained(nc.vector.tensor_tensor(XE[:, grp(q)], XE[:, grp(q)],
                                                sel[:, grp(q)].unsqueeze(2).broadcast_to([P, GB, C]), ALU.mult))
                chained(nc.vector.tensor_tensor(XE[:, grp(q)], XE[:, grp(q)], XC[:, grp(q)], ALU.add))
                statistics(XE, GB * q, GB * q + GB)
            variances()
            for n in range(NB):
                last = nc.vector.tensor_scalar(XA[:, n, :], XE[:, n, :], mv[:, n, 0:1], rstd[:, n:n + 1], ALU.subtract, ALU.mult)
                if n % GB == GB - 1:
                    last.then_inc(out_ready, 1)

        @block.scalar
        def _(act):
            def exponentials(u, g):
                act.wait_ge(max_done, u + 1)
                wait(act, probsT_ps, u - 1)
                for e in range(2):
                    for pr in range(PAIRS):
                        last = nc.scalar.activation(probs[:, g % 2, e, pr, :], S[:, e, pr, :], ACT.Exp,
                                                    bias=negmax[:, g % 2, e, pr:pr + 1],
                                                    accum_out=total[:, g % 2, e, pr:pr + 1])
                last.then_inc(exp_done, 1)

            def keep_probsT(u, g):
                act.wait_ge(probsT_ps, u + 1)
                wait(act, o_ps, u - 1)
                nc.scalar.copy(probsT[:, g % 2], PT[:].rearrange("p (h q) -> p h q", h=GH)).then_inc(probsT_done, 1)

            def keep_v(n, g):
                act.wait_ge(v_ps, n + 1)
                act.wait_ge(v_tail_done, n + 1)
                nc.scalar.copy(v_own[:, g], V_ps.rearrange("p (h d) -> p h d", h=GH)).then_inc(v_own_done, 1)

            def keep_oT(u, g, b):
                act.wait_ge(o_ps, u + 1)
                wait(act, y_ps, b)
                nc.scalar.copy(oT[:, PAIRS * g:PAIRS * g + PAIRS, :],
                               O_ps[:, 0:PAIRS * P].rearrange("p (n q) -> p n q", n=PAIRS)).then_inc(oT_done, 1)

            def stage_x(b, tok):
                wait(act, v_ps, b * G)
                nc.scalar.copy(xv[:], xnT[:, tok]).then_inc(xv_done, 1)

            def keep_xnT(q):
                act.wait_ge(xt_done, q + 1)
                nc.scalar.copy(xnT[:, 512 * q:512 * q + 512], XT_ps[min(q, 1)][:]).then_inc(xnT_done, 1)

            def steps(b):
                fixed = static(b)
                for g in range(G):
                    u = b * G + g
                    if not fixed or 3 <= u <= UNITS + 2:
                        keep_oT(u - 3, (g - 3) % G, b - (1 if g < 3 else 0))
                    if g == 2 and (not fixed or b < NB - 1):
                        stage_x(b + 1, bass.ts(b + 1, P))
                    if not fixed or u + 1 < UNITS:
                        keep_v(u + 1, (g + 1) % G)
                    if not fixed or 2 <= u <= UNITS + 1:
                        keep_probsT(u - 2, (g - 2) % G)
                    if not fixed or b < NB:
                        exponentials(u, g)
                    if fixed and b == 0 and 1 <= g < TG:
                        keep_xnT(g)

            for dst, src, sem_ in ((wq, w_q, ld_wq), (wk, w_k, ld_wk), (wv, w_v, ld_wv)):
                act.dma_start(dst[:], src).then_inc(sem_, 16)
            act.wait_ge(ld_wq, 16)
            nc.scalar.mul(wq[:], wq[:], SCALE).then_inc(scaled_done, 1)
            keep_xnT(0)
            act.wait_ge(xnT_done, 1)
            stage_x(0, slice(0, P))
            for q in range(1, TG):
                act.wait_ge(ld_x[q], 16)
                for n in range(GB * q, GB * q + GB):
                    last = nc.scalar.activation(xn[:, n, :], x_sb[:, n, :], ACT.Square, accum_out=stat[:, n:n + 1])
            last.then_inc(squares_done, 1)
            keep_v(0, 0)
            steps(0)
            steps(1)
            with act.Fori(2, NB - 1) as b:
                steps(b)
            steps(NB - 1)
            steps(NB)
            grp = lambda q: slice(q * 512, (q + 1) * 512)
            bank4 = lambda b: B[b].rearrange("p (n c) -> p n c", n=GB)

            def from_transposes(stage, q, dst, scale=None, bias=None):
                t = stage * TG + q
                act.wait_ge(tr_ps, t + 1)
                if scale is None:
                    nc.scalar.copy(dst[:, grp(q)], B[t % 2]).then_inc(tr_done, 1)
                else:
                    nc.scalar.activation(dst[:, grp(q)], B[t % 2], ACT.Identity, bias=bias, scale=scale).then_inc(tr_done, 1)

            act.wait_ge(ld_late, 80)
            nc.scalar.mul(W["w_l1"], W["w_l1"], W["gam_l"]).then_inc(gam_done, 1)
            nc.scalar.mul(W["w_h1"], W["w_h1"], W["gam_h"]).then_inc(gam_done, 1)
            for q in range(TG + 1):
                if q < TG:
                    from_transposes(0, q, hT)
                if q >= 1:
                    for j in range(NF):
                        act.wait_ge(hid_ps, NF * (q - 1) + j + 1)
                        nc.scalar.activation(hid[:, j, grp(q - 1)], B[2 + j], ACT.Relu,
                                             bias=W["b_f1"][:, j:j + 1]).then_inc(hid_done, 1)
            for q in range(TG):
                from_transposes(1, q, hT, W["dn_g"], W["dn_b"])
            for n in range(NB):
                act.wait_ge(kv_done, n + 1)
                last = nc.scalar.activation(act_junk[:, n % 2], kv[:, n, 0:C], ACT.Square, accum_out=var_eps[:, n:n + 1])
                last.then_inc(asq, 1)
                act.wait_ge(asq, n + 1)
            nc.scalar.copy(act_one[:], act_junk[:, 0, 0:1]).then_inc(rsq_in, 1)
            khT_flat = khT[:].rearrange("p n c -> p (n c)")
            for q in range(TG):
                from_transposes(2, q, khT_flat)
            for q in range(TG):
                act.wait_ge(gram_ps, q + 1)
                nc.scalar.copy(gram[:, GB * q:GB * q + GB], bank4(6 + q % 2)).then_inc(gram_done, 1)
            for q in range(TG):
                act.wait_ge(ix_ps, q + 1)
                nc.scalar.copy(inv[:, GB * q:GB * q + GB], bank4(q % 2)).then_inc(ix_done, 1)
            for l in range(NLEV):
                for q in range(TG):
                    t = l * TG + q
                    act.wait_ge(bx_ps, t + 1)
                    if l > 0:
                        act.wait_ge(invT_done, (l - 1) * TG + q + 1)
                    nc.scalar.copy(bx[:, GB * q:GB * q + GB], bank4(2 + q % 2)).then_inc(bx_done, 1)
            for m in range(NB // 2):
                act.wait_ge(wv_ps, m + 1)
                nc.scalar.copy(wv2[:, 2 * m:2 * m + 2], B[m % 2].rearrange("p (n c) -> p n c", n=2)).then_inc(wv_done, 1)
            for m in range(NB // 2):
                act.wait_ge(aq_ps, m + 1)
                nc.scalar.mul(naq[:, 2 * m:2 * m + 2], B[2 + m % 2].rearrange("p (n c) -> p n c", n=2), -1.0).then_inc(aq_done, 1)
            act.wait_ge(z_ps, 1)
            nc.scalar.copy(zT[:], B[2][:, 0:C + 1]).then_inc(zb_done, 1)
            act.wait_ge(zb_done, 1)
            nc.scalar.copy(z_bias[:], zT[:, C:C + 1].broadcast_to([P, C])).then_inc(zb_done, 1)
            act.wait_ge(e_ps, 1)
            nc.scalar.copy(e_sb[:], B[3][:, 0:C]).then_inc(e_done, 1)
            for q in range(TG):
                from_transposes(3, q, hT, W["mn_g"], W["mn_b"])
            for q in range(TG):
                act.wait_ge(m1_ps, q + 1)
                nc.scalar.activation(hid[:, 0, grp(q)], B[2 + q % 2], ACT.Relu, bias=W["m_b1"]).then_inc(m1_done, 1)
            for n in range(NB):
                act.wait_ge(x6_done, n + 1)
                nc.scalar.activation(act_junk[:, n % 2], XA[:, n, :], ACT.Square, accum_out=nsq[:, n:n + 1]).then_inc(sq_done, 1)
                act.wait_ge(sq_done, n + 1)
            for q in range(TG):
                from_transposes(4, q, hT)
            for q in range(TG):
                act.wait_ge(l1_ps, q + 1)
                nc.scalar.activation(light[0:LF, grp(q)], B[2][0:LF, :], ACT.Gelu, bias=W["b_l1"][0:LF]).then_inc(l1_done, 1)
                for j in range(NHF):
                    n = NHF * q + j
                    act.wait_ge(h1_ps, n + 1)
                    nc.scalar.activation(hid[:, j, grp(q)], B[3 + n % 2], ACT.Gelu,
                                         bias=W["b_h1"][:, j:j + 1]).then_inc(h1_done, 1)
            for m in range(len(REBASE) + 1):
                act.wait_ge(arg_done, m + 1)
                nc.scalar.activation(f_tok[:], args[:], ACT.Exp).then_inc(f_done, 1)
                act.wait_ge(ln_in, m + 1)
                nc.scalar.activation(log_a[:], log_in[:], ACT.Ln).then_inc(ln_done, 1)
            act.wait_ge(strict_done, 1)
            nc.scalar.activation(escore[:], score[:], ACT.Exp).then_inc(score_done, 1)

        @block.gpsimd
        def _(pool):
            def rope_sum(n, g, b):
                nc.gpsimd.tensor_copy(k_tail[:, g], qk[:, g, PAIRS:, KEEP:]).then_inc(tail_done, 1)
                pool.wait_ge(tail_done, n + 1)
                pool.wait_ge(mul_done, n + 1)
                pool.wait_ge(swapped[g], 64 * (b + 1))
                wait(pool, scores_done, n - G + 1)
                nc.gpsimd.tensor_tensor(qk[:, g], t_cos[:, g], t_swap[:, g], ALU.add).then_inc(sum_done, 1)
                pool.wait_ge(sum_done, n + 1)
                nc.gpsimd.tensor_tensor(k_diff[:, g], k_tail[:, g], qk[:, g, PAIRS:, KEEP:],
                                        ALU.subtract).then_inc(rope_done, 1)

            nc.gpsimd.memset(expo[:], -0.5).then_inc(pool_step, 1)
            nc.gpsimd.memset(qk[:], 0.0).then_inc(pool_step, 1)
            pool.wait_ge(pool_step, 2)

            def inverse_rms(k, n0, n1):
                pool.wait_ge(squares_done, k)
                nc.gpsimd.tensor_scalar(mean2[:, n0:n1], stat[:, n0:n1], 1.0 / C, 1e-6, ALU.mult,
                                        ALU.add).then_inc(sumsq_done, 1)
                pool.wait_ge(sumsq_done, k)
                nc.gpsimd.tensor_tensor(rms[:, n0:n1], mean2[:, n0:n1], expo[:, n0:n1], ALU.pow).then_inc(rms_done, 1)

            inverse_rms(1, 0, GB)
            rope_sum(0, 0, 0)
            inverse_rms(2, GB, NB)
            for g in range(1, G):
                rope_sum(g, g, 0)

            def steps(b):
                for g in range(G):
                    rope_sum(b * G + g + G, g, b + 1)

            steps(0)
            steps(1)
            with pool.Fori(2, NB - 1) as b:
                steps(b)
            grp = lambda q: slice(GB * q, GB * q + GB)
            spread = lambda v: v.unsqueeze(1).broadcast_to([P, GB, C])
            roots = [0]

            def inverse_root():
                roots[0] += 1
                pool.wait_ge(rsq_in, roots[0])
                nc.gpsimd.tensor_tensor(rstd[:], var_eps[:], expo[:], ALU.pow).then_inc(rsq_out, 1)

            pool.wait_ge(ld_late, 80)
            inverse_root()
            for q in range(TG):
                pool.wait_ge(x1_done, GB * (q + 1))
                nc.gpsimd.tensor_tensor(XB[:, grp(q)], XA[:, grp(q)], spread(row["b_f2"]), ALU.add).then_inc(x1b_done, 1)
            inverse_root()
            inverse_root()
            nc.gpsimd.memset(invT[:], 0.0).then_inc(zeroed, 1)
            nc.gpsimd.memset(ones[:], 1.0).then_inc(kset, 1)
            nc.gpsimd.memset(kth[:], 1.0 / EFFECTIVE).then_inc(kset, 1)
            inverse_root()
            pool.wait_ge(gram_done, TG)
            for l in range(1, NLEV):
                pool.wait_ge(bt_done, l)
                nc.gpsimd.tensor_tensor(BT[:, l], gram[:], lmask[:, l:l + 1, :].broadcast_to([P, NB, P]),
                                        ALU.mult).then_inc(bt_done, 1)
            inverse_root()
            for q in range(TG):
                pool.wait_ge(x3_done, q + 1)
                nc.gpsimd.tensor_tensor(XC[:, grp(q)], XD[:, grp(q)], XA[:, grp(q)], ALU.add).then_inc(pool_sum, 1)
                pool.wait_ge(pool_sum, q + 1)
                nc.gpsimd.tensor_tensor(XC[:, grp(q)], XC[:, grp(q)], spread(row["b_m2"]), ALU.add).then_inc(x32_done, 1)
            inverse_root()
            inverse_root()
            for q in range(TG):
                nc.gpsimd.tensor_tensor(XC[:, grp(q)], XA[:, grp(q)], spread(row["b_l2"]), ALU.add).then_inc(x6b_done, 1)
            inverse_root()


def lay_out(inputs):
    f = {k: np.asarray(v) for k, v in inputs.items()}
    channels = f["L0_attn_x"].shape[2]
    inner = f["L0_attn_w_out"].shape[1]
    w_q, w_k, w_v = (np.ascontiguousarray(f["L0_attn_w_qkv"][i * inner:(i + 1) * inner].T) for i in range(3))

    def chunks(w):
        return w.reshape(-1, P, w.shape[1]).transpose(1, 0, 2).reshape(P, -1)

    def column(v):
        if v.shape[0] < P:
            v = np.concatenate([v, np.zeros(P - v.shape[0], v.dtype)])
        return v.reshape(-1, P).T

    def padded(w):
        return np.concatenate([w, np.zeros((P - w.shape[0], w.shape[1]), w.dtype)])

    gates, gates_b = f["L1_attn_gates_w"], f["L1_attn_gates_b"]
    parts = [
        ("w_f1", f["L0_ffn_W1"]), ("w_f2", chunks(f["L0_ffn_W2"])), ("b_f1", column(f["L0_ffn_b1"])),
        ("w_kv", np.concatenate([gates[:, channels:], f["L1_attn_lr_w"]], 1)),
        ("w_qT", np.concatenate([gates[:, :channels].T, gates_b[:channels, None]], 1)),
        ("w_do", f["L1_attn_out_w"]), ("w_m1", f["L1_attn_w1"]), ("w_m2", f["L1_attn_w2"]),
        ("dn_g", column(f["L1_attn_dn_g"])), ("dn_b", column(f["L1_attn_dn_b"])),
        ("mn_g", column(f["L1_attn_mn_g"])), ("mn_b", column(f["L1_attn_mn_b"])), ("m_b1", column(f["L1_attn_b1"])),
        ("w_l1", f["L1_ffn_w1_l"].T), ("b_l1", column(f["L1_ffn_b1_l"])), ("w_l2", padded(f["L1_ffn_w2_l"].T)),
        ("w_h1", f["L1_ffn_w1_h"].T), ("b_h1", column(f["L1_ffn_b1_h"])), ("w_h2", chunks(f["L1_ffn_w2_h"].T)),
        ("gam_l", column(f["L1_ffn_gamma_l"])), ("gam_h", column(f["L1_ffn_gamma_h"])),
    ]
    late, at = {}, 0
    for name, a in parts:
        late[name] = (at, at + a.shape[1])
        at += a.shape[1]
    late["end"] = (at, at)
    arrays = {
        "x": f["L0_attn_x"].reshape(-1, channels),
        "w_q": w_q, "w_k": w_k, "w_v": w_v,
        "w_o": np.ascontiguousarray(f["L0_attn_w_out"].T),
        "late_weights": np.ascontiguousarray(np.concatenate([a for _, a in parts], 1)),
        "row_vectors": np.concatenate([f["L0_ffn_b2"], f["L1_attn_out_b"], f["L1_attn_b2"], f["L1_ffn_b2_l"],
                                       f["L1_ffn_b2_h"], f["L1_ffn_routing_token"]]),
        "kv_bias": np.concatenate([gates_b[channels:], f["L1_attn_lr_b"]]),
    }
    return arrays, late


def kernel(**inputs):
    import concourse.bacc as bacc
    from concourse.bass_utils import run_bass_kernel_spmd

    arrays, late = lay_out(inputs)
    nc = bacc.Bacc("TRN2", target_bir_lowering=False, num_devices=1)
    args = {n: nc.dram_tensor(n, a.shape, F32, kind="ExternalInput").ap() for n, a in arrays.items()}
    tokens, channels = arrays["x"].shape
    out = nc.dram_tensor("out", (tokens, channels), F32, kind="ExternalOutput").ap()
    build(nc, out=out, late=late, **args)
    r = run_bass_kernel_spmd(nc, [arrays], core_ids=[0])
    return r.results[0]["out"].reshape(np.asarray(inputs["L0_attn_x"]).shape)
```

```python
from contextlib import ExitStack

import numpy as np

import concourse.bass as bass
from concourse import mybir

F32 = mybir.dt.float32
BF16 = mybir.dt.bfloat16
I32 = mybir.dt.int32
ALU = mybir.AluOpType
ACT = mybir.ActivationFunctionType
AX_X = mybir.AxisListType.X

P = 128


def static(v):
    return isinstance(v, int)


def wait(eng, sem, value):
    if static(value) and value <= 0:
        return
    eng.wait_ge(sem, value)


def rope_tables(tokens, dim):
    half = dim // 2
    inv = (1.0 / 10000.0 ** (np.arange(0, dim, 2, dtype=np.float32) / np.float32(dim))).astype(np.float32)
    angle = np.outer(np.arange(tokens, dtype=np.float32), inv).astype(np.float32)
    cos, sin = np.cos(angle).T, np.sin(angle).T
    return (np.concatenate([cos] * 4).astype(np.float32),
            np.concatenate([sin, -sin, sin, -sin]).astype(np.float32))


def band_masks(window, blocked):
    q, k = np.arange(P)[:, None], np.arange(P)[None, :]
    own = (k <= q) & (q - k <= window)
    before = (q < window) & (k >= P - window) & (q - (k - P) <= window)
    out = np.stack([np.where(own, 0.0, blocked), np.where(own | before, 0.0, blocked)])
    return out.transpose(1, 0, 2).copy()


def level_masks(size, levels):
    i, j = np.arange(P)[:, None], np.arange(P)[None, :]
    out = []
    for _ in range(levels):
        out.append((i // (2 * size) == j // (2 * size)) & (i // size < j // size))
        size *= 2
    return np.stack(out).astype(np.float32).transpose(1, 0, 2).copy()


def build(nc, x, w_q, w_k, w_v, w_o, late_weights, row_vectors, kv_bias, out, late):
    T, C = x.shape
    INNER = w_v.shape[1]
    D = 64
    WINDOW = 32
    H = INNER // D
    NB = T // P
    G = 4
    GH = H // G
    PAIRS = GH // 2
    KEEP = P - WINDOW
    SCALE = float(D) ** -0.5
    BLOCKED = -1e9
    NCH = INNER // P
    UNITS = NB * G
    TG = T // 512
    GB = NB // TG
    NF = (late["b_f1"][1] - late["b_f1"][0])
    NHF = (late["b_h1"][1] - late["b_h1"][0])
    LF = late["w_l1"][1] - late["w_l1"][0]
    KVW = 2 * C + 1
    SUB = 16
    NSUB = P // SUB
    NLEV = 3
    HEAVY = 128
    EFFECTIVE = HEAVY * 9.0 / 8.0
    DESCENT = 50
    REBASE = (12, 24, 36)
    CAP = 80.0
    PIECES = [("in", 0), ("in", 1), ("out", 0), ("in", 2), ("out", 1), ("in", 3), ("out", 2), ("out", 3)]
    PIECES_EACH = 10
    AHEAD = 2 * PIECES_EACH
    EPS = 1e-5
    assert SUB << NLEV == P and GB * TG == NB and NSUB * NB == P

    def pieces_in(i):
        def start(i):
            return AHEAD + i + 3 * sum(r <= i for r in REBASE)
        if i < 0:
            return range(0)
        total = PIECES_EACH * len(PIECES)
        return range(min(start(i), total), total if i == DESCENT - 2 else min(start(i + 1), total))

    cos_np, sin_np = rope_tables(T, D)
    cos_dram = nc.inline_tensor(cos_np, name="rope_cos").ap()
    sin_dram = nc.inline_tensor(sin_np, name="rope_sin").ap()
    mask_np = band_masks(WINDOW, BLOCKED).astype(mybir.dt.np(BF16))
    mask_dram = nc.inline_tensor(mask_np, name="band_masks").ap()
    ident_dram = nc.inline_tensor(np.eye(P, dtype=np.float32), name="identity_f").ap()
    level_dram = nc.inline_tensor(level_masks(SUB, NLEV), name="level_masks").ap()
    before_dram = nc.inline_tensor(np.triu(np.ones((P, P), np.float32), 1), name="tokens_before").ap()

    with ExitStack() as ctx:
        scope = [ctx]

        def sb(name, shape, dt=F32):
            return scope[0].enter_context(nc.sbuf_tensor(name, shape, dt))

        def bank(name):
            return ctx.enter_context(nc.psum_tensor(name, [P, 512], F32))

        def sem(name):
            return ctx.enter_context(nc.semaphore(name))

        ident = sb("ident", [P, P])
        expo = sb("expo", [P, NB])
        r1 = sb("r1", [P, NB, C])
        mv = sb("mv", [P, NB, 2])
        late_sb = sb("late_sb", [P, late["end"][0]])
        W = {n: late_sb[:, a:b] for n, (a, b) in late.items() if n != "end"}
        rows = sb("rows", [P, 6, C])
        row = {n: rows[:, i, :] for i, n in enumerate(("b_f2", "b_do", "b_m2", "b_l2", "b_h2", "token"))}
        kv_b = sb("kv_b", [P, KVW])
        lmask = sb("lmask", [P, NLEV, P])
        before = sb("before", [P, P])
        bns = sb("bns", [P, NB, 6])
        var_eps = sb("var_eps", [P, NB])
        rstd = sb("rstd", [P, NB])
        rstd2 = sb("rstd2", [P, NB])
        spread_var = sb("spread_var", [P, NB])
        first = ExitStack()
        scope[0] = first
        cos = sb("cos", [P, T])
        sin = sb("sin", [P, T])
        wq = sb("wq", [P, INNER])
        wk = sb("wk", [P, INNER])
        x_sb = sb("x_sb", [P, NB, C])
        ident_bf = sb("ident_bf", [P, P], BF16)
        masks = sb("masks", [P, 2, P], BF16)
        wv = sb("wv", [P, INNER])
        wo = sb("wo", [P, NCH, C])
        xn = sb("xn", [P, NB, C])
        xnT = sb("xnT", [P, T])
        xv = sb("xv", [P, P])
        stat = sb("stat", [P, NB])
        mean2 = sb("mean2", [P, NB])
        rms = sb("rms", [P, NB])
        t_cos = sb("t_cos", [P, G, 4, P])
        t_sin = sb("t_sin", [P, G, 4, P])
        t_swap = sb("t_swap", [P, G, 4, P])
        qk = sb("qk", [P, G, 4, P])
        k_tail = sb("k_tail", [P, G, PAIRS, WINDOW])
        k_diff = sb("k_diff", [P, G, PAIRS, WINDOW])
        negmax = sb("negmax", [P, 2, 2, PAIRS])
        total = sb("total", [P, 2, 2, PAIRS])
        inv_total = sb("inv_total", [P, 2, 2, PAIRS])
        probs = sb("probs", [P, 2, 2, PAIRS, P])
        probsT = sb("probsT", [P, 2, GH, P])
        v_own = sb("v_own", [P, G, GH, D])
        v_mix = sb("v_mix", [P, G, GH, D])
        oT = sb("oT", [P, NCH, P])
        first.close()

        scope[0] = ctx
        XA = sb("XA", [P, NB, C])
        XB = sb("XB", [P, NB, C])
        hT = sb("hT", [P, T])
        XC = sb("XC", [P, NB, C])
        XD = sb("XD", [P, NB, C])
        XE = sb("XE", [P, NB, C])
        act_junk = sb("act_junk", [P, C])
        score_junk = sb("score_junk", [P, C])
        kth = sb("kth", [P, P])
        ones = sb("ones", [P, P])
        ones_bf = sb("ones_bf", [P, P], BF16)
        second = ExitStack()
        scope[0] = second
        kv = sb("kv", [P, NB, KVW + 3])
        khT = sb("khT", [P, NB, C])
        gram = sb("gram", [P, NB, P])
        l16 = sb("l16", [P, SUB, SUB])
        x16 = sb("x16", [P, SUB, SUB])
        prod = sb("prod", [P, SUB, SUB])
        BT = sb("BT", [P, NLEV, NB, P])
        invT = sb("invT", [P, NB, P])
        inv = sb("inv", [P, NB, P])
        bx = sb("bx", [P, NB, P])
        naq = sb("naq", [P, NB, 2 * C])
        state = sb("state", [P, NB, C])
        wv2 = sb("wv2", [P, NB, 2 * C])
        g_sb = sb("g_sb", [P, C])
        zT = sb("zT", [P, C + 1])
        z_bias = sb("z_bias", [P, C])
        e_sb = sb("e_sb", [P, C])
        delta_bias = sb("delta_bias", [P, C])
        dk = khT
        second.close()
        scope[0] = ctx
        hid = sb("hid", [P, max(NF, NHF), T])
        light = sb("light", [P, T])
        s_tok = sb("s_tok", [P, NB])
        f_tok = sb("f_tok", [P, NB])
        args = sb("args", [P, NB])
        log_in = sb("log_in", [P, 1])
        one = sb("one", [P, 1])
        escore = sb("escore", [P, NB])
        djunk = sb("djunk", [P, NB])
        cjunk = sb("cjunk", [P, NB])
        dpart = sb("dpart", [P, 2])
        cpart = sb("cpart", [P, 1], BF16)
        widths = sb("widths", [P, DESCENT])
        halves = sb("halves", [P, DESCENT])
        ends = sb("ends", [P, 2])
        ends_t = sb("ends_t", [2, P])
        ends_m = sb("ends_m", [2, 1])
        ends_d = sb("ends_d", [2, 2])
        base = sb("base", [P, 1])
        log_a = sb("log_a", [P, 1])
        theta = sb("theta", [P, 1])
        low = sb("low", [P, 1])
        step_w = sb("step_w", [P, 1])
        need = sb("need", [P, 1])
        key = sb("key", [P, NB])
        strict = sb("strict", [P, NB])
        tie = sb("tie", [P, NB])
        fits = sb("fits", [P, NB])
        tot_t = sb("tot_t", [NB, P])
        sel = sb("sel", [P, NB])
        score = sb("score", [P, NB])

        gram_dram = nc.dram_tensor("gram_dram", [NB, P, P], F32).ap()
        blocks_in = nc.dram_tensor("blocks_in", [NSUB, NB, SUB, SUB], F32).ap()
        S_banks = ctx.enter_context(nc.psum_tensor("S", [P, 2, 4, P], F32))
        S = S_banks[:, :, 0:PAIRS, :]
        QK = [bank("QK0"), bank("QK1")]
        PT = bank("PT")
        V_bank, Y_bank = bank("V"), bank("Y")
        V_ps, Y_ps = V_bank[:, 0:GH * D], Y_bank[:, 0:C]
        O_ps = bank("O")
        XT_ps = [PT, Y_bank]

        B = [S_banks[:, 0].rearrange("p a k -> p (a k)"), S_banks[:, 1].rearrange("p a k -> p (a k)"),
             QK[0][:], QK[1][:], PT[:], V_bank[:], Y_bank[:], O_ps[:]]

        ld_x = [sem(f"ld_x{q}") for q in range(TG)]
        ld_ident, ld_masks, ld_wq, ld_wk, ld_wv, ld_wo = (sem("ld_" + n) for n in
                                                          ("ident", "masks", "wq", "wk", "wv", "wo"))
        ld_rope = [sem(f"ld_rope{q}") for q in range(3)]
        swapped = [sem(f"swapped{g}") for g in range(G)]
        stored = sem("stored")
        dve_step = sem("dve_step")
        pool_step = sem("pool_step")
        act_step = sem("act_step")
        sumsq_done = sem("sumsq_done")
        rms_done = sem("rms_done")
        squares_done = sem("squares_done")
        xn_done = sem("xn_done")
        xt_done = sem("xt_done")
        xnT_done = sem("xnT_done")
        cast_done = sem("cast_done")
        zero_done = sem("zero_done")
        scores_done = sem("scores_done")
        max_done = sem("max_done")
        exp_done = sem("exp_done")
        norm_done = sem("norm_done")
        probsT_ps = sem("probsT_ps")
        probsT_done = sem("probsT_done")
        qk_ps = sem("qk_ps")
        mul_done = sem("mul_done")
        rope_done = sem("rope_done")
        xv_done = sem("xv_done")
        v_ps = sem("v_ps")
        v_own_done = sem("v_own_done")
        v_tail_done = sem("v_tail_done")
        v_mix_done = sem("v_mix_done")
        o_ps = sem("o_ps")
        oT_done = sem("oT_done")
        y_ps = sem("y_ps")
        r1_done = sem("r1_done")
        inv_done = sem("inv_done")
        bn_done = sem("bn_done")
        mv1_done = sem("mv1_done")
        tail_done = sem("tail_done")
        scaled_done = sem("scaled_done")
        sum_done = sem("sum_done")
        ld_late = sem("ld_late")
        late_cast = sem("late_cast")
        rsq_in = sem("rsq_in")
        rsq_out = sem("rsq_out")
        rsq2_out = sem("rsq2_out")
        ld_gram = sem("ld_gram")
        x1_done = sem("x1_done")
        x1b_done = sem("x1b_done")
        tr_src = sem("tr_src")
        tr_ps = sem("tr_ps")
        tr_done = sem("tr_done")
        hid_ps = sem("hid_ps")
        hid_done = sem("hid_done")
        y2_ps = sem("y2_ps")
        r2_done = sem("r2_done")
        kv_ps = sem("kv_ps")
        kv_done = sem("kv_done")
        kh_done = sem("kh_done")
        kh_T = sem("kh_T")
        gram_ps = sem("gram_ps")
        gram_done = sem("gram_done")
        l16_done = sem("l16_done")
        x16_done = sem("x16_done")
        invT_ld = sem("invT_ld")
        bt_done = sem("bt_done")
        bx_ps = sem("bx_ps")
        bx_done = sem("bx_done")
        xbx_ps = sem("xbx_ps")
        inv_done2 = sem("inv_done2")
        xbxt_ps = sem("xbxt_ps")
        invT_done = sem("invT_done")
        ix_ps = sem("ix_ps")
        ix_done = sem("ix_done")
        wv_ps = sem("wv_ps")
        wv_done = sem("wv_done")
        dk_done = sem("dk_done")
        aq_ps = sem("aq_ps")
        aq_done = sem("aq_done")
        st_ps = sem("st_ps")
        st_done = sem("st_done")
        g_ps = sem("g_ps")
        g_done = sem("g_done")
        z_ps = sem("z_ps")
        z_done = sem("z_done")
        zb_done = sem("zb_done")
        e_ps = sem("e_ps")
        e_done = sem("e_done")
        db_ps = sem("db_ps")
        db_done = sem("db_done")
        x3_ps = sem("x3_ps")
        x3_done = sem("x3_done")
        x32_done = sem("x32_done")
        m1_ps = sem("m1_ps")
        m1_done = sem("m1_done")
        m2_ps = sem("m2_ps")
        r3_done = sem("r3_done")
        x6_done = sem("x6_done")
        x6b_done = sem("x6b_done")
        s_done = sem("s_done")
        l1_ps = sem("l1_ps")
        l1_done = sem("l1_done")
        h1_ps = sem("h1_ps")
        h1_done = sem("h1_done")
        l2_ps = sem("l2_ps")
        base_done = sem("base_done")
        h2_ps = sem("h2_ps")
        heavy_done = sem("heavy_done")
        red_done = sem("red_done")
        redT_ps = sem("redT_ps")
        redm_done = sem("redm_done")
        ends_ps = sem("ends_ps")
        desc_in = sem("desc_in")
        desc_ps = sem("desc_ps")
        cnt_in = sem("cnt_in")
        cnt_ps = sem("cnt_ps")
        arg_done = sem("arg_done")
        f_done = sem("f_done")
        ln_in = sem("ln_in")
        ln_done = sem("ln_done")
        low_done = sem("low_done")
        key_done = sem("key_done")
        strict_done = sem("strict_done")
        strict_ps = sem("strict_ps")
        tie_done = sem("tie_done")
        tot_ps = sem("tot_ps")
        tot_done = sem("tot_done")
        pre_ps = sem("pre_ps")
        score_done = sem("score_done")
        final_done = sem("final_done")
        out_ready = sem("out_ready")
        zeroed = sem("zeroed")
        gam_done = sem("gam_done")
        blocks_kept = sem("blocks_kept")
        inverses_kept = sem("inverses_kept")
        mv_all = sem("mv_all")
        x2_done = sem("x2_done")
        x16_set = sem("x16_set")
        dve_misc = sem("dve_misc")
        sq_done = sem("sq_done")
        asq = sem("asq")
        kset = sem("kset")
        pool_sum = sem("pool_sum")
        xbias_done = sem("xbias_done")
        tr_mn = sem("tr_mn")

        block = ctx.enter_context(nc.Block())

        @block.sync
        def _(sp):
            def load_x(q):
                sp.dma_start(x_sb[:, GB * q:GB * q + GB, :],
                             x[512 * q:512 * q + 512, :].rearrange("(n p) c -> p n c", p=P)).then_inc(ld_x[q], 16)

            def swap_halves(n, g, b):
                sp.wait_ge(mul_done, n + 1)
                for r in range(0, P, D // 2):
                    other = r ^ (D // 2)
                    sp.dma_start(t_swap[other:other + D // 2, g], t_sin[r:r + D // 2, g]).then_inc(swapped[g], 16)

            def load_rope(h, cols):
                sp.dma_start(cos[:, cols], cos_dram[:, cols]).then_inc(ld_rope[h], 16)
                sp.dma_start(sin[:, cols], sin_dram[:, cols]).then_inc(ld_rope[h], 16)

            def swap_steps(b):
                for g in range(G):
                    swap_halves(b * G + g + G, g, b + 1)

            load_x(0)
            sp.dma_start(ident[:], ident_dram).then_inc(ld_ident, 16)
            load_rope(0, slice(0, P))
            load_x(1)
            sp.dma_start(masks[:], mask_dram).then_inc(ld_masks, 16)
            for q in range(2, TG):
                load_x(q)
            load_rope(1, slice(P, 4 * P))
            for g in range(G):
                swap_halves(g, g, 0)
            sp.dma_start(wo[:], w_o.rearrange("(n p) c -> p n c", p=P)).then_inc(ld_wo, 16)
            swap_steps(0)
            load_rope(2, slice(4 * P, T))
            swap_steps(1)
            sp.dma_start(late_sb[:], late_weights).then_inc(ld_late, 16)
            sp.dma_start(rows[:].rearrange("p a c -> p (a c)"), row_vectors.unsqueeze(0).broadcast_to([P, 6 * C])).then_inc(ld_late, 16)
            sp.dma_start(kv_b[:], kv_bias.unsqueeze(0).broadcast_to([P, KVW])).then_inc(ld_late, 16)
            sp.dma_start(lmask[:], level_dram).then_inc(ld_late, 16)
            sp.dma_start(before[:], before_dram).then_inc(ld_late, 16)
            with sp.Fori(2, NB - 1) as b:
                swap_steps(b)
            for q in range(TG):
                sp.wait_ge(gram_done, q + 1)
                sp.dma_start(gram_dram[GB * q:GB * q + GB].rearrange("n r k -> r n k"),
                             gram[:, GB * q:GB * q + GB]).then_inc(blocks_kept, 16)
            sp.wait_ge(blocks_kept, 16 * TG)
            for j in range(NSUB):
                r = slice(SUB * j, SUB * j + SUB)
                (sp if j % 2 == 0 else sp).dma_start(l16[NB * j:NB * j + NB], gram_dram[:, r, r]).then_inc(l16_done, 16)
            sp.wait_ge(x16_done, 1)
            sp.dma_start(blocks_in.rearrange("j n k r -> (j n) k r"), x16[:]).then_inc(inverses_kept, 16)
            sp.wait_ge(inverses_kept, 16)
            sp.wait_ge(zeroed, 1)
            for j in range(NSUB):
                r = slice(SUB * j, SUB * j + SUB)
                sp.dma_start(invT[r, :, r], blocks_in[j].rearrange("n k r -> k n r")).then_inc(invT_ld, 16)
            out_v = out.rearrange("(n p) c -> p n c", p=P)
            for q in range(TG):
                sp.wait_ge(out_ready, q + 1)
                sp.dma_start(out_v[:, GB * q:GB * q + GB], XA[:, GB * q:GB * q + GB]).then_inc(stored, 16)
            sp.wait_ge(stored, 16 * TG)

        @block.tensor
        def _(pe):
            def project_qk(n, g, tok):
                wait(pe, mul_done, n - 1)
                for j, w in enumerate((wq, wk)):
                    for pr in range(PAIRS):
                        f = slice((PAIRS * g + pr) * P, (PAIRS * g + pr + 1) * P)
                        c = slice((PAIRS * j + pr) * P, (PAIRS * j + pr + 1) * P)
                        last = nc.tensor.matmul(QK[g % 2][:, c], w[:, f], xnT[:, tok], start=True, stop=True)
                last.then_inc(qk_ps, 1)

            def project_v(n, g, b):
                pe.wait_ge(xv_done, b + 1)
                wait(pe, v_own_done, n)
                nc.tensor.matmul(V_ps, xv[:], wv[:, g * GH * D:(g + 1) * GH * D], start=True,
                                 stop=True).then_inc(v_ps, 1)

            def scores(u, g, variant):
                s = S
                pe.wait_ge(rope_done, u + 1)
                wait(pe, exp_done, u)
                for e in range(2):
                    nc.tensor.matmul(s[:, e], ident_bf[:], masks[:, variant:variant + 1, :].broadcast_to([P, PAIRS, P]),
                                     start=True, stop=False, skip_group_check=True)
                for pr in range(PAIRS):
                    for e in range(2):
                        r = slice(D * e, D * e + D)
                        q, k = qk[r, g, pr, :], qk[r, g, PAIRS + pr, :]
                        nc.tensor.matmul(s[:, e, pr], q, k, start=False, stop=True, skip_group_check=True)
                for pr in range(PAIRS):
                    for e in range(2):
                        r = slice(D * e, D * e + D)
                        last = nc.tensor.matmul(s[0:WINDOW, e, pr, KEEP:], qk[r, g, pr, 0:WINDOW],
                                                k_diff[r, g, pr, :], start=False, stop=True, skip_group_check=True)
                last.then_inc(scores_done, 1)

            def transpose_probs(u, g):
                pe.wait_ge(norm_done, u + 1)
                wait(pe, probsT_done, u)
                for h in range(GH):
                    last = nc.tensor.transpose(PT[:, h * P:(h + 1) * P], probs[:, g % 2, h % 2, h // 2, :], ident[:])
                last.then_inc(probsT_ps, 1)

            def attend(u, g):
                pe.wait_ge(probsT_done, u + 1)
                pe.wait_ge(v_mix_done, u + 1)
                wait(pe, oT_done, u)
                for h in range(GH):
                    r = slice(D * (h % 2), D * (h % 2) + D)
                    c = (h // 2) * P
                    nc.tensor.matmul(O_ps[r, c + WINDOW:c + P], v_own[:, g, h, :],
                                     probsT[:, g % 2, h, WINDOW:P], start=True, stop=True)
                    last = nc.tensor.matmul(O_ps[r, c:c + WINDOW], v_mix[:, g, h, :],
                                            probsT[:, g % 2, h, 0:WINDOW], start=True, stop=True)
                last.then_inc(o_ps, 1)

            def project_out(b):
                pe.wait_ge(oT_done, G * b + G)
                wait(pe, r1_done, b)
                if static(b) and b == 0:
                    pe.wait_ge(xnT_done, TG)
                    pe.wait_ge(ld_wo, 16)
                for n in range(NCH):
                    last = nc.tensor.matmul(Y_ps, oT[:, n, :], wo[:, n, :], start=(n == 0), stop=(n == NCH - 1))
                last.then_inc(y_ps, 1)

            def transpose_x(q):
                pe.wait_ge(xn_done, GB * q + GB)
                wait(pe, xnT_done, q)
                for i in range(GB):
                    last = nc.tensor.transpose(XT_ps[min(q, 1)][:, i * P:(i + 1) * P], xn[:, GB * q + i, :], ident[:])
                last.then_inc(xt_done, 1)

            def steps(b):
                fixed = static(b)
                for g in range(G):
                    u = b * G + g
                    if not fixed or b < NB:
                        scores(u, g, 0 if fixed and b == 0 else 1)
                    if not fixed or b < NB - 1:
                        project_qk(u + G, g, bass.ts(b + 1, P))
                    if g == 2 and (not fixed or b >= 1):
                        project_out(b - 1)
                    if not fixed or 2 <= u <= UNITS + 1:
                        attend(u - 2, (g - 2) % G)
                    if not fixed or 1 <= u <= UNITS:
                        transpose_probs(u - 1, (g - 1) % G)
                    if fixed and b == 0 and 1 <= g < TG:
                        transpose_x(g)
                    if not fixed or u + 2 < UNITS:
                        project_v(u + 2, (g + 2) % G, b + (g + 2) // G)

            pe.wait_ge(ld_ident, 16)
            transpose_x(0)
            pe.wait_ge(xnT_done, 1)
            pe.wait_ge(scaled_done, 1)
            pe.wait_ge(ld_wk, 16)
            for g in range(G):
                project_qk(g, g, slice(0, P))
            pe.wait_ge(ld_wv, 16)
            for g in range(2):
                project_v(g, g, 0)
            pe.wait_ge(ld_masks, 16)
            pe.wait_ge(cast_done, 1)
            steps(0)
            steps(1)
            with pe.Fori(2, NB - 1) as b:
                steps(b)
            steps(NB - 1)
            steps(NB)
            tok = lambda n: slice(n * P, (n + 1) * P)
            grp = lambda q: slice(q * 512, (q + 1) * 512)

            def to_channels(stage, q, src, arrived, count):
                t = stage * TG + q
                pe.wait_ge(arrived, count)
                wait(pe, tr_done, t - 1)
                for i in range(GB):
                    last = nc.tensor.transpose(B[t % 2][:, tok(i)], src(GB * q + i), ident[:])
                last.then_inc(tr_ps, 1)

            pe.wait_ge(ld_late, 80)

            def hidden1(q):
                pe.wait_ge(tr_done, q + 1)
                for j in range(NF):
                    n = NF * q + j
                    wait(pe, hid_done, n - 3)
                    nc.tensor.matmul(B[2 + j], W["w_f1"][:, tok(j)], hT[:, grp(q)], start=True,
                                     stop=True).then_inc(hid_ps, 1)

            def out1(q):
                pe.wait_ge(hid_done, NF * (q + 1))
                wait(pe, r2_done, q - 1)
                for i in range(GB):
                    for j in range(NF):
                        last = nc.tensor.matmul(B[6 + q % 2][:, tok(i)], hid[:, j, tok(GB * q + i)],
                                                W["w_f2"][:, tok(j)], start=(j == 0), stop=(j == NF - 1))
                last.then_inc(y2_ps, 1)

            for q in range(TG):
                to_channels(0, q, lambda n: XA[:, n, :], x1_done, q + 1)
                if q >= 1:
                    hidden1(q - 1)
                if q >= 2:
                    out1(q - 2)
            hidden1(TG - 1)
            out1(TG - 2)
            out1(TG - 1)

            def keys_and_values(q):
                pe.wait_ge(tr_done, TG + q + 1)
                for n in range(GB * q, GB * q + GB):
                    wait(pe, kv_done, n - 3)
                    nc.tensor.matmul(B[2 + n % 4][:, 0:KVW], hT[:, tok(n)], W["w_kv"], start=True,
                                     stop=True).then_inc(kv_ps, 1)

            def key_products(q):
                pe.wait_ge(tr_done, 2 * TG + q + 1)
                wait(pe, gram_done, q - 1)
                for i in range(GB):
                    n = GB * q + i
                    last = nc.tensor.matmul(B[6 + q % 2][:, tok(i)], khT[:, n, :], khT[:, n, :], start=True, stop=True)
                last.then_inc(gram_ps, 1)

            for s in range(TG + 1):
                if s < TG:
                    to_channels(1, s, lambda n: XB[:, n, :], tr_src, s + 1)
                if s >= 1:
                    keys_and_values(s - 1)
            for s in range(TG + 1):
                if s < TG:
                    to_channels(2, s, lambda n: kv[:, n, 0:C], kh_done, s + 1)
                if s >= 1:
                    key_products(s - 1)
            pe.wait_ge(invT_ld, 16 * NSUB)
            pe.wait_ge(gram_done, TG)
            for q in range(TG):
                wait(pe, ix_done, q - 1)
                for i in range(GB):
                    last = nc.tensor.transpose(B[q % 2][:, tok(i)], invT[:, GB * q + i, :], ident[:])
                last.then_inc(ix_ps, 1)
            for l in range(NLEV):
                final = l == NLEV - 1
                pe.wait_ge(bt_done, l + 1)
                for q in range(TG):
                    t = l * TG + q
                    if l == 0:
                        pe.wait_ge(ix_done, q + 1)
                    else:
                        pe.wait_ge(inv_done2, (l - 1) * TG + q + 1)
                    wait(pe, bx_done, t - 1)
                    for i in range(GB):
                        n = GB * q + i
                        last = nc.tensor.matmul(B[2 + q % 2][:, tok(i)], BT[:, l, n, :], inv[:, n, :], start=True, stop=True)
                    last.then_inc(bx_ps, 1)
                for q in range(TG):
                    t = l * TG + q
                    pe.wait_ge(bx_done, t + 1)
                    wait(pe, invT_done, t - 1)
                    if l > 0:
                        pe.wait_ge(invT_done, (l - 1) * TG + q + 1)
                    for i in range(GB):
                        n = GB * q + i
                        if not final:
                            nc.tensor.matmul(B[4 + q % 2][:, tok(i)], invT[:, n, :], bx[:, n, :], start=True, stop=True)
                        last = nc.tensor.matmul(B[6 + q % 2][:, tok(i)], bx[:, n, :], invT[:, n, :], start=True, stop=True)
                    last.then_inc(xbxt_ps, 1)
            for m in range(NB // 2):
                wait(pe, wv_done, m - 1)
                pe.wait_ge(invT_done, (NLEV - 1) * TG + m // 2 + 1)
                for i in range(2):
                    n = 2 * m + i
                    last = nc.tensor.matmul(B[m % 2][:, 256 * i:256 * i + 256], invT[:, n, :], kv[:, n, 0:2 * C],
                                            start=True, stop=True)
                last.then_inc(wv_ps, 1)
            for m in range(NB // 2):
                pe.wait_ge(wv_done, m + 1)
                pe.wait_ge(dk_done, m // 2 + 1)
                wait(pe, aq_done, m - 1)
                for i in range(2):
                    n = 2 * m + i
                    nc.tensor.matmul(B[2 + m % 2][:, 256 * i:256 * i + C], wv2[:, n, 0:C], kv[:, n, 0:C],
                                     start=True, stop=True)
                    last = nc.tensor.matmul(B[2 + m % 2][:, 256 * i + C:256 * i + 256], wv2[:, n, 0:C], dk[:, n, :],
                                            start=True, stop=True)
                last.then_inc(aq_ps, 1)
            for n in range(NB):
                if n > 0:
                    pe.wait_ge(aq_done, n // 2 + 1)
                    pe.wait_ge(st_done, n)
                if n < NB - 1:
                    last = nc.tensor.matmul(B[6][:, 0:C], kv[:, n, 0:C], wv2[:, n, C:], start=(n == 0), stop=(n == 0),
                                            skip_group_check=True)
                    if n > 0:
                        last = nc.tensor.matmul(B[6][:, 0:C], naq[:, n, 0:C], state[:, n, :], start=False, stop=True,
                                                skip_group_check=True)
                    last.then_inc(st_ps, 1)
                last = nc.tensor.matmul(B[7][:, 0:C], dk[:, n, :], wv2[:, n, C:], start=(n == 0), stop=False,
                                        skip_group_check=True)
                if n > 0:
                    last = nc.tensor.matmul(B[7][:, 0:C], naq[:, n, C:], state[:, n, :], start=False, stop=(n == NB - 1),
                                            skip_group_check=True)
            last.then_inc(g_ps, 1)
            pe.wait_ge(g_done, 1)
            nc.tensor.matmul(B[2][:, 0:C + 1], g_sb[:], W["w_qT"], start=True, stop=True).then_inc(z_ps, 1)
            pe.wait_ge(zb_done, 2)
            nc.tensor.matmul(B[3][:, 0:C], zT[:, 0:C], W["w_do"], start=True, stop=True).then_inc(e_ps, 1)
            nc.tensor.matmul(B[4][:, 0:C], z_bias[:], W["w_do"], start=True, stop=True).then_inc(db_ps, 1)
            pe.wait_ge(e_done, 1)
            for q in range(TG):
                wait(pe, x3_done, q - 1)
                for i in range(GB):
                    last = nc.tensor.matmul(B[6 + q % 2][:, tok(i)], hT[:, tok(GB * q + i)], e_sb[:], start=True, stop=True)
                last.then_inc(x3_ps, 1)

            for s in range(TG + 2):
                if s < TG:
                    to_channels(3, s, lambda n: XB[:, n, :], tr_mn, s + 1)
                if 1 <= s <= TG:
                    q = s - 1
                    pe.wait_ge(tr_done, 3 * TG + q + 1)
                    wait(pe, m1_done, q - 1)
                    nc.tensor.matmul(B[2 + q % 2], W["w_m1"], hT[:, grp(q)], start=True, stop=True).then_inc(m1_ps, 1)
                if s >= 2:
                    q = s - 2
                    pe.wait_ge(m1_done, q + 1)
                    wait(pe, r3_done, q - 1)
                    for i in range(GB):
                        last = nc.tensor.matmul(B[6 + q % 2][:, tok(i)], hid[:, 0, tok(GB * q + i)], W["w_m2"],
                                                start=True, stop=True)
                    last.then_inc(m2_ps, 1)

            def ffn_piece(p):
                side, q = PIECES[p // PIECES_EACH]
                part = p % PIECES_EACH
                half = part % 2
                if side == "in" and part < 2:
                    if half == 0:
                        pe.wait_ge(gam_done, 2)
                        pe.wait_ge(tr_done, 4 * TG + q + 1)
                        wait(pe, l1_done, q)
                    c = slice(q * 512 + 256 * half, q * 512 + 256 * half + 256)
                    last = nc.tensor.matmul(B[5][0:LF, 256 * half:256 * half + 256], W["w_l1"], hT[:, c],
                                            start=True, stop=True)
                    if half == 1:
                        last.then_inc(l1_ps, 1)
                elif side == "in":
                    j = part // 2 - 1
                    n = NHF * q + j
                    if half == 0:
                        wait(pe, h1_done, n - 1)
                    c = slice(q * 512 + 256 * half, q * 512 + 256 * half + 256)
                    last = nc.tensor.matmul(B[3 + n % 2][:, 256 * half:256 * half + 256], W["w_h1"][:, tok(j)],
                                            hT[:, c], start=True, stop=True)
                    if half == 1:
                        last.then_inc(h1_ps, 1)
                elif part < 2:
                    if half == 0:
                        pe.wait_ge(tr_done, 5 * TG)
                        pe.wait_ge(l1_done, q + 1)
                        wait(pe, base_done, q)
                    for i in range(2 * half, 2 * half + 2):
                        last = nc.tensor.matmul(B[0][:, tok(i)], light[0:LF, tok(GB * q + i)], W["w_l2"][0:LF],
                                                start=True, stop=True)
                    if half == 1:
                        last.then_inc(l2_ps, 1)
                else:
                    i = part // 2 - 1
                    if part == 2:
                        pe.wait_ge(h1_done, NHF * (q + 1))
                        wait(pe, heavy_done, q)
                    for j in range(NHF // 2 * half, NHF // 2 * (half + 1)):
                        last = nc.tensor.matmul(B[2][:, tok(i)], hid[:, j, tok(GB * q + i)], W["w_h2"][:, tok(j)],
                                                start=(j == 0), stop=(j == NHF - 1))
                    if part == PIECES_EACH - 1:
                        last.then_inc(h2_ps, 1)

            for q in range(TG):
                to_channels(4, q, lambda n: XB[:, n, :], tr_src, TG + q + 1)
                if q == 1 or q == 3:
                    for p in range(PIECES_EACH * (q // 2), PIECES_EACH * (q // 2 + 1)):
                        ffn_piece(p)

            pe.wait_ge(red_done, 2)
            pe.wait_ge(kset, 3)
            nc.tensor.transpose(B[6][0:2, 0:P], ends[:], ident[:]).then_inc(redT_ps, 1)
            pe.wait_ge(redm_done, 2)
            nc.tensor.matmul(B[6][:, 0:2], ones[0:2, :], ends_d[:], start=True, stop=True).then_inc(ends_ps, 1)
            for i in range(DESCENT - 1):
                pe.wait_ge(desc_in, i + 1)
                nc.tensor.matmul(B[6][:, 0:1], kth[:], dpart[:, 0:1], start=True, stop=True).then_inc(desc_ps, 1)
                for p in pieces_in(i):
                    ffn_piece(p)
                pe.wait_ge(cnt_in, i + 1)
                nc.tensor.matmul(B[7][:, 0:1], ones_bf[:], cpart[:, 0:1], start=True, stop=True).then_inc(cnt_ps, 1)
            pe.wait_ge(strict_done, 2)
            nc.tensor.matmul(B[6][:, 0:1], ones[:], dpart[:, 1:2], start=True, stop=True).then_inc(strict_ps, 1)
            pe.wait_ge(tie_done, 1)
            nc.tensor.matmul(B[7][0:NB, 0:P], tie[:], ones[:], start=True, stop=True).then_inc(tot_ps, 1)
            pe.wait_ge(tot_done, 1)
            nc.tensor.matmul(B[5][:, 0:NB], before[:], tie[:], start=True, stop=False)
            nc.tensor.matmul(B[5][:, 0:NB], tot_t[:], before[0:NB, 0:NB], start=False, stop=True).then_inc(pre_ps, 1)

        @block.vector
        def _(dve):
            count = [0]

            def chained(ins):
                count[0] += 1
                ins.then_inc(dve_step, 1)
                dve.wait_ge(dve_step, count[0])

            def rope_products(n, g, tok):
                dve.wait_ge(qk_ps, n + 1)
                wait(dve, rope_done, n - 3)
                for dst, table in ((t_cos, cos), (t_sin, sin)):
                    last = nc.vector.tensor_tensor(dst[:, g], QK[g % 2][:].rearrange("p (j t) -> p j t", j=4),
                                                   table[:, tok].unsqueeze(1).broadcast_to([P, 4, P]), ALU.mult)
                last.then_inc(mul_done, 1)

            def row_max(u, g):
                dve.wait_ge(scores_done, u + 1)
                nc.vector.tensor_reduce(negmax[:, g % 2], S, AX_X,
                                        ALU.max, negate=True).then_inc(max_done, 1)

            def normalise(u, g):
                dve.wait_ge(exp_done, u + 1)
                nc.vector.reciprocal(inv_total[:, g % 2], total[:, g % 2]).then_inc(inv_done, 1)
                dve.wait_ge(inv_done, u + 1)
                nc.vector.tensor_tensor(probs[:, g % 2], probs[:, g % 2],
                                        inv_total[:, g % 2].unsqueeze(3).broadcast_to([P, 2, PAIRS, P]),
                                        ALU.mult).then_inc(norm_done, 1)

            def keep_v_tail(n, g):
                wait(dve, o_ps, n - G + 1)
                nc.vector.tensor_copy(v_mix[KEEP:P, g], v_own[KEEP:P, g]).then_inc(v_tail_done, 1)

            def mix_v(n, g):
                dve.wait_ge(v_own_done, n + 1)
                nc.vector.tensor_copy(v_mix[0:KEEP, g], v_own[0:KEEP, g]).then_inc(v_mix_done, 1)

            def residual(b, tile):
                dve.wait_ge(y_ps, b + 1)
                nc.vector.tensor_tensor(r1[:, tile, :], x_sb[:, tile, :], Y_ps.unsqueeze(1), ALU.add).then_inc(r1_done, 1)

            roots = [0]
            mv_count = [0]

            def norm_request(src, q):
                for n in range(GB * q, GB * q + GB):
                    last = nc.vector.bn_stats(bns[:, n, :], src[:, n, :])
                chained(last)
                for n in range(GB * q, GB * q + GB):
                    last = nc.vector.bn_aggr(mv[:, n, :], bns[:, n, :])
                chained(last)
                nc.vector.tensor_scalar(var_eps[:, GB * q:GB * q + GB], mv[:, GB * q:GB * q + GB, 1], EPS, None,
                                        ALU.add).then_inc(rsq_in, 1)
                roots[0] += 1

            def standardise(dst, src, q, done):
                dve.wait_ge(rsq_out, roots[0] - (roots[0] - 1 - q) % TG)
                for n in range(GB * q, GB * q + GB):
                    last = nc.vector.tensor_scalar(dst[:, n, :], src[:, n, :], mv[:, n, 0:1], rstd[:, n:n + 1],
                                                   ALU.subtract, ALU.mult)
                last.then_inc(done, 1)

            def normalise_x(q):
                dve.wait_ge(rms_done, 1 if q == 0 else 2)
                dve.wait_ge(ld_x[q], 16)
                for n in range(GB * q, GB * q + GB):
                    nc.vector.tensor_scalar(xn[:, n, :], x_sb[:, n, :], rms[:, n:n + 1], None, ALU.mult).then_inc(xn_done, 1)

            def steps(b):
                fixed = static(b)
                for g in range(G):
                    u = b * G + g
                    if not fixed or u + 1 < UNITS:
                        keep_v_tail(u + 1, (g + 1) % G)
                    if not fixed or u < UNITS:
                        mix_v(u, g)
                    if not fixed or b < NB:
                        row_max(u, g)
                    if not fixed or 1 <= u <= UNITS:
                        normalise(u - 1, (g - 1) % G)
                    if g == 3 and (not fixed or b >= 1):
                        residual(b - 1, bass.ds(b - 1, 1))
                    if not fixed or b < NB - 1:
                        rope_products(u + G, g, bass.ts(b + 1, P))
                    if fixed and b == 0 and g < TG - 1:
                        normalise_x(g + 1)
                    if fixed and b == NB - 1 and g >= 1:
                        dve.wait_ge(r1_done, GB * g)
                        norm_request(r1, g - 1)
                    if fixed and b == NB and 1 <= g:
                        standardise(XA, r1, g - 1, x1_done)

            nc.vector.memset(v_own[:], 0.0).then_inc(zero_done, 1)
            grp = lambda q: slice(GB * q, GB * q + GB)
            bank4 = lambda b: B[b].rearrange("p (n c) -> p n c", n=GB)
            spread = lambda v: v.unsqueeze(1).broadcast_to([P, GB, C])

            dve.wait_ge(ld_x[0], 16)
            for n in range(GB):
                last = nc.vector.tensor_tensor_reduce(out=xn[:, n, :], in0=x_sb[:, n, :], in1=x_sb[:, n, :],
                                                      scale=1.0, scalar=0.0, op0=ALU.mult, op1=ALU.add,
                                                      accum_out=stat[:, n:n + 1])
            last.then_inc(squares_done, 1)
            dve.wait_ge(ld_ident, 16)
            nc.vector.tensor_copy(ident_bf[:], ident[:]).then_inc(cast_done, 1)
            normalise_x(0)
            dve.wait_ge(ld_rope[0], 32)
            for g in range(G):
                rope_products(g, g, slice(0, P))
            dve.wait_ge(ld_rope[1], 32)
            dve.wait_ge(zero_done, 1)
            keep_v_tail(0, 0)
            steps(0)
            steps(1)
            dve.wait_ge(ld_rope[2], 32)
            with dve.Fori(2, NB - 1) as b:
                steps(b)
            steps(NB - 1)
            steps(NB)
            dve.wait_ge(r1_done, NB)
            norm_request(r1, TG - 1)
            standardise(XA, r1, TG - 1, x1_done)
            for q in range(TG):
                dve.wait_ge(y2_ps, q + 1)
                dve.wait_ge(x1b_done, q + 1)
                nc.vector.tensor_tensor(XC[:, grp(q)], bank4(6 + q % 2), XB[:, grp(q)], ALU.add).then_inc(r2_done, 1)
                dve.wait_ge(r2_done, q + 1)
                norm_request(XC, q)
                if q >= 1:
                    standardise(XA, XC, q - 1, x2_done)
            standardise(XA, XC, TG - 1, x2_done)

            def normalised_keys(q):
                dve.wait_ge(rsq_out, roots[0] - TG + q + 1)
                nc.vector.tensor_tensor(kv[:, grp(q), 0:C], kv[:, grp(q), 0:C],
                                        rstd[:, grp(q)].unsqueeze(2).broadcast_to([P, GB, C]), ALU.mult).then_inc(kh_done, 1)

            roots[0] += TG
            for q in range(TG):
                for n in range(GB * q, GB * q + GB):
                    dve.wait_ge(kv_ps, n + 1)
                    nc.vector.tensor_tensor(kv[:, n, 0:KVW], B[2 + n % 4][:, 0:KVW], kv_b[:], ALU.add).then_inc(kv_done, 1)
                if q >= 2:
                    normalised_keys(q - 2)
            normalised_keys(TG - 2)
            normalised_keys(TG - 1)
            nc.vector.memset(x16[:], 0.0).then_inc(x16_set, 1)
            dve.wait_ge(x16_set, 1)
            nc.vector.memset(x16[:].rearrange("p a b -> p (a b)")[:, 0:SUB * SUB:SUB + 1], 1.0).then_inc(x16_set, 1)
            dve.wait_ge(gram_done, TG)
            nc.vector.tensor_tensor(BT[:, 0], gram[:], lmask[:, 0:1, :].broadcast_to([P, NB, P]), ALU.mult).then_inc(bt_done, 1)
            for q in range(TG):
                nc.vector.tensor_tensor(dk[:, grp(q)], kv[:, grp(q), 0:C],
                                        kv[:, grp(q), 2 * C:2 * C + 1].broadcast_to([P, GB, C]), ALU.mult).then_inc(dk_done, 1)
            dve.wait_ge(l16_done, 16 * NSUB)
            dve.wait_ge(x16_set, 2)
            for i in range(1, SUB):
                chained(nc.vector.tensor_tensor(prod[:, 0:i, 0:i], l16[:, i:i + 1, 0:i].broadcast_to([P, i, i]),
                                                x16[:, 0:i, 0:i], ALU.mult))
                last = nc.vector.tensor_reduce(x16[:, 0:i, i], prod[:, 0:i, 0:i], AX_X, ALU.add, negate=True)
                if i < SUB - 1:
                    chained(last)
            last.then_inc(x16_done, 1)
            for l in range(NLEV):
                for q in range(TG):
                    t = l * TG + q
                    dve.wait_ge(xbxt_ps, t + 1)
                    if l < NLEV - 1:
                        nc.vector.tensor_tensor(inv[:, grp(q)], inv[:, grp(q)], bank4(4 + q % 2), ALU.subtract).then_inc(inv_done2, 1)
                    nc.vector.tensor_tensor(invT[:, grp(q)], invT[:, grp(q)], bank4(6 + q % 2), ALU.subtract).then_inc(invT_done, 1)
            for n in range(NB - 1):
                dve.wait_ge(st_ps, n + 1)
                nc.vector.tensor_copy(state[:, n + 1, :], B[6][:, 0:C]).then_inc(st_done, 1)
            dve.wait_ge(g_ps, 1)
            nc.vector.tensor_copy(g_sb[:], B[7][:, 0:C]).then_inc(g_done, 1)
            dve.wait_ge(db_ps, 1)
            nc.vector.tensor_tensor(delta_bias[:], B[4][:, 0:C], row["b_do"], ALU.add).then_inc(db_done, 1)
            for q in range(TG):
                dve.wait_ge(x3_ps, q + 1)
                dve.wait_ge(xbias_done, q + 1)
                nc.vector.tensor_tensor(XD[:, grp(q)], bank4(6 + q % 2), XC[:, grp(q)], ALU.add).then_inc(x3_done, 1)
                dve.wait_ge(x3_done, q + 1)
                norm_request(XD, q)
                if q >= 1:
                    standardise(XB, XD, q - 1, tr_mn)
            standardise(XB, XD, TG - 1, tr_mn)

            def routing_scores(q):
                dve.wait_ge(x6_done, q + 1)
                for n in range(GB * q, GB * q + GB):
                    last = nc.vector.tensor_tensor_reduce(out=XC[:, n, :], in0=XA[:, n, :], in1=row["token"], scale=1.0,
                                                          scalar=0.0, op0=ALU.mult, op1=ALU.add, accum_out=s_tok[:, n:n + 1])
                last.then_inc(s_done, 1)

            for q in range(TG):
                dve.wait_ge(m2_ps, q + 1)
                dve.wait_ge(x32_done, q + 1)
                nc.vector.tensor_tensor(XE[:, grp(q)], bank4(6 + q % 2), XC[:, grp(q)], ALU.add).then_inc(r3_done, 1)
                dve.wait_ge(r3_done, q + 1)
                norm_request(XE, q)
                if q >= 1:
                    standardise(XA, XE, q - 1, x6_done)
                    routing_scores(q - 1)
            standardise(XA, XE, TG - 1, x6_done)
            routing_scores(TG - 1)
            dve.wait_ge(s_done, TG)
            nc.vector.tensor_reduce(ends[:, 0:1], s_tok[:], AX_X, ALU.max).then_inc(red_done, 1)
            nc.vector.tensor_reduce(ends[:, 1:2], s_tok[:], AX_X, ALU.max, apply_absolute_value=True).then_inc(red_done, 1)

            def take_ffn(p):
                side, q = PIECES[p // PIECES_EACH]
                if side == "out" and p % PIECES_EACH == 1:
                    dve.wait_ge(l2_ps, q + 1)
                    dve.wait_ge(x6b_done, q + 1)
                    nc.vector.tensor_tensor(XC[:, grp(q)], bank4(0), XC[:, grp(q)], ALU.add).then_inc(base_done, 1)
                if side == "out" and p % PIECES_EACH == PIECES_EACH - 1:
                    dve.wait_ge(h2_ps, q + 1)
                    nc.vector.tensor_tensor(XE[:, grp(q)], bank4(2), spread(row["b_h2"]), ALU.add).then_inc(heavy_done, 1)

            dve.wait_ge(redT_ps, 1)
            chained(nc.vector.tensor_reduce(ends_m[:], B[6][0:2, 0:P], AX_X, ALU.max))
            nc.vector.tensor_scalar(ends_d[:], ident[0:2, 0:2], ends_m[:], None, ALU.mult).then_inc(redm_done, 1)
            nc.vector.memset(halves[:, 0:1], 2.0).then_inc(redm_done, 1)
            for i in range(1, DESCENT):
                last = nc.vector.memset(halves[:, i:i + 1], 2.0 ** (1 - i))
            chained(last)
            dve.wait_ge(ends_ps, 1)
            nc.vector.tensor_scalar(base[:], B[6][:, 0:1], float(np.log(T / EFFECTIVE)), None, ALU.min).then_inc(dve_misc, 1)
            chained(nc.vector.tensor_copy(step_w[:], B[6][:, 1:2]))
            chained(nc.vector.tensor_scalar(step_w[:].bitcast(I32), step_w[:].bitcast(I32), 0x7F800000, None, ALU.bitwise_and))
            chained(nc.vector.tensor_scalar(widths[:], halves[:], step_w[:], None, ALU.mult))
            chained(nc.vector.tensor_scalar(low[:], step_w[:], -2.0, None, ALU.mult))
            nc.vector.memset(one[:], 1.0).then_inc(dve_misc, 1)
            dve.wait_ge(dve_misc, 2)
            marks = [0]

            def exponentials_from_base():
                marks[0] += 1
                nc.vector.tensor_scalar(args[:], s_tok[:], base[:], CAP, ALU.subtract, ALU.min).then_inc(arg_done, 1)
                dve.wait_ge(f_done, marks[0])

            exponentials_from_base()
            for i in range(DESCENT - 1):
                a_now = one[:] if i == 0 or i in REBASE else B[6][:, 0:1]
                if i > 0:
                    dve.wait_ge(desc_ps, i)
                if i in REBASE:
                    nc.vector.tensor_copy(log_in[:], B[6][:, 0:1]).then_inc(ln_in, 1)
                    dve.wait_ge(ln_done, REBASE.index(i) + 1)
                    chained(nc.vector.tensor_tensor(base[:], base[:], log_a[:], ALU.add))
                    exponentials_from_base()
                nc.vector.tensor_scalar(djunk[:], f_tok[:], a_now, None, ALU.min, ALU.add,
                                        accum_out=dpart[:, 0:1]).then_inc(desc_in, 1)
                if i > 0:
                    dve.wait_ge(cnt_ps, i)
                    chained(nc.vector.tensor_scalar(step_w[:], B[7][:, 0:1], HEAVY - 0.5, widths[:, i - 1:i], ALU.is_ge, ALU.mult))
                    chained(nc.vector.tensor_tensor(low[:], low[:], step_w[:], ALU.add))
                nc.vector.scalar_tensor_tensor(cjunk[:], s_tok[:], low[:], widths[:, i:i + 1].broadcast_to([P, NB]),
                                               ALU.subtract, ALU.is_ge, accum_out=cpart[:, 0:1]).then_inc(cnt_in, 1)
                for p in pieces_in(i - 1):
                    take_ffn(p)
            last_i = DESCENT - 1
            for p in pieces_in(last_i - 1):
                take_ffn(p)
            dve.wait_ge(desc_ps, last_i)
            nc.vector.tensor_copy(log_in[:], B[6][:, 0:1]).then_inc(ln_in, 1)
            dve.wait_ge(cnt_ps, last_i)
            chained(nc.vector.tensor_scalar(step_w[:], B[7][:, 0:1], HEAVY - 0.5, widths[:, last_i - 1:last_i], ALU.is_ge, ALU.mult))
            chained(nc.vector.tensor_tensor(low[:], low[:], step_w[:], ALU.add))
            dve.wait_ge(ln_done, len(REBASE) + 1)
            chained(nc.vector.tensor_tensor(theta[:], base[:], log_a[:], ALU.add))
            nc.vector.tensor_scalar(key[:], s_tok[:], theta[:], None, ALU.min).then_inc(key_done, 1)
            chained(nc.vector.tensor_tensor(low[:], low[:], theta[:], ALU.min))
            dve.wait_ge(key_done, 1)
            nc.vector.tensor_scalar(score[:], key[:], theta[:], None, ALU.subtract).then_inc(strict_done, 1)
            nc.vector.tensor_scalar(strict[:], key[:], low[:], None, ALU.is_gt, ALU.add,
                                    accum_out=dpart[:, 1:2]).then_inc(strict_done, 1)
            nc.vector.tensor_scalar(tie[:], key[:], low[:], None, ALU.is_equal).then_inc(tie_done, 1)
            dve.wait_ge(strict_ps, 1)
            nc.vector.tensor_scalar(need[:], B[6][:, 0:1], -1.0, float(HEAVY), ALU.mult, ALU.add).then_inc(dve_misc, 1)
            dve.wait_ge(tot_ps, 1)
            nc.vector.tensor_copy(tot_t[:], B[7][0:NB, 0:P]).then_inc(tot_done, 1)
            dve.wait_ge(dve_misc, 3)
            dve.wait_ge(pre_ps, 1)
            chained(nc.vector.tensor_scalar(fits[:], B[5][:, 0:NB], need[:], None, ALU.is_lt))
            chained(nc.vector.tensor_tensor(fits[:], fits[:], tie[:], ALU.mult))
            chained(nc.vector.tensor_tensor(sel[:], fits[:], strict[:], ALU.add))
            dve.wait_ge(score_done, 1)
            chained(nc.vector.tensor_scalar(fits[:], escore[:], -1.0, 1.0, ALU.mult, ALU.add))
            chained(nc.vector.tensor_tensor(fits[:], fits[:], escore[:], ALU.add))
            chained(nc.vector.tensor_tensor(sel[:], sel[:], fits[:], ALU.mult))
            for q in range(TG):
                for n in range(GB * q, GB * q + GB):
                    last = nc.vector.scalar_tensor_tensor(XE[:, n, :], XE[:, n, :], sel[:, n:n + 1], XC[:, n, :],
                                                          ALU.mult, ALU.add)
                chained(last)
                norm_request(XE, q)
                if q >= 1:
                    standardise(XA, XE, q - 1, out_ready)
            standardise(XA, XE, TG - 1, out_ready)

        @block.scalar
        def _(act):
            def exponentials(u, g):
                act.wait_ge(max_done, u + 1)
                wait(act, probsT_ps, u - 1)
                for e in range(2):
                    for pr in range(PAIRS):
                        last = nc.scalar.activation(probs[:, g % 2, e, pr, :], S[:, e, pr, :], ACT.Exp,
                                                    bias=negmax[:, g % 2, e, pr:pr + 1],
                                                    accum_out=total[:, g % 2, e, pr:pr + 1])
                last.then_inc(exp_done, 1)

            def keep_probsT(u, g):
                act.wait_ge(probsT_ps, u + 1)
                wait(act, o_ps, u - 1)
                nc.scalar.copy(probsT[:, g % 2], PT[:].rearrange("p (h q) -> p h q", h=GH)).then_inc(probsT_done, 1)

            def keep_v(n, g):
                act.wait_ge(v_ps, n + 1)
                act.wait_ge(v_tail_done, n + 1)
                nc.scalar.copy(v_own[:, g], V_ps.rearrange("p (h d) -> p h d", h=GH)).then_inc(v_own_done, 1)

            def keep_oT(u, g, b):
                act.wait_ge(o_ps, u + 1)
                wait(act, y_ps, b)
                nc.scalar.copy(oT[:, PAIRS * g:PAIRS * g + PAIRS, :],
                               O_ps[:, 0:PAIRS * P].rearrange("p (n q) -> p n q", n=PAIRS)).then_inc(oT_done, 1)

            def stage_x(b, tok):
                wait(act, v_ps, b * G)
                nc.scalar.copy(xv[:], xnT[:, tok]).then_inc(xv_done, 1)

            def keep_xnT(q):
                act.wait_ge(xt_done, q + 1)
                nc.scalar.copy(xnT[:, 512 * q:512 * q + 512], XT_ps[min(q, 1)][:]).then_inc(xnT_done, 1)

            def steps(b):
                fixed = static(b)
                for g in range(G):
                    u = b * G + g
                    if not fixed or 3 <= u <= UNITS + 2:
                        keep_oT(u - 3, (g - 3) % G, b - (1 if g < 3 else 0))
                    if g == 2 and (not fixed or b < NB - 1):
                        stage_x(b + 1, bass.ts(b + 1, P))
                    if not fixed or u + 1 < UNITS:
                        keep_v(u + 1, (g + 1) % G)
                    if not fixed or 2 <= u <= UNITS + 1:
                        keep_probsT(u - 2, (g - 2) % G)
                    if not fixed or b < NB:
                        exponentials(u, g)
                    if fixed and b == 0 and 1 <= g < TG:
                        keep_xnT(g)

            for dst, src, sem_ in ((wq, w_q, ld_wq), (wk, w_k, ld_wk), (wv, w_v, ld_wv)):
                act.dma_start(dst[:], src).then_inc(sem_, 16)
            act.wait_ge(ld_wq, 16)
            nc.scalar.mul(wq[:], wq[:], SCALE).then_inc(scaled_done, 1)
            keep_xnT(0)
            act.wait_ge(xnT_done, 1)
            stage_x(0, slice(0, P))
            for q in range(1, TG):
                act.wait_ge(ld_x[q], 16)
                for n in range(GB * q, GB * q + GB):
                    last = nc.scalar.activation(xn[:, n, :], x_sb[:, n, :], ACT.Square, accum_out=stat[:, n:n + 1])
            last.then_inc(squares_done, 1)
            keep_v(0, 0)
            steps(0)
            steps(1)
            with act.Fori(2, NB - 1) as b:
                steps(b)
            steps(NB - 1)
            steps(NB)
            grp = lambda q: slice(q * 512, (q + 1) * 512)
            bank4 = lambda b: B[b].rearrange("p (n c) -> p n c", n=GB)

            def from_transposes(stage, q, dst, scale=None, bias=None):
                t = stage * TG + q
                act.wait_ge(tr_ps, t + 1)
                if scale is None:
                    nc.scalar.copy(dst[:, grp(q)], B[t % 2]).then_inc(tr_done, 1)
                else:
                    nc.scalar.activation(dst[:, grp(q)], B[t % 2], ACT.Identity, bias=bias, scale=scale).then_inc(tr_done, 1)

            act.wait_ge(ld_late, 80)
            nc.scalar.mul(W["w_l1"], W["w_l1"], W["gam_l"]).then_inc(gam_done, 1)
            nc.scalar.mul(W["w_h1"], W["w_h1"], W["gam_h"]).then_inc(gam_done, 1)
            for q in range(TG + 1):
                if q < TG:
                    from_transposes(0, q, hT)
                if q >= 1:
                    for j in range(NF):
                        act.wait_ge(hid_ps, NF * (q - 1) + j + 1)
                        nc.scalar.activation(hid[:, j, grp(q - 1)], B[2 + j], ACT.Relu,
                                             bias=W["b_f1"][:, j:j + 1]).then_inc(hid_done, 1)
            def scaled(q, stage, arrived):
                act.wait_ge(arrived, q + 1)
                act.wait_ge(rsq2_out, stage * TG + q + 1)
                for n in range(GB * q, GB * q + GB):
                    last = nc.scalar.mul(XB[:, n, :], XA[:, n, :], rstd2[:, n:n + 1])
                last.then_inc(tr_src, 1)

            def key_squares(q):
                for n in range(GB * q, GB * q + GB):
                    act.wait_ge(kv_done, n + 1)
                    last = nc.scalar.activation(XD[:, n, :], kv[:, n, 0:C], ACT.Square, accum_out=var_eps[:, n:n + 1])
                last.then_inc(rsq_in, 1)

            for s in range(TG + 2):
                if s < TG:
                    scaled(s, 0, x2_done)
                if 1 <= s <= TG:
                    from_transposes(1, s - 1, hT, W["dn_g"], W["dn_b"])
                if s >= 2:
                    key_squares(s - 2)
            khT_flat = khT[:].rearrange("p n c -> p (n c)")
            for s in range(TG + 1):
                if s < TG:
                    from_transposes(2, s, khT_flat)
                if s >= 1:
                    act.wait_ge(gram_ps, s)
                    nc.scalar.copy(gram[:, GB * s - GB:GB * s], bank4(6 + (s - 1) % 2)).then_inc(gram_done, 1)
            for q in range(TG):
                act.wait_ge(ix_ps, q + 1)
                nc.scalar.copy(inv[:, GB * q:GB * q + GB], bank4(q % 2)).then_inc(ix_done, 1)
            for l in range(NLEV):
                for q in range(TG):
                    t = l * TG + q
                    act.wait_ge(bx_ps, t + 1)
                    if l > 0:
                        act.wait_ge(invT_done, (l - 1) * TG + q + 1)
                    nc.scalar.copy(bx[:, GB * q:GB * q + GB], bank4(2 + q % 2)).then_inc(bx_done, 1)
            for m in range(NB // 2):
                act.wait_ge(wv_ps, m + 1)
                nc.scalar.copy(wv2[:, 2 * m:2 * m + 2], B[m % 2].rearrange("p (n c) -> p n c", n=2)).then_inc(wv_done, 1)
            for m in range(NB // 2):
                act.wait_ge(aq_ps, m + 1)
                nc.scalar.mul(naq[:, 2 * m:2 * m + 2], B[2 + m % 2].rearrange("p (n c) -> p n c", n=2), -1.0).then_inc(aq_done, 1)
            act.wait_ge(z_ps, 1)
            nc.scalar.copy(zT[:], B[2][:, 0:C + 1]).then_inc(zb_done, 1)
            act.wait_ge(zb_done, 1)
            nc.scalar.copy(z_bias[:], zT[:, C:C + 1].broadcast_to([P, C])).then_inc(zb_done, 1)
            act.wait_ge(e_ps, 1)
            nc.scalar.copy(e_sb[:], B[3][:, 0:C]).then_inc(e_done, 1)
            for s in range(TG + 1):
                if s < TG:
                    from_transposes(3, s, hT, W["mn_g"], W["mn_b"])
                if s >= 1:
                    act.wait_ge(m1_ps, s)
                    nc.scalar.activation(hid[:, 0, grp(s - 1)], B[2 + (s - 1) % 2], ACT.Relu,
                                         bias=W["m_b1"]).then_inc(m1_done, 1)

            def activate(p):
                side, q = PIECES[p // PIECES_EACH]
                part = p % PIECES_EACH
                if side == "in" and part == 1:
                    act.wait_ge(l1_ps, q + 1)
                    nc.scalar.activation(light[0:LF, grp(q)], B[5][0:LF, :], ACT.Gelu, bias=W["b_l1"][0:LF]).then_inc(l1_done, 1)
                elif side == "in" and part % 2 == 1:
                    j = part // 2 - 1
                    n = NHF * q + j
                    act.wait_ge(h1_ps, n + 1)
                    nc.scalar.activation(hid[:, j, grp(q)], B[3 + n % 2], ACT.Gelu,
                                         bias=W["b_h1"][:, j:j + 1]).then_inc(h1_done, 1)

            for q in range(TG):
                scaled(q, 1, x6_done)
                from_transposes(4, q, hT)
                if q == 1 or q == 3:
                    for p in range(PIECES_EACH * (q // 2), PIECES_EACH * (q // 2 + 1)):
                        activate(p)

            def exponentials_of_scores(m):
                act.wait_ge(arg_done, m)
                nc.scalar.activation(f_tok[:], args[:], ACT.Exp).then_inc(f_done, 1)

            exponentials_of_scores(1)
            for i in range(DESCENT):
                if i in REBASE or i == DESCENT - 1:
                    m = sum(r <= i for r in REBASE) + (i == DESCENT - 1)
                    act.wait_ge(ln_in, m)
                    nc.scalar.activation(log_a[:], log_in[:], ACT.Ln).then_inc(ln_done, 1)
                if i in REBASE:
                    exponentials_of_scores(m + 1)
                for p in pieces_in(i - 1) if i > 0 else ():
                    activate(p)
            act.wait_ge(strict_done, 1)
            nc.scalar.activation(escore[:], score[:], ACT.Exp).then_inc(score_done, 1)

        @block.gpsimd
        def _(pool):
            def rope_sum(n, g, b):
                nc.gpsimd.tensor_copy(k_tail[:, g], qk[:, g, PAIRS:, KEEP:]).then_inc(tail_done, 1)
                pool.wait_ge(tail_done, n + 1)
                pool.wait_ge(mul_done, n + 1)
                pool.wait_ge(swapped[g], 64 * (b + 1))
                wait(pool, scores_done, n - G + 1)
                nc.gpsimd.tensor_tensor(qk[:, g], t_cos[:, g], t_swap[:, g], ALU.add).then_inc(sum_done, 1)
                pool.wait_ge(sum_done, n + 1)
                nc.gpsimd.tensor_tensor(k_diff[:, g], k_tail[:, g], qk[:, g, PAIRS:, KEEP:],
                                        ALU.subtract).then_inc(rope_done, 1)

            nc.gpsimd.memset(expo[:], -0.5).then_inc(pool_step, 1)
            nc.gpsimd.memset(qk[:], 0.0).then_inc(pool_step, 1)
            pool.wait_ge(pool_step, 2)

            def inverse_rms(k, n0, n1):
                pool.wait_ge(squares_done, k)
                nc.gpsimd.tensor_scalar(mean2[:, n0:n1], stat[:, n0:n1], 1.0 / C, 1e-6, ALU.mult,
                                        ALU.add).then_inc(sumsq_done, 1)
                pool.wait_ge(sumsq_done, k)
                nc.gpsimd.tensor_tensor(rms[:, n0:n1], mean2[:, n0:n1], expo[:, n0:n1], ALU.pow).then_inc(rms_done, 1)

            inverse_rms(1, 0, GB)
            rope_sum(0, 0, 0)
            inverse_rms(2, GB, NB)
            for g in range(1, G):
                rope_sum(g, g, 0)

            def steps(b):
                for g in range(G):
                    rope_sum(b * G + g + G, g, b + 1)

            steps(0)
            steps(1)
            with pool.Fori(2, NB - 1) as b:
                steps(b)
            grp = lambda q: slice(GB * q, GB * q + GB)
            spread = lambda v: v.unsqueeze(1).broadcast_to([P, GB, C])
            roots = [0]

            def inverse_root(q):
                roots[0] += 1
                pool.wait_ge(rsq_in, roots[0])
                nc.gpsimd.tensor_tensor(rstd[:, grp(q)], var_eps[:, grp(q)], expo[:, grp(q)], ALU.pow).then_inc(rsq_out, 1)

            def second_root(q, op, bound):
                pool.wait_ge(rsq_out, roots[0])
                v = spread_var[:, grp(q)]
                pooled(nc.gpsimd.tensor_tensor(v, mv[:, grp(q), 1], rstd[:, grp(q)], ALU.mult))
                pooled(nc.gpsimd.tensor_tensor(v, v, rstd[:, grp(q)], ALU.mult))
                pooled(nc.gpsimd.tensor_scalar(v, v, bound, None, op))
                nc.gpsimd.tensor_tensor(rstd2[:, grp(q)], v, expo[:, grp(q)], ALU.pow).then_inc(rsq2_out, 1)

            small = [2]

            def pooled(ins):
                small[0] += 1
                ins.then_inc(pool_step, 1)
                pool.wait_ge(pool_step, small[0])

            for q in range(TG):
                inverse_root(q)
            pool.wait_ge(ld_late, 80)
            for q in range(TG):
                pool.wait_ge(x1_done, q + 1)
                nc.gpsimd.tensor_tensor(XB[:, grp(q)], XA[:, grp(q)], spread(row["b_f2"]), ALU.add).then_inc(x1b_done, 1)
            for q in range(TG):
                inverse_root(q)
                second_root(q, ALU.add, EPS)
            for q in range(TG):
                inverse_root(q)
            nc.gpsimd.memset(invT[:], 0.0).then_inc(zeroed, 1)
            nc.gpsimd.memset(ones[:], 1.0).then_inc(kset, 1)
            nc.gpsimd.memset(ones_bf[:], 1.0).then_inc(kset, 1)
            nc.gpsimd.memset(kth[:], 1.0 / EFFECTIVE).then_inc(kset, 1)
            pool.wait_ge(gram_done, TG)
            for l in range(1, NLEV):
                pool.wait_ge(bt_done, l)
                nc.gpsimd.tensor_tensor(BT[:, l], gram[:], lmask[:, l:l + 1, :].broadcast_to([P, NB, P]),
                                        ALU.mult).then_inc(bt_done, 1)
            pool.wait_ge(db_done, 1)
            for q in range(TG):
                nc.gpsimd.tensor_tensor(XC[:, grp(q)], XA[:, grp(q)], spread(delta_bias[:]), ALU.add).then_inc(xbias_done, 1)
            for q in range(TG):
                inverse_root(q)
            for q in range(TG):
                pool.wait_ge(x3_done, q + 1)
                nc.gpsimd.tensor_tensor(XC[:, grp(q)], XD[:, grp(q)], XA[:, grp(q)], ALU.add).then_inc(pool_sum, 1)
                pool.wait_ge(pool_sum, q + 1)
                nc.gpsimd.tensor_tensor(XC[:, grp(q)], XC[:, grp(q)], spread(row["b_m2"]), ALU.add).then_inc(x32_done, 1)
            for q in range(TG):
                inverse_root(q)
                second_root(q, ALU.max, 1e-24 / C)
            pool.wait_ge(s_done, TG)
            for q in range(TG):
                nc.gpsimd.tensor_tensor(XC[:, grp(q)], XA[:, grp(q)], spread(row["b_l2"]), ALU.add).then_inc(x6b_done, 1)
            for q in range(TG):
                inverse_root(q)


def lay_out(inputs):
    f = {k: np.asarray(v) for k, v in inputs.items()}
    channels = f["L0_attn_x"].shape[2]
    inner = f["L0_attn_w_out"].shape[1]
    w_q, w_k, w_v = (np.ascontiguousarray(f["L0_attn_w_qkv"][i * inner:(i + 1) * inner].T) for i in range(3))

    def chunks(w):
        return w.reshape(-1, P, w.shape[1]).transpose(1, 0, 2).reshape(P, -1)

    def column(v):
        if v.shape[0] < P:
            v = np.concatenate([v, np.zeros(P - v.shape[0], v.dtype)])
        return v.reshape(-1, P).T

    def padded(w):
        return np.concatenate([w, np.zeros((P - w.shape[0], w.shape[1]), w.dtype)])

    gates, gates_b = f["L1_attn_gates_w"], f["L1_attn_gates_b"]
    parts = [
        ("w_f1", f["L0_ffn_W1"]), ("w_f2", chunks(f["L0_ffn_W2"])), ("b_f1", column(f["L0_ffn_b1"])),
        ("w_kv", np.concatenate([gates[:, channels:], f["L1_attn_lr_w"]], 1)),
        ("w_qT", np.concatenate([gates[:, :channels].T, gates_b[:channels, None]], 1)),
        ("w_do", f["L1_attn_out_w"]), ("w_m1", f["L1_attn_w1"]), ("w_m2", f["L1_attn_w2"]),
        ("dn_g", column(f["L1_attn_dn_g"])), ("dn_b", column(f["L1_attn_dn_b"])),
        ("mn_g", column(f["L1_attn_mn_g"])), ("mn_b", column(f["L1_attn_mn_b"])), ("m_b1", column(f["L1_attn_b1"])),
        ("w_l1", f["L1_ffn_w1_l"].T), ("b_l1", column(f["L1_ffn_b1_l"])), ("w_l2", padded(f["L1_ffn_w2_l"].T)),
        ("w_h1", f["L1_ffn_w1_h"].T), ("b_h1", column(f["L1_ffn_b1_h"])), ("w_h2", chunks(f["L1_ffn_w2_h"].T)),
        ("gam_l", column(f["L1_ffn_gamma_l"])), ("gam_h", column(f["L1_ffn_gamma_h"])),
    ]
    late, at = {}, 0
    for name, a in parts:
        late[name] = (at, at + a.shape[1])
        at += a.shape[1]
    late["end"] = (at, at)
    arrays = {
        "x": f["L0_attn_x"].reshape(-1, channels),
        "w_q": w_q, "w_k": w_k, "w_v": w_v,
        "w_o": np.ascontiguousarray(f["L0_attn_w_out"].T),
        "late_weights": np.ascontiguousarray(np.concatenate([a for _, a in parts], 1)),
        "row_vectors": np.concatenate([f["L0_ffn_b2"], f["L1_attn_out_b"], f["L1_attn_b2"], f["L1_ffn_b2_l"],
                                       f["L1_ffn_b2_h"], f["L1_ffn_routing_token"]]),
        "kv_bias": np.concatenate([gates_b[channels:], f["L1_attn_lr_b"]]),
    }
    return arrays, late


def kernel(**inputs):
    import concourse.bacc as bacc
    from concourse.bass_utils import run_bass_kernel_spmd

    arrays, late = lay_out(inputs)
    nc = bacc.Bacc("TRN2", target_bir_lowering=False, num_devices=1)
    args = {n: nc.dram_tensor(n, a.shape, F32, kind="ExternalInput").ap() for n, a in arrays.items()}
    tokens, channels = arrays["x"].shape
    out = nc.dram_tensor("out", (tokens, channels), F32, kind="ExternalOutput").ap()
    build(nc, out=out, late=late, **args)
    r = run_bass_kernel_spmd(nc, [arrays], core_ids=[0])
    return r.results[0]["out"].reshape(np.asarray(inputs["L0_attn_x"]).shape)
```

```python
from contextlib import ExitStack

import numpy as np

import concourse.bass as bass
from concourse import mybir

F32 = mybir.dt.float32
BF16 = mybir.dt.bfloat16
I32 = mybir.dt.int32
ALU = mybir.AluOpType
ACT = mybir.ActivationFunctionType
AX_X = mybir.AxisListType.X

P = 128


def static(v):
    return isinstance(v, int)


def wait(eng, sem, value):
    if static(value) and value <= 0:
        return
    eng.wait_ge(sem, value)


def rope_tables(tokens, dim):
    half = dim // 2
    inv = (1.0 / 10000.0 ** (np.arange(0, dim, 2, dtype=np.float32) / np.float32(dim))).astype(np.float32)
    angle = np.outer(np.arange(tokens, dtype=np.float32), inv).astype(np.float32)
    cos, sin = np.cos(angle).T, np.sin(angle).T
    return (np.concatenate([cos] * 4).astype(np.float32),
            np.concatenate([sin, -sin, sin, -sin]).astype(np.float32))


def band_masks(window, blocked):
    q, k = np.arange(P)[:, None], np.arange(P)[None, :]
    own = (k <= q) & (q - k <= window)
    before = (q < window) & (k >= P - window) & (q - (k - P) <= window)
    out = np.stack([np.where(own, 0.0, blocked), np.where(own | before, 0.0, blocked)])
    return out.transpose(1, 0, 2).copy()


def level_masks(size, levels):
    i, j = np.arange(P)[:, None], np.arange(P)[None, :]
    out = []
    for _ in range(levels):
        out.append((i // (2 * size) == j // (2 * size)) & (i // size < j // size))
        size *= 2
    return np.stack(out).astype(np.float32).transpose(1, 0, 2).copy()


def build(nc, x, w_q, w_k, w_v, w_o, late_weights, row_vectors, kv_bias, out, late):
    T, C = x.shape
    INNER = w_v.shape[1]
    D = 64
    WINDOW = 32
    H = INNER // D
    NB = T // P
    G = 4
    GH = H // G
    PAIRS = GH // 2
    KEEP = P - WINDOW
    SCALE = float(D) ** -0.5
    BLOCKED = -1e9
    NCH = INNER // P
    UNITS = NB * G
    TG = T // 512
    GB = NB // TG
    NF = (late["b_f1"][1] - late["b_f1"][0])
    NHF = (late["b_h1"][1] - late["b_h1"][0])
    LF = late["w_l1"][1] - late["w_l1"][0]
    KVW = 2 * C + 1
    WARMING = 18
    X3_BANKS = (6, 7, 5, 4)
    SUB = 16
    NSUB = P // SUB
    NLEV = 3
    HEAVY = 128
    EFFECTIVE = HEAVY * 9.0 / 8.0
    DESCENT = 50
    DIGITS = 3
    ROUNDS = DESCENT // 2
    REBASE = (8, 16, 24, 32, 40)
    LEAD = 5
    CAP = 80.0
    PIECES = [("in", 0), ("in", 1), ("out", 0), ("in", 2), ("out", 1), ("in", 3), ("out", 2), ("out", 3)]
    PIECES_EACH = 10
    AHEAD = 2 * PIECES_EACH
    BEFORE_ENDS = 4
    BEFORE_EXP = 8
    AT_START = 7
    EPS = 1e-5
    assert SUB << NLEV == P and GB * TG == NB and NSUB * NB == P

    def pieces_in(i):
        def start(i):
            return AHEAD + AT_START + i
        if i < 0:
            return range(AHEAD, AHEAD + AT_START)
        total = PIECES_EACH * len(PIECES)
        return range(min(start(i), total), total if i == DESCENT - 2 else min(start(i + 1), total))

    cos_np, sin_np = rope_tables(T, D)
    cos_dram = nc.inline_tensor(cos_np, name="rope_cos").ap()
    sin_dram = nc.inline_tensor(sin_np, name="rope_sin").ap()
    mask_np = band_masks(WINDOW, BLOCKED).astype(np.float32)
    mask_dram = nc.inline_tensor(mask_np, name="band_masks").ap()
    ident_dram = nc.inline_tensor(np.eye(P, dtype=np.float32), name="identity_f").ap()
    level_dram = nc.inline_tensor(level_masks(SUB, NLEV), name="level_masks").ap()
    before_dram = nc.inline_tensor(np.triu(np.ones((P, P), np.float32), 1), name="tokens_before").ap()

    digit_np = (4.0 ** -np.arange(ROUNDS)[:, None] * (1 + np.arange(DIGITS))).astype(np.float32)
    digit_dram = nc.inline_tensor(digit_np.reshape(-1), name="digit_widths").ap()

    with ExitStack() as ctx:
        scope = [ctx]

        def sb(name, shape, dt=F32):
            return scope[0].enter_context(nc.sbuf_tensor(name, shape, dt))

        def bank(name):
            return ctx.enter_context(nc.psum_tensor(name, [P, 512], F32))

        def sem(name):
            return ctx.enter_context(nc.semaphore(name))

        ident = sb("ident", [P, P])
        expo = sb("expo", [P, NB])
        r1 = sb("r1", [P, NB, C])
        mv = sb("mv", [P, NB, 2])
        late_sb = sb("late_sb", [P, late["end"][0]])
        W = {n: late_sb[:, a:b] for n, (a, b) in late.items() if n != "end"}
        rows = sb("rows", [P, 6, C])
        row = {n: rows[:, i, :] for i, n in enumerate(("b_f2", "b_do", "b_m2", "b_l2", "b_h2", "token"))}
        kv_b = sb("kv_b", [P, KVW])
        lmask = sb("lmask", [P, NLEV, P])
        before = sb("before", [P, P])
        digits = sb("digits", [P, ROUNDS, DIGITS])
        bns = sb("bns", [P, NB, 6])
        var_eps = sb("var_eps", [P, NB])
        rstd = sb("rstd", [P, NB])
        rstd2 = sb("rstd2", [P, NB])
        spread_var = sb("spread_var", [P, NB])
        first = ExitStack()
        scope[0] = first
        cos = sb("cos", [P, T])
        sin = sb("sin", [P, T])
        wq = sb("wq", [P, INNER])
        wk = sb("wk", [P, INNER])
        x_sb = sb("x_sb", [P, NB, C])
        masks = sb("masks", [P, 2, P])
        wv = sb("wv", [P, INNER])
        wo = sb("wo", [P, NCH, C])
        xn = sb("xn", [P, NB, C])
        xnT = sb("xnT", [P, T])
        xv = sb("xv", [P, P])
        stat = sb("stat", [P, NB])
        mean2 = sb("mean2", [P, NB])
        rms = sb("rms", [P, NB])
        t_cos = sb("t_cos", [P, G, 4, P])
        t_sin = sb("t_sin", [P, G, 4, P])
        t_swap = sb("t_swap", [P, G, 4, P])
        qk = sb("qk", [P, G, 4, P])
        k_tail = sb("k_tail", [P, G, PAIRS, WINDOW])
        zeros = sb("zeros", [P, PAIRS, WINDOW])
        negmax = sb("negmax", [P, 2, 2, PAIRS])
        total = sb("total", [P, 2, 2, PAIRS])
        inv_total = sb("inv_total", [P, 2, 2, PAIRS])
        probs = sb("probs", [P, 2, 2, PAIRS, P])
        probsT = sb("probsT", [P, 2, GH, P])
        v_own = sb("v_own", [P, G, GH, D])
        v_mix = sb("v_mix", [P, G, GH, D])
        oT = sb("oT", [P, NCH, P])
        first.close()

        scope[0] = ctx
        XA = sb("XA", [P, NB, C])
        XB = sb("XB", [P, NB, C])
        hT = sb("hT", [P, T])
        XC = sb("XC", [P, NB, C])
        XD = sb("XD", [P, NB, C])
        XE = sb("XE", [P, NB, C])
        kth = sb("kth", [P, P])
        ones = sb("ones", [P, P])
        ones_bf = sb("ones_bf", [P, P], BF16)
        second = ExitStack()
        scope[0] = second
        kv = sb("kv", [P, NB, KVW + 3])
        khT = sb("khT", [P, NB, C])
        gram = sb("gram", [P, NB, P])
        l16 = sb("l16", [P, 2 * SUB * SUB // 2 + SUB])
        x16 = sb("x16", [P, 2 * SUB * SUB // 2 + SUB])
        prod = sb("prod", [P, (SUB // 2) ** 3])
        lx = sb("lx", [P, SUB // 2, SUB // 2])
        BT = sb("BT", [P, NLEV, NB, P])
        invT = sb("invT", [P, NB, P])
        inv = sb("inv", [P, NB, P])
        bx = sb("bx", [P, NB, P])
        naq = sb("naq", [P, NB, 2 * C])
        state = sb("state", [P, NB, C])
        wv2 = sb("wv2", [P, NB, 2 * C])
        g_sb = sb("g_sb", [P, C])
        zT = sb("zT", [P, C + 1])
        z_bias = sb("z_bias", [P, C])
        e_sb = sb("e_sb", [P, C])
        delta_bias = sb("delta_bias", [P, C])
        dk = khT
        second.close()
        scope[0] = ctx
        hid = sb("hid", [P, max(NF, NHF), T])
        light = sb("light", [P, T])
        s_tok = sb("s_tok", [P, NB])
        f_tok = sb("f_tok", [P, 2, NB])
        args = sb("args", [P, NB])
        log_in = sb("log_in", [P, 1])
        one = sb("one", [P, 1])
        a_unit = sb("a_unit", [P, 1])
        a_rebased = sb("a_rebased", [P, 1])
        escore = sb("escore", [P, NB])
        djunk = sb("djunk", [P, NB])
        cjunk = sb("cjunk", [P, DIGITS + 1, NB])
        dpart = sb("dpart", [P, 2])
        cpart = sb("cpart", [P, DIGITS], BF16)
        widths = sb("widths", [P, ROUNDS, DIGITS])
        tried = sb("tried", [P, DIGITS])
        ends = sb("ends", [P, 2])
        ends_m = sb("ends_m", [2, 1])
        ends_d = sb("ends_d", [2, 2])
        base = sb("base", [P, 1])
        log_a = sb("log_a", [P, 1])
        theta = sb("theta", [P, 1])
        low = sb("low", [P, 1])
        step_w = sb("step_w", [P, 1])
        need = sb("need", [P, 1])
        key = sb("key", [P, NB])
        strict = sb("strict", [P, NB])
        tie = sb("tie", [P, NB])
        tied = sb("tied", [P, NB])
        fits = sb("fits", [P, NB])
        tot_t = sb("tot_t", [NB, P])
        sel = sb("sel", [P, NB])
        score = sb("score", [P, NB])

        STRIDE = SUB * P + SUB
        gram_flat = nc.dram_tensor("gram_dram", [NB, NSUB * STRIDE], F32).ap()
        inverse_flat = nc.dram_tensor("inverse_dram", [NB, NSUB * STRIDE], F32).ap()
        tiles_of = lambda t: t[:, 0:P * P].rearrange("n (r k) -> r n k", r=P)
        blocks_of = lambda t: (t.rearrange("n (j a) -> (n j) a", j=NSUB)[:, 0:SUB * P]
                               .rearrange("b (r k) -> b r k", r=SUB)[:, :, 0:SUB])
        S_banks = ctx.enter_context(nc.psum_tensor("S", [P, 2, 4, P], F32))
        S = S_banks[:, :, 0:PAIRS, :]
        QK = [bank("QK0"), bank("QK1")]
        PT = bank("PT")
        V_bank, Y_bank = bank("V"), bank("Y")
        V_ps, Y_ps = V_bank[:, 0:GH * D], Y_bank[:, 0:C]
        O_ps = bank("O")
        XT_ps = [PT, Y_bank]

        B = [S_banks[:, 0].rearrange("p a k -> p (a k)"), S_banks[:, 1].rearrange("p a k -> p (a k)"),
             QK[0][:], QK[1][:], PT[:], V_bank[:], Y_bank[:], O_ps[:]]

        ld_x = [sem(f"ld_x{q}") for q in range(TG)]
        ld_ident, ld_masks, ld_wq, ld_wk, ld_wv, ld_wo = (sem("ld_" + n) for n in
                                                          ("ident", "masks", "wq", "wk", "wv", "wo"))
        ld_rope = [sem(f"ld_rope{q}") for q in range(3)]
        swapped = [sem(f"swapped{g}") for g in range(G)]
        stored = sem("stored")
        dve_step = sem("dve_step")
        pool_step = sem("pool_step")
        sumsq_done = sem("sumsq_done")
        rms_done = sem("rms_done")
        squares_done = sem("squares_done")
        xn_done = sem("xn_done")
        xt_done = sem("xt_done")
        xnT_done = sem("xnT_done")
        zero_done = sem("zero_done")
        scores_done = sem("scores_done")
        max_done = sem("max_done")
        exp_done = sem("exp_done")
        norm_done = sem("norm_done")
        probsT_ps = sem("probsT_ps")
        probsT_done = sem("probsT_done")
        qk_ps = sem("qk_ps")
        mul_done = sem("mul_done")
        rope_done = sem("rope_done")
        xv_done = sem("xv_done")
        v_ps = sem("v_ps")
        v_own_done = sem("v_own_done")
        v_tail_done = sem("v_tail_done")
        v_mix_done = sem("v_mix_done")
        o_ps = sem("o_ps")
        oT_done = sem("oT_done")
        y_ps = sem("y_ps")
        r1_done = sem("r1_done")
        inv_done = sem("inv_done")
        tail_done = sem("tail_done")
        scaled_done = sem("scaled_done")
        ld_late = sem("ld_late")
        rsq_in = sem("rsq_in")
        rsq_out = sem("rsq_out")
        rsq2_out = sem("rsq2_out")
        x1_done = sem("x1_done")
        x1b_done = sem("x1b_done")
        tr_src = sem("tr_src")
        tr_ps = sem("tr_ps")
        tr_done = sem("tr_done")
        hid_ps = sem("hid_ps")
        hid_done = sem("hid_done")
        y2_ps = sem("y2_ps")
        r2_done = sem("r2_done")
        kv_ps = sem("kv_ps")
        kv_done = sem("kv_done")
        kh_done = sem("kh_done")
        gram_ps = sem("gram_ps")
        gram_done = sem("gram_done")
        l16_done = sem("l16_done")
        x16_done = sem("x16_done")
        invT_ld = [sem(f"invT_ld{q}") for q in range(TG)]
        zeros_kept = sem("zeros_kept")
        bt_done = sem("bt_done")
        bx_ps = sem("bx_ps")
        bx_done = sem("bx_done")
        xbxt_ps = sem("xbxt_ps")
        invT_done = sem("invT_done")
        ix_ps = sem("ix_ps")
        ix_done = sem("ix_done")
        wv_ps = sem("wv_ps")
        wv_done = sem("wv_done")
        dk_done = sem("dk_done")
        aq_ps = sem("aq_ps")
        aq_done = sem("aq_done")
        st_ps = sem("st_ps")
        st_done = sem("st_done")
        g_ps = sem("g_ps")
        g_done = sem("g_done")
        z_ps = sem("z_ps")
        zb_done = sem("zb_done")
        e_ps = sem("e_ps")
        e_done = sem("e_done")
        db_ps = sem("db_ps")
        db_done = sem("db_done")
        x3_ps = sem("x3_ps")
        x3_done = sem("x3_done")
        x32_done = sem("x32_done")
        m1_ps = sem("m1_ps")
        m1_done = sem("m1_done")
        m2_ps = sem("m2_ps")
        r3_done = sem("r3_done")
        x6_done = sem("x6_done")
        x6b_done = sem("x6b_done")
        s_done = sem("s_done")
        l1_ps = sem("l1_ps")
        l1_done = sem("l1_done")
        h1_ps = sem("h1_ps")
        h1_done = sem("h1_done")
        l2_ps = sem("l2_ps")
        base_done = sem("base_done")
        h2_ps = sem("h2_ps")
        heavy_done = sem("heavy_done")
        red_done = sem("red_done")
        redT_ps = sem("redT_ps")
        redm_done = sem("redm_done")
        ends_ps = sem("ends_ps")
        desc_in = sem("desc_in")
        desc_ps = sem("desc_ps")
        cnt_in = sem("cnt_in")
        cnt_ps = sem("cnt_ps")
        arg_done = sem("arg_done")
        f_done = sem("f_done")
        ln_in = sem("ln_in")
        ln_done = sem("ln_done")
        key_done = sem("key_done")
        strict_done = sem("strict_done")
        strict_ps = sem("strict_ps")
        tie_done = sem("tie_done")
        tot_ps = sem("tot_ps")
        tot_done = sem("tot_done")
        pre_ps = sem("pre_ps")
        score_done = sem("score_done")
        out_ready = sem("out_ready")
        zeroed = sem("zeroed")
        gam_done = sem("gam_done")
        blocks_kept = sem("blocks_kept")
        inverses_kept = sem("inverses_kept")
        x2_done = sem("x2_done")
        x16_set = sem("x16_set")
        dve_misc = sem("dve_misc")
        kset = sem("kset")
        pool_sum = sem("pool_sum")
        xbias_done = sem("xbias_done")
        tr_mn = sem("tr_mn")
        combined = sem("combined")

        block = ctx.enter_context(nc.Block())

        @block.sync
        def _(sp):
            grp = lambda q: slice(GB * q, GB * q + GB)

            def load_x(q):
                sp.dma_start(x_sb[:, GB * q:GB * q + GB, :],
                             x[512 * q:512 * q + 512, :].rearrange("(n p) c -> p n c", p=P)).then_inc(ld_x[q], 16)

            def swap_halves(n, g, b):
                sp.wait_ge(mul_done, n + 1)
                for r in range(0, P, D // 2):
                    other = r ^ (D // 2)
                    sp.dma_start(t_swap[other:other + D // 2, g], t_sin[r:r + D // 2, g]).then_inc(swapped[g], 16)

            def load_rope(h, cols):
                sp.dma_start(cos[:, cols], cos_dram[:, cols]).then_inc(ld_rope[h], 16)
                sp.dma_start(sin[:, cols], sin_dram[:, cols]).then_inc(ld_rope[h], 16)

            def swap_steps(b):
                for g in range(G):
                    swap_halves(b * G + g + G, g, b + 1)

            load_x(0)
            sp.dma_start(ident[:], ident_dram).then_inc(ld_ident, 16)
            load_rope(0, slice(0, P))
            load_x(1)
            sp.dma_start(masks[:], mask_dram).then_inc(ld_masks, 16)
            for q in range(2, TG):
                load_x(q)
            load_rope(1, slice(P, 4 * P))
            for g in range(G):
                swap_halves(g, g, 0)
            sp.dma_start(wo[:], w_o.rearrange("(n p) c -> p n c", p=P)).then_inc(ld_wo, 16)
            swap_steps(0)
            load_rope(2, slice(4 * P, T))
            swap_steps(1)
            sp.dma_start(late_sb[:], late_weights).then_inc(ld_late, 16)
            sp.dma_start(rows[:].rearrange("p a c -> p (a c)"), row_vectors.unsqueeze(0).broadcast_to([P, 6 * C])).then_inc(ld_late, 16)
            sp.dma_start(kv_b[:], kv_bias.unsqueeze(0).broadcast_to([P, KVW])).then_inc(ld_late, 16)
            sp.dma_start(lmask[:], level_dram).then_inc(ld_late, 16)
            sp.dma_start(before[:], before_dram).then_inc(ld_late, 16)
            sp.dma_start(digits[:].rearrange("p r k -> p (r k)"),
                         digit_dram.unsqueeze(0).broadcast_to([P, ROUNDS * DIGITS])).then_inc(ld_late, 16)
            with sp.Fori(2, NB - 1) as b:
                swap_steps(b)
            sp.wait_ge(zeroed, 1)
            sp.dma_start(tiles_of(inverse_flat), invT[:]).then_inc(zeros_kept, 16)
            for q in range(TG):
                sp.wait_ge(gram_done, q + 1)
                sp.dma_start(tiles_of(gram_flat)[:, grp(q)], gram[:, grp(q)]).then_inc(blocks_kept, 16)
            sp.wait_ge(blocks_kept, 16 * TG)
            sp.dma_start(l16[:, 0:SUB * SUB].rearrange("b (r k) -> b r k", r=SUB),
                         blocks_of(gram_flat)).then_inc(l16_done, 16)
            sp.wait_ge(x16_done, 1)
            sp.wait_ge(zeros_kept, 16)
            sp.dma_start(blocks_of(inverse_flat),
                         x16[:, 0:SUB * SUB].rearrange("b (k r) -> b k r", k=SUB)).then_inc(inverses_kept, 16)
            sp.wait_ge(inverses_kept, 16)
            for q in range(TG):
                sp.dma_start(invT[:, grp(q)], tiles_of(inverse_flat)[:, grp(q)]).then_inc(invT_ld[q], 16)
            out_v = out.rearrange("(n p) c -> p n c", p=P)
            for q in range(TG):
                sp.wait_ge(out_ready, q + 1)
                sp.dma_start(out_v[:, GB * q:GB * q + GB], XA[:, GB * q:GB * q + GB]).then_inc(stored, 16)
            sp.wait_ge(stored, 16 * TG)

        @block.tensor
        def _(pe):
            def project_qk(n, g, tok):
                wait(pe, mul_done, n - 1)
                for j, w in enumerate((wq, wk)):
                    for pr in range(PAIRS):
                        f = slice((PAIRS * g + pr) * P, (PAIRS * g + pr + 1) * P)
                        c = slice((PAIRS * j + pr) * P, (PAIRS * j + pr + 1) * P)
                        last = nc.tensor.matmul(QK[g % 2][:, c], w[:, f], xnT[:, tok], start=True, stop=True)
                last.then_inc(qk_ps, 1)

            def project_v(n, g, b):
                pe.wait_ge(xv_done, b + 1)
                wait(pe, v_own_done, n)
                nc.tensor.matmul(V_ps, xv[:], wv[:, g * GH * D:(g + 1) * GH * D], start=True,
                                 stop=True).then_inc(v_ps, 1)

            def scores(u, g):
                pe.wait_ge(rope_done, u + 1)
                wait(pe, max_done, u)
                for pr in range(PAIRS):
                    for e in range(2):
                        r = slice(D * e, D * e + D)
                        nc.tensor.matmul(S[:, e, pr], qk[r, g, pr, :], qk[r, g, PAIRS + pr, :], start=True, stop=True)
                for pr in range(PAIRS):
                    for e in range(2):
                        r = slice(D * e, D * e + D)
                        last = nc.tensor.matmul(S[0:WINDOW, e, pr, KEEP:], qk[r, g, pr, 0:WINDOW],
                                                k_tail[r, g, pr, :], start=True, stop=True)
                last.then_inc(scores_done, 1)

            def transpose_probs(u, g):
                pe.wait_ge(norm_done, u + 1)
                wait(pe, probsT_done, u)
                for h in range(GH):
                    last = nc.tensor.transpose(PT[:, h * P:(h + 1) * P], probs[:, g % 2, h % 2, h // 2, :], ident[:])
                last.then_inc(probsT_ps, 1)

            def attend(u, g):
                pe.wait_ge(probsT_done, u + 1)
                pe.wait_ge(v_mix_done, u + 1)
                wait(pe, oT_done, u)
                for h in range(GH):
                    r = slice(D * (h % 2), D * (h % 2) + D)
                    c = (h // 2) * P
                    nc.tensor.matmul(O_ps[r, c + WINDOW:c + P], v_own[:, g, h, :],
                                     probsT[:, g % 2, h, WINDOW:P], start=True, stop=True)
                    last = nc.tensor.matmul(O_ps[r, c:c + WINDOW], v_mix[:, g, h, :],
                                            probsT[:, g % 2, h, 0:WINDOW], start=True, stop=True)
                last.then_inc(o_ps, 1)

            def project_out(b):
                pe.wait_ge(oT_done, G * b + G)
                wait(pe, r1_done, b)
                if static(b) and b == 0:
                    pe.wait_ge(xnT_done, TG)
                    pe.wait_ge(ld_wo, 16)
                for n in range(NCH):
                    last = nc.tensor.matmul(Y_ps, oT[:, n, :], wo[:, n, :], start=(n == 0), stop=(n == NCH - 1))
                last.then_inc(y_ps, 1)

            def transpose_x(q):
                pe.wait_ge(xn_done, GB * q + GB)
                wait(pe, xnT_done, q)
                for i in range(GB):
                    last = nc.tensor.transpose(XT_ps[min(q, 1)][:, i * P:(i + 1) * P], xn[:, GB * q + i, :], ident[:])
                last.then_inc(xt_done, 1)

            def steps(b):
                fixed = static(b)
                for g in range(G):
                    u = b * G + g
                    if not fixed or b < NB:
                        scores(u, g)
                    if not fixed or b < NB - 1:
                        project_qk(u + G, g, bass.ts(b + 1, P))
                    if g == 2 and (not fixed or b >= 1):
                        project_out(b - 1)
                    if not fixed or 2 <= u <= UNITS + 1:
                        attend(u - 2, (g - 2) % G)
                    if not fixed or 1 <= u <= UNITS:
                        transpose_probs(u - 1, (g - 1) % G)
                    if fixed and b == 0 and 1 <= g < TG:
                        transpose_x(g)
                    if not fixed or u + 2 < UNITS:
                        project_v(u + 2, (g + 2) % G, b + (g + 2) // G)

            pe.wait_ge(ld_ident, 16)
            transpose_x(0)
            pe.wait_ge(xnT_done, 1)
            pe.wait_ge(scaled_done, 1)
            pe.wait_ge(ld_wk, 16)
            for g in range(G):
                project_qk(g, g, slice(0, P))
            pe.wait_ge(ld_wv, 16)
            for g in range(2):
                project_v(g, g, 0)
            steps(0)
            steps(1)
            with pe.Fori(2, NB - 1) as b:
                steps(b)
            steps(NB - 1)
            steps(NB)
            tok = lambda n: slice(n * P, (n + 1) * P)
            grp = lambda q: slice(q * 512, (q + 1) * 512)

            def to_channels(stage, q, src, arrived, count):
                t = stage * TG + q
                pe.wait_ge(arrived, count)
                wait(pe, tr_done, t - 1)
                for i in range(GB):
                    last = nc.tensor.transpose(B[t % 2][:, tok(i)], src(GB * q + i), ident[:])
                last.then_inc(tr_ps, 1)

            pe.wait_ge(ld_late, 96)

            def hidden1(q):
                pe.wait_ge(tr_done, q + 1)
                for j in range(NF):
                    n = NF * q + j
                    wait(pe, hid_done, n - 3)
                    nc.tensor.matmul(B[2 + j], W["w_f1"][:, tok(j)], hT[:, grp(q)], start=True,
                                     stop=True).then_inc(hid_ps, 1)

            def out1(q):
                pe.wait_ge(hid_done, NF * (q + 1))
                wait(pe, r2_done, q - 1)
                for i in range(GB):
                    for j in range(NF):
                        last = nc.tensor.matmul(B[6 + q % 2][:, tok(i)], hid[:, j, tok(GB * q + i)],
                                                W["w_f2"][:, tok(j)], start=(j == 0), stop=(j == NF - 1))
                last.then_inc(y2_ps, 1)

            for q in range(TG):
                to_channels(0, q, lambda n: XA[:, n, :], x1_done, q + 1)
                if q >= 1:
                    hidden1(q - 1)
                if q >= 2:
                    out1(q - 2)
            hidden1(TG - 1)
            out1(TG - 2)
            out1(TG - 1)

            def keys_and_values(q):
                pe.wait_ge(tr_done, TG + q + 1)
                for n in range(GB * q, GB * q + GB):
                    wait(pe, kv_done, n - 3)
                    nc.tensor.matmul(B[2 + n % 4][:, 0:KVW], hT[:, tok(n)], W["w_kv"], start=True,
                                     stop=True).then_inc(kv_ps, 1)

            def key_products(q):
                pe.wait_ge(tr_done, 2 * TG + q + 1)
                wait(pe, gram_done, q - 1)
                for i in range(GB):
                    n = GB * q + i
                    last = nc.tensor.matmul(B[6 + q % 2][:, tok(i)], khT[:, n, :], khT[:, n, :], start=True, stop=True)
                last.then_inc(gram_ps, 1)

            for s in range(TG + 1):
                if s < TG:
                    to_channels(1, s, lambda n: XB[:, n, :], tr_src, s + 1)
                if s >= 1:
                    keys_and_values(s - 1)
            for s in range(TG + 1):
                if s < TG:
                    to_channels(2, s, lambda n: kv[:, n, 0:C], kh_done, s + 1)
                if s >= 1:
                    key_products(s - 1)
            pe.wait_ge(gram_done, TG)
            pe.wait_ge(inverses_kept, 16)
            for _ in range(WARMING):
                nc.tensor.matmul(B[2][:, 0:P], ones_bf[:], ones_bf[:], start=True, stop=True)
            for l in range(NLEV):
                for q in range(TG):
                    t = l * TG + q
                    if l == 0:
                        pe.wait_ge(invT_ld[q], 16)
                    else:
                        pe.wait_ge(invT_done, (l - 1) * TG + q + 1)
                    wait(pe, ix_done, t - 1)
                    for i in range(GB):
                        last = nc.tensor.transpose(B[q % 2][:, tok(i)], invT[:, GB * q + i, :], ident[:])
                    last.then_inc(ix_ps, 1)
                pe.wait_ge(bt_done, l + 1)
                for q in range(TG):
                    t = l * TG + q
                    pe.wait_ge(ix_done, t + 1)
                    wait(pe, bx_done, t - 1)
                    for i in range(GB):
                        n = GB * q + i
                        last = nc.tensor.matmul(B[2 + q % 2][:, tok(i)], BT[:, l, n, :], inv[:, n, :], start=True, stop=True)
                    last.then_inc(bx_ps, 1)
                for q in range(TG):
                    t = l * TG + q
                    pe.wait_ge(bx_done, t + 1)
                    wait(pe, invT_done, t - 1)
                    for i in range(GB):
                        n = GB * q + i
                        last = nc.tensor.matmul(B[6 + q % 2][:, tok(i)], bx[:, n, :], invT[:, n, :], start=True, stop=True)
                    last.then_inc(xbxt_ps, 1)
            for m in range(NB // 2):
                wait(pe, wv_done, m - 1)
                pe.wait_ge(invT_done, (NLEV - 1) * TG + m // 2 + 1)
                for i in range(2):
                    n = 2 * m + i
                    last = nc.tensor.matmul(B[m % 2][:, 256 * i:256 * i + 256], invT[:, n, :], kv[:, n, 0:2 * C],
                                            start=True, stop=True)
                last.then_inc(wv_ps, 1)
            for m in range(NB // 2):
                pe.wait_ge(wv_done, m + 1)
                pe.wait_ge(dk_done, m // 2 + 1)
                wait(pe, aq_done, m - 1)
                for i in range(2):
                    n = 2 * m + i
                    nc.tensor.matmul(B[2 + m % 2][:, 256 * i:256 * i + C], wv2[:, n, 0:C], kv[:, n, 0:C],
                                     start=True, stop=True)
                    last = nc.tensor.matmul(B[2 + m % 2][:, 256 * i + C:256 * i + 256], wv2[:, n, 0:C], dk[:, n, :],
                                            start=True, stop=True)
                last.then_inc(aq_ps, 1)
            for n in range(NB):
                last = nc.tensor.matmul(B[7][:, 0:C], dk[:, n, :], wv2[:, n, C:], start=(n == 0), stop=False,
                                        skip_group_check=True)
                if n < NB - 1:
                    wait(pe, st_done, n - 1)
                    last = nc.tensor.matmul(B[5 + n % 2][:, 0:C], kv[:, n, 0:C], wv2[:, n, C:], start=True, stop=(n == 0),
                                            skip_group_check=True)
                if n > 0:
                    pe.wait_ge(aq_done, n // 2 + 1)
                    pe.wait_ge(st_done, n)
                if 0 < n < NB - 1:
                    last = nc.tensor.matmul(B[5 + n % 2][:, 0:C], naq[:, n, 0:C], state[:, n, :], start=False, stop=True,
                                            skip_group_check=True)
                if n < NB - 1:
                    last.then_inc(st_ps, 1)
                if n > 0:
                    last = nc.tensor.matmul(B[7][:, 0:C], naq[:, n, C:], state[:, n, :], start=False, stop=(n == NB - 1),
                                            skip_group_check=True)
            last.then_inc(g_ps, 1)
            pe.wait_ge(g_done, 1)
            nc.tensor.matmul(B[2][:, 0:C + 1], g_sb[:], W["w_qT"], start=True, stop=True).then_inc(z_ps, 1)
            pe.wait_ge(zb_done, 1)
            nc.tensor.matmul(B[3][:, 0:C], zT[:, 0:C], W["w_do"], start=True, stop=True).then_inc(e_ps, 1)
            pe.wait_ge(zb_done, 2)
            nc.tensor.matmul(B[4][:, 0:C], z_bias[:], W["w_do"], start=True, stop=True).then_inc(db_ps, 1)
            pe.wait_ge(e_done, 1)
            for q in range(TG):
                if q == TG - 1:
                    pe.wait_ge(db_done, 1)
                for i in range(GB):
                    last = nc.tensor.matmul(B[X3_BANKS[q]][:, tok(i)], hT[:, tok(GB * q + i)], e_sb[:], start=True, stop=True)
                last.then_inc(x3_ps, 1)

            for s in range(TG + 2):
                if s < TG:
                    to_channels(3, s, lambda n: XB[:, n, :], tr_mn, s + 1)
                if 1 <= s <= TG:
                    q = s - 1
                    pe.wait_ge(tr_done, 3 * TG + q + 1)
                    wait(pe, m1_done, q - 1)
                    nc.tensor.matmul(B[2 + q % 2], W["w_m1"], hT[:, grp(q)], start=True, stop=True).then_inc(m1_ps, 1)
                if s >= 2:
                    q = s - 2
                    pe.wait_ge(m1_done, q + 1)
                    pe.wait_ge(x3_done, min(q + 1, 2))
                    wait(pe, r3_done, q - 1)
                    for i in range(GB):
                        last = nc.tensor.matmul(B[6 + q % 2][:, tok(i)], hid[:, 0, tok(GB * q + i)], W["w_m2"],
                                                start=True, stop=True)
                    last.then_inc(m2_ps, 1)

            def ffn_piece(p):
                side, q = PIECES[p // PIECES_EACH]
                part = p % PIECES_EACH
                half = part % 2
                if side == "in" and part < 2:
                    if half == 0:
                        pe.wait_ge(gam_done, 2)
                        pe.wait_ge(tr_done, 4 * TG + q + 1)
                        wait(pe, l1_done, q)
                    c = slice(q * 512 + 256 * half, q * 512 + 256 * half + 256)
                    last = nc.tensor.matmul(B[5][0:LF, 256 * half:256 * half + 256], W["w_l1"], hT[:, c],
                                            start=True, stop=True)
                    if half == 1:
                        last.then_inc(l1_ps, 1)
                elif side == "in":
                    j = part // 2 - 1
                    n = NHF * q + j
                    if half == 0:
                        wait(pe, h1_done, n - 1)
                    c = slice(q * 512 + 256 * half, q * 512 + 256 * half + 256)
                    last = nc.tensor.matmul(B[3 + n % 2][:, 256 * half:256 * half + 256], W["w_h1"][:, tok(j)],
                                            hT[:, c], start=True, stop=True)
                    if half == 1:
                        last.then_inc(h1_ps, 1)
                elif part < 2:
                    if half == 0:
                        pe.wait_ge(tr_done, 5 * TG)
                        pe.wait_ge(l1_done, q + 1)
                        wait(pe, base_done, q)
                    for i in range(2 * half, 2 * half + 2):
                        last = nc.tensor.matmul(B[0][:, tok(i)], light[0:LF, tok(GB * q + i)], W["w_l2"][0:LF],
                                                start=True, stop=True)
                    if half == 1:
                        last.then_inc(l2_ps, 1)
                else:
                    i = part // 2 - 1
                    if part == 2:
                        pe.wait_ge(h1_done, NHF * (q + 1))
                        wait(pe, heavy_done, q)
                    for j in range(NHF // 2 * half, NHF // 2 * (half + 1)):
                        last = nc.tensor.matmul(B[2][:, tok(i)], hid[:, j, tok(GB * q + i)], W["w_h2"][:, tok(j)],
                                                start=(j == 0), stop=(j == NHF - 1))
                    if part == PIECES_EACH - 1:
                        last.then_inc(h2_ps, 1)

            for q in range(TG):
                to_channels(4, q, lambda n: XB[:, n, :], tr_src, TG + q + 1)
                if q == 1:
                    for p in range(PIECES_EACH):
                        ffn_piece(p)

            pe.wait_ge(red_done, 2)
            pe.wait_ge(kset, 3)
            nc.tensor.transpose(B[6][0:2, 0:P], ends[:], ident[:]).then_inc(redT_ps, 1)
            for p in range(PIECES_EACH, PIECES_EACH + BEFORE_ENDS):
                ffn_piece(p)
            pe.wait_ge(redm_done, 1)
            nc.tensor.matmul(B[6][:, 0:2], ones[0:2, :], ends_d[:], start=True, stop=True).then_inc(ends_ps, 1)
            for p in range(PIECES_EACH + BEFORE_ENDS, AHEAD):
                ffn_piece(p)
            for p in pieces_in(-1):
                ffn_piece(p)
            for i in range(DESCENT - 1):
                pe.wait_ge(desc_in, i + 1)
                nc.tensor.matmul(B[6][:, 0:1], kth[:], dpart[:, 0:1], start=True, stop=True).then_inc(desc_ps, 1)
                if i % 2 == 1:
                    pe.wait_ge(cnt_in, (i + 1) // 2)
                    nc.tensor.matmul(B[7][:, 0:DIGITS], ones_bf[:], cpart[:], start=True, stop=True).then_inc(cnt_ps, 1)
                if i % 2 == 0:
                    for _ in range(4):
                        nc.tensor.matmul(B[1][:, 0:P], ones_bf[:], ones_bf[:], start=True, stop=True)
                for p in pieces_in(i):
                    ffn_piece(p)
            pe.wait_ge(cnt_in, ROUNDS)
            nc.tensor.matmul(B[7][:, 0:DIGITS], ones_bf[:], cpart[:], start=True, stop=True).then_inc(cnt_ps, 1)
            pe.wait_ge(strict_done, 2)
            nc.tensor.matmul(B[6][:, 0:1], ones[:], dpart[:, 1:2], start=True, stop=True).then_inc(strict_ps, 1)
            pe.wait_ge(tie_done, 1)
            nc.tensor.matmul(B[7][0:NB, 0:P], tie[:], ones[:], start=True, stop=True).then_inc(tot_ps, 1)
            pe.wait_ge(tot_done, 1)
            nc.tensor.matmul(B[5][:, 0:NB], before[:], tie[:], start=True, stop=False)
            nc.tensor.matmul(B[5][:, 0:NB], tot_t[:], before[0:NB, 0:NB], start=False, stop=True).then_inc(pre_ps, 1)

        @block.vector
        def _(dve):
            count = [0]

            def chained(ins):
                count[0] += 1
                ins.then_inc(dve_step, 1)
                dve.wait_ge(dve_step, count[0])

            def rope_products(n, g, tok):
                dve.wait_ge(qk_ps, n + 1)
                wait(dve, rope_done, n - 3)
                for dst, table in ((t_cos, cos), (t_sin, sin)):
                    last = nc.vector.tensor_tensor(dst[:, g], QK[g % 2][:].rearrange("p (j t) -> p j t", j=4),
                                                   table[:, tok].unsqueeze(1).broadcast_to([P, 4, P]), ALU.mult)
                last.then_inc(mul_done, 1)

            def mask_scores(u, g, variant):
                for e in range(2):
                    for pr in range(PAIRS):
                        last = nc.vector.tensor_tensor_reduce(out=probs[:, g % 2, e, pr, :], in0=S[:, e, pr, :],
                                                              in1=masks[:, variant, :], scale=-1.0, scalar=3e38, op0=ALU.add,
                                                              op1=ALU.min, accum_out=negmax[:, g % 2, e, pr:pr + 1])
                last.then_inc(max_done, 1)

            def normalise(u, g):
                dve.wait_ge(exp_done, u + 1)
                nc.vector.reciprocal(inv_total[:, g % 2], total[:, g % 2]).then_inc(inv_done, 1)
                dve.wait_ge(inv_done, u + 1)
                nc.vector.tensor_tensor(probs[:, g % 2], probs[:, g % 2],
                                        inv_total[:, g % 2].unsqueeze(3).broadcast_to([P, 2, PAIRS, P]),
                                        ALU.mult).then_inc(norm_done, 1)

            def keep_v_tail(n, g):
                wait(dve, o_ps, n - G + 1)
                nc.vector.tensor_copy(v_mix[KEEP:P, g], v_own[KEEP:P, g]).then_inc(v_tail_done, 1)

            def mix_v(n, g):
                dve.wait_ge(v_own_done, n + 1)
                nc.vector.tensor_copy(v_mix[0:KEEP, g], v_own[0:KEEP, g]).then_inc(v_mix_done, 1)

            def residual(b, tile):
                dve.wait_ge(y_ps, b + 1)
                nc.vector.tensor_tensor(r1[:, tile, :], x_sb[:, tile, :], Y_ps.unsqueeze(1), ALU.add).then_inc(r1_done, 1)

            roots = [0]
            mv_count = [0]

            def norm_request(src, q, meanwhile=lambda: None):
                for n in range(GB * q, GB * q + GB):
                    last = nc.vector.bn_stats(bns[:, n, :], src[:, n, :])
                count[0] += 1
                last.then_inc(dve_step, 1)
                stats_kept = count[0]
                meanwhile()
                dve.wait_ge(dve_step, stats_kept)
                for n in range(GB * q, GB * q + GB):
                    last = nc.vector.bn_aggr(mv[:, n, :], bns[:, n, :])
                chained(last)
                nc.vector.tensor_scalar(var_eps[:, GB * q:GB * q + GB], mv[:, GB * q:GB * q + GB, 1], EPS, None,
                                        ALU.add).then_inc(rsq_in, 1)
                roots[0] += 1

            def standardise(dst, src, q, done):
                dve.wait_ge(rsq_out, roots[0] - (roots[0] - 1 - q) % TG)
                for n in range(GB * q, GB * q + GB):
                    last = nc.vector.tensor_scalar(dst[:, n, :], src[:, n, :], mv[:, n, 0:1], rstd[:, n:n + 1],
                                                   ALU.subtract, ALU.mult)
                last.then_inc(done, 1)

            def normalise_x(q):
                dve.wait_ge(rms_done, 1 if q == 0 else 2)
                dve.wait_ge(ld_x[q], 16)
                for n in range(GB * q, GB * q + GB):
                    nc.vector.tensor_scalar(xn[:, n, :], x_sb[:, n, :], rms[:, n:n + 1], None, ALU.mult).then_inc(xn_done, 1)

            def steps(b):
                fixed = static(b)
                for g in range(G):
                    u = b * G + g
                    if not fixed or u + 1 < UNITS:
                        keep_v_tail(u + 1, (g + 1) % G)
                    if not fixed or 1 <= u <= UNITS:
                        normalise(u - 1, (g - 1) % G)
                    if not fixed or u < UNITS:
                        dve.wait_ge(scores_done, u + 1)
                        wait(dve, probsT_ps, u - 1)
                        mix_v(u, g)
                        mask_scores(u, g, 0 if fixed and b == 0 else 1)
                    if g == 3 and (not fixed or b >= 1):
                        residual(b - 1, bass.ds(b - 1, 1))
                    if not fixed or b < NB - 1:
                        rope_products(u + G, g, bass.ts(b + 1, P))
                    if fixed and b == 0 and g < TG - 1:
                        normalise_x(g + 1)
                    if fixed and b == NB - 1 and g >= 1:
                        dve.wait_ge(r1_done, GB * g)
                        norm_request(r1, g - 1)
                    if fixed and b == NB and 1 <= g:
                        standardise(XA, r1, g - 1, x1_done)

            nc.vector.memset(v_own[:], 0.0).then_inc(zero_done, 1)
            grp = lambda q: slice(GB * q, GB * q + GB)
            bank4 = lambda b: B[b].rearrange("p (n c) -> p n c", n=GB)
            spread = lambda v: v.unsqueeze(1).broadcast_to([P, GB, C])

            dve.wait_ge(ld_x[0], 16)
            for n in range(GB):
                last = nc.vector.tensor_tensor_reduce(out=xn[:, n, :], in0=x_sb[:, n, :], in1=x_sb[:, n, :],
                                                      scale=1.0, scalar=0.0, op0=ALU.mult, op1=ALU.add,
                                                      accum_out=stat[:, n:n + 1])
            last.then_inc(squares_done, 1)
            normalise_x(0)
            dve.wait_ge(ld_rope[0], 32)
            for g in range(G):
                rope_products(g, g, slice(0, P))
            dve.wait_ge(ld_rope[1], 32)
            dve.wait_ge(zero_done, 1)
            dve.wait_ge(ld_masks, 16)
            keep_v_tail(0, 0)
            steps(0)
            steps(1)
            dve.wait_ge(ld_rope[2], 32)
            with dve.Fori(2, NB - 1) as b:
                steps(b)
            steps(NB - 1)
            steps(NB)
            dve.wait_ge(r1_done, NB)
            norm_request(r1, TG - 1)
            standardise(XA, r1, TG - 1, x1_done)
            for q in range(TG):
                dve.wait_ge(y2_ps, q + 1)
                dve.wait_ge(x1b_done, q + 1)
                nc.vector.tensor_tensor(XC[:, grp(q)], bank4(6 + q % 2), XB[:, grp(q)], ALU.add).then_inc(r2_done, 1)
                dve.wait_ge(r2_done, q + 1)
                norm_request(XC, q)
                if q >= 1:
                    standardise(XA, XC, q - 1, x2_done)
            standardise(XA, XC, TG - 1, x2_done)

            def normalised_keys(q):
                dve.wait_ge(rsq_out, roots[0] - TG + q + 1)
                nc.vector.tensor_tensor(kv[:, grp(q), 0:C], kv[:, grp(q), 0:C],
                                        rstd[:, grp(q)].unsqueeze(2).broadcast_to([P, GB, C]), ALU.mult).then_inc(kh_done, 1)

            roots[0] += TG
            for q in range(TG):
                for n in range(GB * q, GB * q + GB):
                    dve.wait_ge(kv_ps, n + 1)
                    nc.vector.tensor_tensor(kv[:, n, 0:KVW], B[2 + n % 4][:, 0:KVW], kv_b[:], ALU.add).then_inc(kv_done, 1)
                if q >= 2:
                    normalised_keys(q - 2)
            normalised_keys(TG - 2)
            normalised_keys(TG - 1)
            HALF = SUB // 2
            halves_of = lambda t: t[:].rearrange("p (h a) -> p h a", h=2)
            square = lambda t: t[:, 0:SUB * SUB].rearrange("p (c r) -> p c r", c=SUB)
            l_half, l_all, x_all = halves_of(l16), square(l16), square(x16)
            x_half = halves_of(x16)[:, :, 0:HALF * SUB].rearrange("p h (c r) -> p h c r", c=HALF)
            prod3 = prod[:].rearrange("p (a b c) -> p a b c", a=HALF, b=HALF)
            nc.vector.memset(x16[:], 0.0).then_inc(x16_set, 1)
            dve.wait_ge(x16_set, 1)
            nc.vector.memset(x16[:, 0:SUB * SUB:SUB + 1], 1.0).then_inc(x16_set, 1)
            dve.wait_ge(gram_done, TG)
            nc.vector.tensor_tensor(BT[:, 0], gram[:], lmask[:, 0:1, :].broadcast_to([P, NB, P]), ALU.mult).then_inc(bt_done, 1)
            for q in range(TG):
                nc.vector.tensor_tensor(dk[:, grp(q)], kv[:, grp(q), 0:C],
                                        kv[:, grp(q), 2 * C:2 * C + 1].broadcast_to([P, GB, C]), ALU.mult).then_inc(dk_done, 1)
            dve.wait_ge(l16_done, 16)
            dve.wait_ge(x16_set, 2)
            for i in range(1, HALF):
                part = prod[:, 0:2 * i * i].rearrange("p (h c j) -> p h c j", h=2, c=i)
                chained(nc.vector.tensor_tensor(part, l_half[:, :, SUB * i:SUB * i + i].unsqueeze(2).broadcast_to([P, 2, i, i]),
                                                x_half[:, :, 0:i, 0:i], ALU.mult))
                chained(nc.vector.tensor_reduce(x_half[:, :, 0:i, i], part, AX_X, ALU.add, negate=True))
            cube = lambda v, d: v.unsqueeze(d).broadcast_to([P, HALF, HALF, HALF])
            chained(nc.vector.tensor_tensor(prod3, cube(l_all[:, HALF:, 0:HALF], 1), cube(x_all[:, 0:HALF, 0:HALF], 2), ALU.mult))
            chained(nc.vector.tensor_reduce(lx[:], prod3, AX_X, ALU.add))
            chained(nc.vector.tensor_tensor(prod3, cube(x_all[:, HALF:, HALF:].rearrange("p j r -> p r j"), 1),
                                            cube(lx[:], 2), ALU.mult))
            nc.vector.tensor_reduce(x_all[:, 0:HALF, HALF:], prod3, AX_X, ALU.add, negate=True).then_inc(x16_done, 1)
            for l in range(NLEV):
                for q in range(TG):
                    t = l * TG + q
                    dve.wait_ge(xbxt_ps, t + 1)
                    nc.vector.tensor_tensor(invT[:, grp(q)], invT[:, grp(q)], bank4(6 + q % 2), ALU.subtract).then_inc(invT_done, 1)
            for n in range(NB - 1):
                dve.wait_ge(st_ps, n + 1)
                if n == 0:
                    last = nc.vector.tensor_copy(state[:, 1, :], B[5][:, 0:C])
                else:
                    dve.wait_ge(st_done, n)
                    last = nc.vector.tensor_tensor(state[:, n + 1, :], state[:, n, :], B[5 + n % 2][:, 0:C], ALU.add)
                last.then_inc(st_done, 1)
            dve.wait_ge(g_ps, 1)
            nc.vector.tensor_copy(g_sb[:], B[7][:, 0:C]).then_inc(g_done, 1)
            dve.wait_ge(db_ps, 1)
            nc.vector.tensor_tensor(delta_bias[:], B[4][:, 0:C], row["b_do"], ALU.add).then_inc(db_done, 1)
            for q in range(TG):
                dve.wait_ge(x3_ps, q + 1)
                dve.wait_ge(xbias_done, q + 1)
                nc.vector.tensor_tensor(XD[:, grp(q)], bank4(X3_BANKS[q]), XC[:, grp(q)], ALU.add).then_inc(x3_done, 1)
                dve.wait_ge(x3_done, q + 1)
                norm_request(XD, q)
                if q >= 1:
                    standardise(XB, XD, q - 1, tr_mn)
            standardise(XB, XD, TG - 1, tr_mn)

            def routing_scores(q):
                dve.wait_ge(x6_done, q + 1)
                for n in range(GB * q, GB * q + GB):
                    last = nc.vector.tensor_tensor_reduce(out=XC[:, n, :], in0=XA[:, n, :], in1=row["token"], scale=1.0,
                                                          scalar=0.0, op0=ALU.mult, op1=ALU.add, accum_out=s_tok[:, n:n + 1])
                last.then_inc(s_done, 1)

            for q in range(TG):
                dve.wait_ge(m2_ps, q + 1)
                dve.wait_ge(x32_done, q + 1)
                nc.vector.tensor_tensor(XE[:, grp(q)], bank4(6 + q % 2), XC[:, grp(q)], ALU.add).then_inc(r3_done, 1)
                dve.wait_ge(r3_done, q + 1)
                norm_request(XE, q, lambda: routing_scores(q - 2) if q >= 2 else None)
                if q >= 1:
                    standardise(XA, XE, q - 1, x6_done)
            standardise(XA, XE, TG - 1, x6_done)
            routing_scores(TG - 2)
            routing_scores(TG - 1)
            dve.wait_ge(s_done, TG)
            nc.vector.tensor_reduce(ends[:, 0:1], s_tok[:], AX_X, ALU.max).then_inc(red_done, 1)
            nc.vector.tensor_reduce(ends[:, 1:2], s_tok[:], AX_X, ALU.max, apply_absolute_value=True).then_inc(red_done, 1)

            def take_ffn(p):
                side, q = PIECES[p // PIECES_EACH]
                if side == "out" and p % PIECES_EACH == 1:
                    dve.wait_ge(l2_ps, q + 1)
                    dve.wait_ge(x6b_done, q + 1)
                    nc.vector.tensor_tensor(XC[:, grp(q)], bank4(0), XC[:, grp(q)], ALU.add).then_inc(base_done, 1)
                if side == "out" and p % PIECES_EACH == PIECES_EACH - 1:
                    dve.wait_ge(h2_ps, q + 1)
                    nc.vector.tensor_tensor(XE[:, grp(q)], bank4(2), spread(row["b_h2"]), ALU.add).then_inc(heavy_done, 1)

            dve.wait_ge(redT_ps, 1)
            chained(nc.vector.tensor_reduce(ends_m[:], B[6][0:2, 0:P], AX_X, ALU.max))
            nc.vector.tensor_scalar(ends_d[:], ident[0:2, 0:2], ends_m[:], None, ALU.mult).then_inc(redm_done, 1)
            dve.wait_ge(ends_ps, 1)
            nc.vector.tensor_scalar(base[:], B[6][:, 0:1], float(np.log(T / EFFECTIVE)), None, ALU.min).then_inc(dve_misc, 1)
            chained(nc.vector.tensor_copy(step_w[:], B[6][:, 1:2]))
            chained(nc.vector.tensor_scalar(step_w[:].bitcast(I32), step_w[:].bitcast(I32), 0x7F800000, None, ALU.bitwise_and))
            chained(nc.vector.tensor_scalar(widths[:], digits[:], step_w[:], None, ALU.mult))
            chained(nc.vector.tensor_scalar(low[:], step_w[:], -2.0, None, ALU.mult))
            nc.vector.memset(one[:], 1.0).then_inc(dve_misc, 1)
            dve.wait_ge(dve_misc, 2)
            nc.vector.tensor_scalar(args[:], s_tok[:], base[:], CAP, ALU.subtract, ALU.min).then_inc(arg_done, 1)

            def found_digit(r):
                dve.wait_ge(cnt_ps, r + 1)
                chained(nc.vector.scalar_tensor_tensor(cjunk[:, DIGITS, 0:DIGITS], B[7][:, 0:DIGITS], HEAVY - 0.5,
                                                       widths[:, r, 0:1].broadcast_to([P, DIGITS]),
                                                       ALU.is_ge, ALU.mult, accum_out=step_w[:]))

            def try_values(r):
                if r == 0:
                    chained(nc.vector.tensor_scalar(tried[:], widths[:, r], low[:], None, ALU.add))
                else:
                    found_digit(r - 1)
                    chained(nc.vector.tensor_scalar(tried[:], widths[:, r], step_w[:], low[:], ALU.add, ALU.add))

            def count_reached():
                for k in range(DIGITS):
                    last = nc.vector.tensor_scalar(cjunk[:, k], s_tok[:], tried[:, k:k + 1], None, ALU.is_ge, ALU.add,
                                                   accum_out=cpart[:, k:k + 1])
                last.then_inc(cnt_in, 1)

            dve.wait_ge(f_done, 1)
            for i in range(DESCENT - 1):
                used = sum(r + LEAD <= i for r in REBASE)
                a_now = one[:] if i == 0 else B[6][:, 0:1]
                if i > 0:
                    dve.wait_ge(desc_ps, i)
                if i in REBASE:
                    count[0] += 1
                    nc.vector.reciprocal(a_unit[:], B[6][:, 0:1]).then_inc(dve_step, 1)
                    nc.vector.tensor_copy(log_in[:], B[6][:, 0:1]).then_inc(ln_in, 1)
                if i - LEAD in REBASE:
                    dve.wait_ge(f_done, used + 1)
                    chained(nc.vector.tensor_tensor(a_rebased[:], B[6][:, 0:1], a_unit[:], ALU.mult))
                    a_now = a_rebased[:]
                nc.vector.tensor_scalar(djunk[:], f_tok[:, used % 2], a_now, None, ALU.min, ALU.add,
                                        accum_out=dpart[:, 0:1]).then_inc(desc_in, 1)
                if i - 3 in REBASE:
                    dve.wait_ge(ln_done, REBASE.index(i - 3) + 1)
                    chained(nc.vector.tensor_tensor(base[:], base[:], log_a[:], ALU.add))
                    nc.vector.tensor_scalar(args[:], s_tok[:], base[:], CAP, ALU.subtract, ALU.min).then_inc(arg_done, 1)
                if i % 2 == 0:
                    try_values(i // 2)
                else:
                    if i > 1:
                        count[0] += 1
                        nc.vector.tensor_tensor(low[:], low[:], step_w[:], ALU.add).then_inc(dve_step, 1)
                    count_reached()
                for p in pieces_in(i - 1):
                    take_ffn(p)
            last_i = DESCENT - 1
            dve.wait_ge(desc_ps, last_i)
            nc.vector.tensor_copy(log_in[:], B[6][:, 0:1]).then_inc(ln_in, 1)
            count[0] += 1
            nc.vector.tensor_tensor(low[:], low[:], step_w[:], ALU.add).then_inc(dve_step, 1)
            count_reached()
            for p in pieces_in(last_i - 1):
                take_ffn(p)
            found_digit(ROUNDS - 1)
            chained(nc.vector.tensor_tensor(low[:], low[:], step_w[:], ALU.add))
            dve.wait_ge(ln_done, len(REBASE) + 1)
            chained(nc.vector.tensor_tensor(theta[:], base[:], log_a[:], ALU.add))
            nc.vector.tensor_scalar(key[:], s_tok[:], theta[:], None, ALU.min).then_inc(key_done, 1)
            chained(nc.vector.tensor_tensor(low[:], low[:], theta[:], ALU.min))
            dve.wait_ge(key_done, 1)
            nc.vector.tensor_scalar(score[:], key[:], theta[:], None, ALU.subtract).then_inc(strict_done, 1)
            nc.vector.tensor_scalar(strict[:], key[:], low[:], None, ALU.is_gt, ALU.add,
                                    accum_out=dpart[:, 1:2]).then_inc(strict_done, 1)
            nc.vector.tensor_scalar(tie[:], key[:], low[:], None, ALU.is_equal).then_inc(tie_done, 1)
            dve.wait_ge(score_done, 1)
            chained(nc.vector.tensor_scalar(fits[:], escore[:], -1.0, 1.0, ALU.mult, ALU.add))
            chained(nc.vector.tensor_tensor(fits[:], fits[:], escore[:], ALU.add))
            dve.wait_ge(strict_ps, 1)
            nc.vector.tensor_scalar(need[:], B[6][:, 0:1], -1.0, float(HEAVY), ALU.mult, ALU.add).then_inc(dve_misc, 1)
            dve.wait_ge(tot_ps, 1)
            nc.vector.tensor_copy(tot_t[:], B[7][0:NB, 0:P]).then_inc(tot_done, 1)
            dve.wait_ge(tie_done, 1)
            nc.vector.tensor_tensor(tied[:], tie[:], fits[:], ALU.mult).then_inc(dve_misc, 1)
            nc.vector.tensor_tensor(strict[:], strict[:], fits[:], ALU.mult).then_inc(dve_misc, 1)
            dve.wait_ge(dve_misc, 5)
            dve.wait_ge(pre_ps, 1)
            chained(nc.vector.scalar_tensor_tensor(sel[:], B[5][:, 0:NB], need[:], tied[:], ALU.is_lt, ALU.mult))
            chained(nc.vector.tensor_tensor(sel[:], sel[:], strict[:], ALU.add))
            for q in range(TG):
                for n in range(GB * q, GB * q + GB):
                    last = nc.vector.scalar_tensor_tensor(XE[:, n, :], XE[:, n, :], sel[:, n:n + 1], XC[:, n, :],
                                                          ALU.mult, ALU.add)
                last.then_inc(combined, 1)
                if q >= 1:
                    standardise(XA, XE, q - 1, out_ready)
                dve.wait_ge(combined, q + 1)
                norm_request(XE, q)
            standardise(XA, XE, TG - 1, out_ready)

        @block.scalar
        def _(act):
            def exponentials(u, g):
                act.wait_ge(max_done, u + 1)
                for e in range(2):
                    for pr in range(PAIRS):
                        last = nc.scalar.activation(probs[:, g % 2, e, pr, :], probs[:, g % 2, e, pr, :], ACT.Exp,
                                                    scale=-1.0,
                                                    bias=negmax[:, g % 2, e, pr:pr + 1],
                                                    accum_out=total[:, g % 2, e, pr:pr + 1])
                last.then_inc(exp_done, 1)

            def keep_probsT(u, g):
                act.wait_ge(probsT_ps, u + 1)
                wait(act, o_ps, u - 1)
                nc.scalar.copy(probsT[:, g % 2], PT[:].rearrange("p (h q) -> p h q", h=GH)).then_inc(probsT_done, 1)

            def keep_v(n, g):
                act.wait_ge(v_ps, n + 1)
                act.wait_ge(v_tail_done, n + 1)
                nc.scalar.copy(v_own[:, g], V_ps.rearrange("p (h d) -> p h d", h=GH)).then_inc(v_own_done, 1)

            def keep_oT(u, g, b):
                act.wait_ge(o_ps, u + 1)
                wait(act, y_ps, b)
                nc.scalar.copy(oT[:, PAIRS * g:PAIRS * g + PAIRS, :],
                               O_ps[:, 0:PAIRS * P].rearrange("p (n q) -> p n q", n=PAIRS)).then_inc(oT_done, 1)

            def stage_x(b, tok):
                wait(act, v_ps, b * G)
                nc.scalar.copy(xv[:], xnT[:, tok]).then_inc(xv_done, 1)

            def keep_xnT(q):
                act.wait_ge(xt_done, q + 1)
                nc.scalar.copy(xnT[:, 512 * q:512 * q + 512], XT_ps[min(q, 1)][:]).then_inc(xnT_done, 1)

            def steps(b):
                fixed = static(b)
                for g in range(G):
                    u = b * G + g
                    if not fixed or 3 <= u <= UNITS + 2:
                        keep_oT(u - 3, (g - 3) % G, b - (1 if g < 3 else 0))
                    if g == 2 and (not fixed or b < NB - 1):
                        stage_x(b + 1, bass.ts(b + 1, P))
                    if not fixed or u + 1 < UNITS:
                        keep_v(u + 1, (g + 1) % G)
                    if not fixed or 2 <= u <= UNITS + 1:
                        keep_probsT(u - 2, (g - 2) % G)
                    if not fixed or b < NB:
                        exponentials(u, g)
                    if fixed and b == 0 and 1 <= g < TG:
                        keep_xnT(g)

            for dst, src, sem_ in ((wq, w_q, ld_wq), (wk, w_k, ld_wk), (wv, w_v, ld_wv)):
                act.dma_start(dst[:], src).then_inc(sem_, 16)
            act.wait_ge(ld_wq, 16)
            nc.scalar.mul(wq[:], wq[:], SCALE).then_inc(scaled_done, 1)
            keep_xnT(0)
            act.wait_ge(xnT_done, 1)
            stage_x(0, slice(0, P))
            for q in range(1, TG):
                act.wait_ge(ld_x[q], 16)
                for n in range(GB * q, GB * q + GB):
                    last = nc.scalar.activation(xn[:, n, :], x_sb[:, n, :], ACT.Square, accum_out=stat[:, n:n + 1])
            last.then_inc(squares_done, 1)
            keep_v(0, 0)
            steps(0)
            steps(1)
            with act.Fori(2, NB - 1) as b:
                steps(b)
            steps(NB - 1)
            steps(NB)
            grp = lambda q: slice(q * 512, (q + 1) * 512)
            bank4 = lambda b: B[b].rearrange("p (n c) -> p n c", n=GB)

            def from_transposes(stage, q, dst, scale=None, bias=None):
                t = stage * TG + q
                act.wait_ge(tr_ps, t + 1)
                if scale is None:
                    nc.scalar.copy(dst[:, grp(q)], B[t % 2]).then_inc(tr_done, 1)
                else:
                    nc.scalar.activation(dst[:, grp(q)], B[t % 2], ACT.Identity, bias=bias, scale=scale).then_inc(tr_done, 1)

            act.wait_ge(ld_late, 96)
            nc.scalar.mul(W["w_l1"], W["w_l1"], W["gam_l"]).then_inc(gam_done, 1)
            nc.scalar.mul(W["w_h1"], W["w_h1"], W["gam_h"]).then_inc(gam_done, 1)
            for q in range(TG + 1):
                if q < TG:
                    from_transposes(0, q, hT)
                if q >= 1:
                    for j in range(NF):
                        act.wait_ge(hid_ps, NF * (q - 1) + j + 1)
                        nc.scalar.activation(hid[:, j, grp(q - 1)], B[2 + j], ACT.Relu,
                                             bias=W["b_f1"][:, j:j + 1]).then_inc(hid_done, 1)
            def scaled(q, stage, arrived):
                act.wait_ge(arrived, q + 1)
                act.wait_ge(rsq2_out, stage * TG + q + 1)
                for n in range(GB * q, GB * q + GB):
                    last = nc.scalar.mul(XB[:, n, :], XA[:, n, :], rstd2[:, n:n + 1])
                last.then_inc(tr_src, 1)

            def key_squares(q):
                for n in range(GB * q, GB * q + GB):
                    act.wait_ge(kv_done, n + 1)
                    last = nc.scalar.activation(XD[:, n, :], kv[:, n, 0:C], ACT.Square, accum_out=var_eps[:, n:n + 1])
                last.then_inc(rsq_in, 1)

            for s in range(TG + 2):
                if s < TG:
                    scaled(s, 0, x2_done)
                if 1 <= s <= TG:
                    from_transposes(1, s - 1, hT, W["dn_g"], W["dn_b"])
                if s >= 2:
                    key_squares(s - 2)
            khT_flat = khT[:].rearrange("p n c -> p (n c)")
            for s in range(TG + 1):
                if s < TG:
                    from_transposes(2, s, khT_flat)
                if s >= 1:
                    act.wait_ge(gram_ps, s)
                    nc.scalar.copy(gram[:, GB * s - GB:GB * s], bank4(6 + (s - 1) % 2)).then_inc(gram_done, 1)
            for l in range(NLEV):
                for q in range(TG):
                    act.wait_ge(ix_ps, l * TG + q + 1)
                    nc.scalar.copy(inv[:, GB * q:GB * q + GB], bank4(q % 2)).then_inc(ix_done, 1)
                for q in range(TG):
                    act.wait_ge(bx_ps, l * TG + q + 1)
                    nc.scalar.copy(bx[:, GB * q:GB * q + GB], bank4(2 + q % 2)).then_inc(bx_done, 1)
            for m in range(NB // 2):
                act.wait_ge(wv_ps, m + 1)
                nc.scalar.copy(wv2[:, 2 * m:2 * m + 2], B[m % 2].rearrange("p (n c) -> p n c", n=2)).then_inc(wv_done, 1)
            for m in range(NB // 2):
                act.wait_ge(aq_ps, m + 1)
                nc.scalar.mul(naq[:, 2 * m:2 * m + 2], B[2 + m % 2].rearrange("p (n c) -> p n c", n=2), -1.0).then_inc(aq_done, 1)
            act.wait_ge(z_ps, 1)
            nc.scalar.copy(zT[:], B[2][:, 0:C + 1]).then_inc(zb_done, 1)
            act.wait_ge(zb_done, 1)
            nc.scalar.copy(z_bias[:], zT[:, C:C + 1].broadcast_to([P, C])).then_inc(zb_done, 1)
            act.wait_ge(e_ps, 1)
            nc.scalar.copy(e_sb[:], B[3][:, 0:C]).then_inc(e_done, 1)
            for s in range(TG + 1):
                if s < TG:
                    from_transposes(3, s, hT, W["mn_g"], W["mn_b"])
                if s >= 1:
                    act.wait_ge(m1_ps, s)
                    nc.scalar.activation(hid[:, 0, grp(s - 1)], B[2 + (s - 1) % 2], ACT.Relu,
                                         bias=W["m_b1"]).then_inc(m1_done, 1)

            def activate(p):
                side, q = PIECES[p // PIECES_EACH]
                part = p % PIECES_EACH
                if side == "in" and part == 1:
                    act.wait_ge(l1_ps, q + 1)
                    nc.scalar.activation(light[0:LF, grp(q)], B[5][0:LF, :], ACT.Gelu, bias=W["b_l1"][0:LF]).then_inc(l1_done, 1)
                elif side == "in" and part % 2 == 1:
                    j = part // 2 - 1
                    n = NHF * q + j
                    act.wait_ge(h1_ps, n + 1)
                    nc.scalar.activation(hid[:, j, grp(q)], B[3 + n % 2], ACT.Gelu,
                                         bias=W["b_h1"][:, j:j + 1]).then_inc(h1_done, 1)

            for q in range(TG):
                scaled(q, 1, x6_done)
                from_transposes(4, q, hT)
                if q == 1:
                    for p in range(PIECES_EACH):
                        activate(p)

            def exponentials_of_scores(m):
                act.wait_ge(arg_done, m + 1)
                nc.scalar.activation(f_tok[:, m % 2], args[:], ACT.Exp).then_inc(f_done, 1)

            for p in range(PIECES_EACH, PIECES_EACH + BEFORE_EXP):
                activate(p)
            exponentials_of_scores(0)
            for p in range(PIECES_EACH + BEFORE_EXP, AHEAD):
                activate(p)
            for p in pieces_in(-1):
                activate(p)
            for i in range(DESCENT):
                if i in REBASE or i == DESCENT - 1:
                    m = sum(r <= i for r in REBASE) + (i == DESCENT - 1)
                    act.wait_ge(ln_in, m)
                    nc.scalar.activation(log_a[:], log_in[:], ACT.Ln).then_inc(ln_done, 1)
                if i - 3 in REBASE:
                    exponentials_of_scores(REBASE.index(i - 3) + 1)
                for p in pieces_in(i - 1) if i > 0 else ():
                    activate(p)
            act.wait_ge(strict_done, 1)
            nc.scalar.activation(escore[:], score[:], ACT.Exp).then_inc(score_done, 1)

        @block.gpsimd
        def _(pool):
            def rope_sum(n, g, b):
                wait(pool, scores_done, n - G + 1)
                nc.gpsimd.tensor_tensor(k_tail[:, g], qk[:, g, PAIRS:, KEEP:], zeros[:], ALU.add).then_inc(tail_done, 1)
                pool.wait_ge(mul_done, n + 1)
                pool.wait_ge(swapped[g], 64 * (b + 1))
                pool.wait_ge(tail_done, n + 1)
                nc.gpsimd.tensor_tensor(qk[:, g], t_cos[:, g], t_swap[:, g], ALU.add).then_inc(rope_done, 1)

            nc.gpsimd.memset(expo[:], -0.5).then_inc(pool_step, 1)
            nc.gpsimd.memset(qk[:], 0.0).then_inc(pool_step, 1)
            nc.gpsimd.memset(zeros[:], 0.0).then_inc(pool_step, 1)
            pool.wait_ge(pool_step, 3)

            def inverse_rms(k, n0, n1):
                pool.wait_ge(squares_done, k)
                nc.gpsimd.tensor_scalar(mean2[:, n0:n1], stat[:, n0:n1], 1.0 / C, 1e-6, ALU.mult,
                                        ALU.add).then_inc(sumsq_done, 1)
                pool.wait_ge(sumsq_done, k)
                nc.gpsimd.tensor_tensor(rms[:, n0:n1], mean2[:, n0:n1], expo[:, n0:n1], ALU.pow).then_inc(rms_done, 1)

            inverse_rms(1, 0, GB)
            rope_sum(0, 0, 0)
            inverse_rms(2, GB, NB)
            for g in range(1, G):
                rope_sum(g, g, 0)

            def steps(b):
                for g in range(G):
                    rope_sum(b * G + g + G, g, b + 1)

            steps(0)
            steps(1)
            with pool.Fori(2, NB - 1) as b:
                steps(b)
            grp = lambda q: slice(GB * q, GB * q + GB)
            spread = lambda v: v.unsqueeze(1).broadcast_to([P, GB, C])
            roots = [0]

            def inverse_root(q):
                roots[0] += 1
                pool.wait_ge(rsq_in, roots[0])
                nc.gpsimd.tensor_tensor(rstd[:, grp(q)], var_eps[:, grp(q)], expo[:, grp(q)], ALU.pow).then_inc(rsq_out, 1)

            def second_root(q, op, bound):
                pool.wait_ge(rsq_out, roots[0])
                v = spread_var[:, grp(q)]
                pooled(nc.gpsimd.tensor_tensor(v, mv[:, grp(q), 1], rstd[:, grp(q)], ALU.mult))
                pooled(nc.gpsimd.tensor_tensor(v, v, rstd[:, grp(q)], ALU.mult))
                pooled(nc.gpsimd.tensor_scalar(v, v, bound, None, op))
                nc.gpsimd.tensor_tensor(rstd2[:, grp(q)], v, expo[:, grp(q)], ALU.pow).then_inc(rsq2_out, 1)

            small = [3]

            def pooled(ins):
                small[0] += 1
                ins.then_inc(pool_step, 1)
                pool.wait_ge(pool_step, small[0])

            for q in range(TG):
                inverse_root(q)
            pool.wait_ge(ld_late, 96)
            for q in range(TG):
                pool.wait_ge(x1_done, q + 1)
                nc.gpsimd.tensor_tensor(XB[:, grp(q)], XA[:, grp(q)], spread(row["b_f2"]), ALU.add).then_inc(x1b_done, 1)
            nc.gpsimd.memset(invT[:], 0.0).then_inc(zeroed, 1)
            nc.gpsimd.memset(ones[:], 1.0).then_inc(kset, 1)
            nc.gpsimd.memset(ones_bf[:], 1.0).then_inc(kset, 1)
            nc.gpsimd.memset(kth[:], 1.0 / EFFECTIVE).then_inc(kset, 1)
            for q in range(TG):
                inverse_root(q)
                second_root(q, ALU.add, EPS)
            for q in range(TG):
                inverse_root(q)
            pool.wait_ge(gram_done, TG)
            for l in range(1, NLEV):
                pool.wait_ge(bt_done, l)
                nc.gpsimd.tensor_tensor(BT[:, l], gram[:], lmask[:, l:l + 1, :].broadcast_to([P, NB, P]),
                                        ALU.mult).then_inc(bt_done, 1)
            for q in range(TG):
                nc.gpsimd.tensor_tensor(XE[:, grp(q)], XA[:, grp(q)], spread(row["b_m2"]), ALU.add).then_inc(pool_sum, 1)
            pool.wait_ge(pool_sum, TG)
            pool.wait_ge(db_done, 1)
            for q in range(TG):
                nc.gpsimd.tensor_tensor(XC[:, grp(q)], XA[:, grp(q)], spread(delta_bias[:]), ALU.add).then_inc(xbias_done, 1)
            for q in range(TG):
                inverse_root(q)
            for q in range(TG):
                pool.wait_ge(x3_done, q + 1)
                nc.gpsimd.tensor_tensor(XC[:, grp(q)], XD[:, grp(q)], XE[:, grp(q)], ALU.add).then_inc(x32_done, 1)
            for q in range(TG):
                inverse_root(q)
                second_root(q, ALU.max, 1e-24 / C)
            pool.wait_ge(s_done, TG)
            for q in range(TG):
                nc.gpsimd.tensor_tensor(XC[:, grp(q)], XA[:, grp(q)], spread(row["b_l2"]), ALU.add).then_inc(x6b_done, 1)
            for q in range(TG):
                inverse_root(q)


def lay_out(inputs):
    f = {k: np.asarray(v) for k, v in inputs.items()}
    channels = f["L0_attn_x"].shape[2]
    inner = f["L0_attn_w_out"].shape[1]
    w_q, w_k, w_v = (np.ascontiguousarray(f["L0_attn_w_qkv"][i * inner:(i + 1) * inner].T) for i in range(3))

    def chunks(w):
        return w.reshape(-1, P, w.shape[1]).transpose(1, 0, 2).reshape(P, -1)

    def column(v):
        if v.shape[0] < P:
            v = np.concatenate([v, np.zeros(P - v.shape[0], v.dtype)])
        return v.reshape(-1, P).T

    def padded(w):
        return np.concatenate([w, np.zeros((P - w.shape[0], w.shape[1]), w.dtype)])

    gates, gates_b = f["L1_attn_gates_w"], f["L1_attn_gates_b"]
    parts = [
        ("w_f1", f["L0_ffn_W1"]), ("w_f2", chunks(f["L0_ffn_W2"])), ("b_f1", column(f["L0_ffn_b1"])),
        ("w_kv", np.concatenate([gates[:, channels:], f["L1_attn_lr_w"]], 1)),
        ("w_qT", np.concatenate([gates[:, :channels].T, gates_b[:channels, None]], 1)),
        ("w_do", f["L1_attn_out_w"]), ("w_m1", f["L1_attn_w1"]), ("w_m2", f["L1_attn_w2"]),
        ("dn_g", column(f["L1_attn_dn_g"])), ("dn_b", column(f["L1_attn_dn_b"])),
        ("mn_g", column(f["L1_attn_mn_g"])), ("mn_b", column(f["L1_attn_mn_b"])), ("m_b1", column(f["L1_attn_b1"])),
        ("w_l1", f["L1_ffn_w1_l"].T), ("b_l1", column(f["L1_ffn_b1_l"])), ("w_l2", padded(f["L1_ffn_w2_l"].T)),
        ("w_h1", f["L1_ffn_w1_h"].T), ("b_h1", column(f["L1_ffn_b1_h"])), ("w_h2", chunks(f["L1_ffn_w2_h"].T)),
        ("gam_l", column(f["L1_ffn_gamma_l"])), ("gam_h", column(f["L1_ffn_gamma_h"])),
    ]
    late, at = {}, 0
    for name, a in parts:
        late[name] = (at, at + a.shape[1])
        at += a.shape[1]
    late["end"] = (at, at)
    arrays = {
        "x": f["L0_attn_x"].reshape(-1, channels),
        "w_q": w_q, "w_k": w_k, "w_v": w_v,
        "w_o": np.ascontiguousarray(f["L0_attn_w_out"].T),
        "late_weights": np.ascontiguousarray(np.concatenate([a for _, a in parts], 1)),
        "row_vectors": np.concatenate([f["L0_ffn_b2"], f["L1_attn_out_b"], f["L1_attn_b2"], f["L1_ffn_b2_l"],
                                       f["L1_ffn_b2_h"], f["L1_ffn_routing_token"]]),
        "kv_bias": np.concatenate([gates_b[channels:], f["L1_attn_lr_b"]]),
    }
    return arrays, late


def kernel(**inputs):
    import concourse.bacc as bacc
    from concourse.bass_utils import run_bass_kernel_spmd

    arrays, late = lay_out(inputs)
    nc = bacc.Bacc("TRN2", target_bir_lowering=False, num_devices=1)
    args = {n: nc.dram_tensor(n, a.shape, F32, kind="ExternalInput").ap() for n, a in arrays.items()}
    tokens, channels = arrays["x"].shape
    out = nc.dram_tensor("out", (tokens, channels), F32, kind="ExternalOutput").ap()
    build(nc, out=out, late=late, **args)
    r = run_bass_kernel_spmd(nc, [arrays], core_ids=[0])
    return r.results[0]["out"].reshape(np.asarray(inputs["L0_attn_x"]).shape)
```
